# Optimizing a Trainium2 kernel written in Bass

```python
import numpy as np
import jax
import jax.numpy as jnp

def _softmax(x, axis=-1):
    return jax.nn.softmax(x, axis=axis)

def _gelu(x):
    return jax.nn.gelu(x, approximate=True)

def _silu(x):
    return jax.nn.silu(x)

def _sigmoid(x):
    return jax.nn.sigmoid(x)

def _layernorm(x, axis=-1, eps=1e-05):
    m = jnp.mean(x, axis=axis, keepdims=True)
    v = jnp.var(x, axis=axis, keepdims=True)
    return (x - m) / jnp.sqrt(v + eps)

def _scatter_add(tgt, idx, src, axis=0):
    return tgt.at[idx].add(src)

def _segment_sum(src, seg, n):
    return jax.ops.segment_sum(src, seg, n)
kernel_name = 'mk_gnn_resnorm_d2_gnn_r64_44a89c'

def setup_inputs(seed: int=0):
    np.random.seed(seed)
    _w = jnp.asarray

    def _rec_inputs():
        import jax
        import jax.numpy as jnp
        _gk = jax.random.key(seed)
        x = -0.0003019 + 1 * jax.random.normal(jax.random.fold_in(_gk, 1), (10000, 1024), jnp.float32)
        _s = jax.random.randint(jax.random.fold_in(_gk, 2), (1250,), 0, 10000, jnp.int32)
        _d = jax.random.randint(jax.random.fold_in(_gk, 3), (1250,), 0, 10000, jnp.int32)
        _loop = jnp.arange(10000, dtype=jnp.int32)
        src = jnp.concatenate([_s, _d, _loop])
        dst = jnp.concatenate([_d, _s, _loop])
        _o = jnp.argsort(dst, stable=True)
        src = src[_o]
        dst = dst[_o]
        return (x, src, dst)
    x, src, dst = _rec_inputs()

    def _L0_gnn_setup():
        import jax, jax.numpy as jnp
        import numpy as np
        N = 20000
        E = 5000
        IN = 1024
        HID = 256
        H = 4
        D = HID // H
        OUT = 1024
        EPS = 1e-06
        NEG_SLOPE = 0.2
        key = jax.random.key(seed)
        ks = jax.random.split(key, 8)
        x = jax.random.normal(ks[0], (N, IN), dtype=jnp.float32)
        edge_index = jax.random.randint(ks[1], (2, E), 0, N, dtype=jnp.int64)
        s = 0.02
        return {'x': x, 'edge_index': edge_index, 'rms_w': jnp.ones((IN,), dtype=jnp.float32), 'W_down': jax.random.normal(ks[2], (IN, HID), dtype=jnp.float32) * s, 'Wl': jax.random.normal(ks[3], (HID, HID), dtype=jnp.float32) * s, 'Wr': jax.random.normal(ks[4], (HID, HID), dtype=jnp.float32) * s, 'att': jax.random.normal(ks[5], (H, D), dtype=jnp.float32) * s, 'W_up': jax.random.normal(ks[6], (HID, OUT), dtype=jnp.float32) * s}
    _L0_gnn_all = _L0_gnn_setup()
    _L0_gnn_in = {k: v for k, v in _L0_gnn_all.items() if k in ('rms_w', 'W_down', 'Wl', 'Wr', 'att', 'W_up')}
    del _L0_gnn_all

    def _L1_gnn_setup():
        import jax, jax.numpy as jnp
        import numpy as np
        N = 50000
        E = 12500
        D_IN = 1024
        D_HID = 512
        D_B = 256
        N_LAYERS = 3
        LN_EPS = 1e-05

        def layernorm(x, g, b):
            m = jnp.mean(x, axis=-1, keepdims=True)
            v = jnp.mean((x - m) ** 2, axis=-1, keepdims=True)
            return (x - m) * jax.lax.rsqrt(v + LN_EPS) * g + b
        key = jax.random.key(seed)
        ks = jax.random.split(key, 16)
        s = 0.02
        inp = {'x': jax.random.normal(ks[0], (N, D_IN), dtype=jnp.float32), 'edge_index': jax.random.randint(ks[1], (2, E), 0, N, dtype=jnp.int32), 'ln_in_g': jnp.ones((D_IN,), jnp.float32), 'ln_in_b': jnp.zeros((D_IN,), jnp.float32), 'W1': jax.random.normal(ks[2], (D_IN, D_HID), jnp.float32) * s, 'b1': jnp.zeros((D_HID,), jnp.float32), 'W2': jax.random.normal(ks[3], (D_HID, D_B), jnp.float32) * s, 'b2': jnp.zeros((D_B,), jnp.float32), 'layer_Wa': jax.random.normal(ks[4], (N_LAYERS, D_B, D_B), jnp.float32) * s, 'layer_ba': jnp.zeros((N_LAYERS, D_B), jnp.float32), 'layer_Wb': jax.random.normal(ks[5], (N_LAYERS, D_B, D_B), jnp.float32) * s, 'layer_bb': jnp.zeros((N_LAYERS, D_B), jnp.float32), 'layer_ng': jnp.ones((N_LAYERS, D_B), jnp.float32), 'layer_nb': jnp.zeros((N_LAYERS, D_B), jnp.float32), 'Wd1': jax.random.normal(ks[6], (D_B, D_HID), jnp.float32) * s, 'bd1': jnp.zeros((D_HID,), jnp.float32), 'Wd2': jax.random.normal(ks[7], (D_HID, D_IN), jnp.float32) * s, 'bd2': jnp.zeros((D_IN,), jnp.float32), 'out_g': jnp.ones((D_IN,), jnp.float32), 'out_b': jnp.zeros((D_IN,), jnp.float32)}
        return inp
    _L1_gnn_all = _L1_gnn_setup()
    _L1_gnn_in = {k: v for k, v in _L1_gnn_all.items() if k in ('ln_in_g', 'ln_in_b', 'W1', 'b1', 'W2', 'b2', 'layer_Wa', 'layer_ba', 'layer_Wb', 'layer_bb', 'layer_ng', 'layer_nb', 'Wd1', 'bd1', 'Wd2', 'bd2', 'out_g', 'out_b')}
    del _L1_gnn_all
    return {'x': x, 'src': src, 'dst': dst, 'L0_gnn_rms_w': _L0_gnn_in['rms_w'], 'L0_gnn_W_down': _L0_gnn_in['W_down'], 'L0_gnn_Wl': _L0_gnn_in['Wl'], 'L0_gnn_Wr': _L0_gnn_in['Wr'], 'L0_gnn_att': _L0_gnn_in['att'], 'L0_gnn_W_up': _L0_gnn_in['W_up'], 'L1_gnn_ln_in_g': _L1_gnn_in['ln_in_g'], 'L1_gnn_ln_in_b': _L1_gnn_in['ln_in_b'], 'L1_gnn_W1': _L1_gnn_in['W1'], 'L1_gnn_b1': _L1_gnn_in['b1'], 'L1_gnn_W2': _L1_gnn_in['W2'], 'L1_gnn_b2': _L1_gnn_in['b2'], 'L1_gnn_layer_Wa': _L1_gnn_in['layer_Wa'], 'L1_gnn_layer_ba': _L1_gnn_in['layer_ba'], 'L1_gnn_layer_Wb': _L1_gnn_in['layer_Wb'], 'L1_gnn_layer_bb': _L1_gnn_in['layer_bb'], 'L1_gnn_layer_ng': _L1_gnn_in['layer_ng'], 'L1_gnn_layer_nb': _L1_gnn_in['layer_nb'], 'L1_gnn_Wd1': _L1_gnn_in['Wd1'], 'L1_gnn_bd1': _L1_gnn_in['bd1'], 'L1_gnn_Wd2': _L1_gnn_in['Wd2'], 'L1_gnn_bd2': _L1_gnn_in['bd2'], 'L1_gnn_out_g': _L1_gnn_in['out_g'], 'L1_gnn_out_b': _L1_gnn_in['out_b']}

def reference(x, src, dst, L0_gnn_rms_w, L0_gnn_W_down, L0_gnn_Wl, L0_gnn_Wr, L0_gnn_att, L0_gnn_W_up, L1_gnn_ln_in_g, L1_gnn_ln_in_b, L1_gnn_W1, L1_gnn_b1, L1_gnn_W2, L1_gnn_b2, L1_gnn_layer_Wa, L1_gnn_layer_ba, L1_gnn_layer_Wb, L1_gnn_layer_bb, L1_gnn_layer_ng, L1_gnn_layer_nb, L1_gnn_Wd1, L1_gnn_bd1, L1_gnn_Wd2, L1_gnn_bd2, L1_gnn_out_g, L1_gnn_out_b):
    import jax
    import jax.numpy as jnp

    def _L0_gnn_ref(x, edge_index, rms_w, W_down, Wl, Wr, att, W_up):
        import jax, jax.numpy as jnp
        import numpy as np
        N = 20000
        E = 5000
        IN = 1024
        HID = 256
        H = 4
        D = HID // H
        OUT = 1024
        EPS = 1e-06
        NEG_SLOPE = 0.2
        n = x.shape[0]
        ms = jnp.mean(jnp.square(x), axis=-1, keepdims=True)
        x = x * jax.lax.rsqrt(ms + EPS) * rms_w
        x = x @ W_down
        loop = jnp.arange(n, dtype=edge_index.dtype)
        src = jnp.concatenate([edge_index[0], loop])
        dst = jnp.concatenate([edge_index[1], loop])
        xl = (x @ Wl).reshape(n, H, D)
        xr = (x @ Wr).reshape(n, H, D)
        msg = xl[src] + xr[dst]
        act = jnp.where(msg > 0, msg, NEG_SLOPE * msg)
        e = jnp.einsum('ehd,hd->eh', act, att)
        m = jax.ops.segment_max(e, dst, num_segments=n)
        p = jnp.exp(e - m[dst])
        denom = jax.ops.segment_sum(p, dst, num_segments=n)
        alpha = p / (denom[dst] + 1e-16)
        out = jax.ops.segment_sum(alpha[..., None] * xl[src], dst, num_segments=n)
        out = out.reshape(n, HID)
        return out @ W_up

    def _L1_gnn_ref(x, edge_index, ln_in_g, ln_in_b, W1, b1, W2, b2, layer_Wa, layer_ba, layer_Wb, layer_bb, layer_ng, layer_nb, Wd1, bd1, Wd2, bd2, out_g, out_b):
        import jax, jax.numpy as jnp
        import numpy as np
        N = 50000
        E = 12500
        D_IN = 1024
        D_HID = 512
        D_B = 256
        N_LAYERS = 3
        LN_EPS = 1e-05

        def layernorm(x, g, b):
            m = jnp.mean(x, axis=-1, keepdims=True)
            v = jnp.mean((x - m) ** 2, axis=-1, keepdims=True)
            return (x - m) * jax.lax.rsqrt(v + LN_EPS) * g + b
        n = x.shape[0]
        src, dst = (edge_index[0], edge_index[1])
        h = layernorm(x, ln_in_g, ln_in_b)
        h = jax.nn.relu(h @ W1 + b1)
        h = h @ W2 + b2
        for i in range(N_LAYERS):
            agg = jax.ops.segment_sum(h[src], dst, num_segments=n)
            z = h + agg
            z = jax.nn.relu(z @ layer_Wa[i] + layer_ba[i])
            z = z @ layer_Wb[i] + layer_bb[i]
            z = jax.nn.relu(layernorm(z, layer_ng[i], layer_nb[i]))
            h = h + z
        delta = jax.nn.relu(h @ Wd1 + bd1) @ Wd2 + bd2
        return layernorm(x + delta, out_g, out_b)
    edge_index = jnp.stack([src, dst])
    x = _layernorm(x + _L0_gnn_ref(x, edge_index, L0_gnn_rms_w, L0_gnn_W_down, L0_gnn_Wl, L0_gnn_Wr, L0_gnn_att, L0_gnn_W_up), axis=-1)
    x = _layernorm(x + _L1_gnn_ref(x, edge_index, L1_gnn_ln_in_g, L1_gnn_ln_in_b, L1_gnn_W1, L1_gnn_b1, L1_gnn_W2, L1_gnn_b2, L1_gnn_layer_Wa, L1_gnn_layer_ba, L1_gnn_layer_Wb, L1_gnn_layer_bb, L1_gnn_layer_ng, L1_gnn_layer_nb, L1_gnn_Wd1, L1_gnn_bd1, L1_gnn_Wd2, L1_gnn_bd2, L1_gnn_out_g, L1_gnn_out_b), axis=-1)
    return x

_drawn_inputs = setup_inputs


def setup_inputs(seed=0):
    import zlib

    import numpy as np

    out = dict(_drawn_inputs(seed))
    spreads = {'L0_gnn_rms_w': (1.0, 0.6),
     'L1_gnn_ln_in_g': (1.0, 0.6),
     'L1_gnn_ln_in_b': (0.0, 0.8),
     'L1_gnn_b1': (0.0, 0.8),
     'L1_gnn_b2': (0.0, 0.8),
     'L1_gnn_layer_ba': (0.0, 2.0),
     'L1_gnn_layer_bb': (0.0, 0.735),
     'L1_gnn_layer_ng': (1.0, 0.6),
     'L1_gnn_layer_nb': (0.0, 0.8),
     'L1_gnn_bd1': (0.0, 0.462),
     'L1_gnn_bd2': (0.0, 0.1),
     'L1_gnn_out_g': (1.0, 0.2),
     'L1_gnn_out_b': (0.0, 0.1)}
    factors = {'L0_gnn_Wr': 64.0, 'L0_gnn_att': 64.0, 'L1_gnn_W1': 3.782, 'L1_gnn_W2': 3.014}
    for name, (base, spread) in spreads.items():
        noise = np.random.default_rng([zlib.crc32(name.encode()), seed]).standard_normal(out[name].shape)
        drawn = base * np.exp(spread * noise) if base else spread * noise
        out[name] = jnp.asarray(drawn.astype(out[name].dtype))
    for name, factor in factors.items():
        out[name] = (out[name] * factor).astype(out[name].dtype)
    return out
```

```python
from contextlib import ExitStack

import concourse.bass as bass
from concourse import mybir

ALU = mybir.AluOpType
ACT = mybir.ActivationFunctionType
AX = mybir.AxisListType
F32 = mybir.dt.float32
BF16 = mybir.dt.bfloat16
I32 = mybir.dt.int32

P = 128
N_NODES = 10000
D = 1024
HID = 256
MID = 512
HEADS = 4
HD = HID // HEADS
HDA = HD + 1
EDGES = 12500
LAYERS = 3
RMS_EPS = 1e-6
LN_EPS = 1e-5
NEG_SLOPE = 0.2
DEN_EPS = 1e-16

GROUP = 512
SUB = GROUP // P
GROUPS = -(-N_NODES // GROUP)
TILES = GROUPS * SUB
ROWS = GROUPS * GROUP
KD = D // P
KH = HID // P
KM = MID // P
PAIR = 2 * P
WIDE = TILES // 2
ACC = HEADS * HDA
STRIDE = 2 * ACC

EP = 125
EC = EDGES // EP


def items_for(tiles, unroll):
    return -(-((EDGES + tiles * (P - 1)) // P) // unroll) * unroll


UA = 8
UL = 4
NARROW_TILES = -(-N_NODES // P)
WIDE_TILES = -(-N_NODES // PAIR)
ITEMS_A = items_for(NARROW_TILES, UA)
ITEMS_L = items_for(WIDE_TILES, UL)
SLOTS = P * (ITEMS_A + ITEMS_L)
MAGIC = 12582912.0
BIG = float(2.0 ** 100)
FIRST_SEM = 160
PAD_SRC = ROWS


class Done:

    def __init__(self, stage, name, slots=0, per=1):
        self.sem = stage.sem(name)
        self.slots, self.per = slots, per

    def open(self, eng):
        eng.sem_inc(self.sem, self.slots * self.per)

    def after(self, k):
        return k * self.per + (1 + self.slots) * self.per

    def room(self, k):
        return k * self.per + self.per


class Chain:

    def __init__(self, stage, eng, name, per):
        self.sem = stage.sem(name)
        self.eng, self.per, self.base, self.n = eng, per, 0, 0

    def start(self, k):
        self.base, self.n = k * self.per, 0

    def link(self, ins):
        ins.then_inc(self.sem, 1)
        self.n += 1
        assert self.n <= self.per
        self.eng.wait_ge(self.sem, self.base + self.n)

    def mark(self, ins):
        ins.then_inc(self.sem, 1)
        self.n += 1
        assert self.n <= self.per
        return self.base + self.n


def run(eng, total, unroll, skew, step, last=0):
    for i in range(unroll):
        step(i, i, 0)
    with eng.Fori(1, (total - last) // unroll) as q:
        for u in range(unroll):
            step(eng.snap(q * unroll + u), u, q)
    for i in range(total - last, total + skew):
        step(i, i % unroll, i // unroll)


def wait_apart(eng, reached, *waits):
    waits = [(sem, value if isinstance(value, int) else eng.to_reg(value)) for sem, value in waits]
    eng.wait_ge(*reached)
    for sem, value in waits:
        eng.wait_ge(sem, value)


def inside(k, total):
    return not isinstance(k, int) or 0 <= k < total


def tile_rows(t):
    return max(0, min(P, N_NODES - t * P))


class Env:
    pass


class Stage:

    def __init__(self, nc, ctx, name):
        self.nc, self.ctx, self.name = nc, ctx, name
        self.sems = []

    def sb(self, name, shape, dt=F32):
        return self.ctx.enter_context(self.nc.sbuf_tensor(f"{self.name}_{name}", shape, dt))

    def ps(self, name, shape):
        return self.ctx.enter_context(self.nc.psum_tensor(f"{self.name}_{name}", shape, F32))

    def sem(self, name):
        number = FIRST_SEM + len(self.sems)
        self.sems.append(number)
        return self.ctx.enter_context(self.nc.semaphore(f"{self.name}_{name}", num=number))

    def gpsimd_dma_sem(self, name):
        return self.ctx.enter_context(self.nc.semaphore(f"{self.name}_{name}"))

    def clear(self):
        self.nc.all_engine_barrier(sems_to_clear=range(FIRST_SEM, FIRST_SEM + len(self.sems)))

    def done(self, name, slots=0, per=1):
        return Done(self, name, slots, per)


def consts(nc, ctx):
    env = Env()

    def sb(name, shape, dt=F32):
        return ctx.enter_context(nc.sbuf_tensor(name, shape, dt))

    env.state = sb("state", [P, WIDE, STRIDE])
    env.acc = env.state[:].rearrange("p w (t h d) -> p (w t) h d", t=2, h=HEADS)
    env.featT = env.state[:, :, 0:2 * PAIR].rearrange("p w (c n) -> p w c n", c=KH)
    env.ident = sb("ident", [P, P])
    env.iota_row = sb("iota_row", [P, PAIR])
    env.nmax = sb("nmax", [P, TILES, HEADS])
    env.slots_a = sb("slots_a", [P, ITEMS_A, 2], I32)
    env.slots_l = sb("slots_l", [P, ITEMS_L, 2], I32)
    env.tile_a = sb("tile_a", [1, 2 * P], I32)
    env.tile_l = sb("tile_l", [1, 2 * P], I32)
    env.eps = sb("eps", [P, 2])
    return env


def place_edges(nc, env, src, dst, slots_dram, item_tiles_dram, moves_dram):
    with ExitStack() as ctx:
        stage = Stage(nc, ctx, "place")
        sb, ps, sem, done = stage.sb, stage.ps, stage.sem, stage.done
        src_i = sb("src_i", [EP, EC], I32)
        dst_i = sb("dst_i", [EP, EC], I32)
        dst_f = sb("dst_f", [EP, EC])
        tile_f = sb("tile_f", [EP, EC])
        tile_no = sb("tile_no", [EP, TILES])
        onehot = sb("onehot", [EP, TILES, EC])
        rank = sb("rank", [EP, TILES, EC])
        zeros = sb("zeros", [EP, TILES, EC], BF16)
        count = sb("count", [EP, TILES])
        total = sb("total", [P, TILES])
        items = sb("items", [P, TILES])
        ends = sb("ends", [P, TILES])
        shift = sb("shift", [P, TILES])
        ones_t = sb("ones_t", [P, TILES])
        position = sb("position", [EP, EC])
        item_f = sb("item_f", [EP, EC])
        before = sb("before", [EP, P])
        ones = sb("ones", [EP, P])
        item_no = sb("item_no", [P, 2])
        item_tile = sb("item_tile", [P, 2, 2])
        item_tile_i = sb("item_tile_i", [P, 2, 2], I32)
        le_junk = sb("le_junk", [P, TILES])
        moves = sb("moves", [EP, 2 * EC, 3], I32)
        blank = sb("blank", [P, ITEMS_A + ITEMS_L, 2], I32)
        base_ps = ps("base_ps", [P, 512])
        total_ps = ps("total_ps", [P, 512])
        edges_in = sem("edges_in")
        made = sem("made")
        counted = sem("counted")
        summed = sem("summed")
        placed = sem("placed")
        blank_out = sem("blank_out")
        out_done = sem("out_done")
        widths = ((P, NARROW_TILES, ITEMS_A, 0), (PAIR, WIDE_TILES, ITEMS_L, P * ITEMS_A))

        ctx.callback(stage.clear)
        block = ctx.enter_context(nc.Block())

        @block.sync
        def _(sp):
            sp.dma_start(src_i[:], src.rearrange("(p c) -> p c", p=EP)).then_inc(edges_in, 16)
            sp.dma_start(dst_i[:], dst.rearrange("(p c) -> p c", p=EP)).then_inc(edges_in, 16)
            sp.wait_ge(made, 8)
            sp.dma_start(slots_dram.rearrange("(p k) c -> p k c", p=P), blank[:]).then_inc(blank_out, 16)
            sp.wait_ge(placed, 2)
            sp.dma_start(moves_dram, moves[:]).then_inc(out_done, 16)
            for w in range(2):
                sp.dma_start(item_tiles_dram[w].rearrange("(p c) -> p c", p=P), item_tile_i[:, w, :]).then_inc(out_done, 16)
            sp.wait_ge(out_done, 48)
            sp.wait_ge(blank_out, 16)
            for w, t in enumerate((env.tile_a, env.tile_l)):
                sp.dma_start(t[:], item_tiles_dram[w:w + 1, :]).then_inc(out_done, 16)
            sp.wait_ge(out_done, 80)

        @block.gpsimd
        def _(pool):
            one = pool.to_reg(1.0)
            zero = pool.to_reg(0.0)
            nc.gpsimd.iota(tile_no[:], pattern=[[1, TILES]], base=0, channel_multiplier=0, allow_small_or_imprecise_dtypes=True).then_inc(made, 1)
            nc.gpsimd.iota(item_no[:], pattern=[[1, 2]], base=0, channel_multiplier=2, allow_small_or_imprecise_dtypes=True).then_inc(made, 1)
            nc.gpsimd.memset(ones[:], 1.0).then_inc(made, 1)
            pool.wait_ge(made, 3)
            nc.gpsimd.affine_select(out=before[:], in_=ones[:], compare_op=ALU.is_gt, fill=zero, base=0,
                                    pattern=[[1, P]], channel_multiplier=-1).then_inc(made, 1)
            nc.gpsimd.memset(ones_t[:], 1.0).then_inc(made, 1)
            nc.gpsimd.memset(zeros[:], 0.0).then_inc(made, 1)
            nc.gpsimd.memset(blank[:, :, 0:1], PAD_SRC).then_inc(made, 1)
            nc.gpsimd.memset(blank[:, :, 1:2].bitcast(F32), -1.0).then_inc(made, 1)
            nc.gpsimd.iota(env.iota_row[:], pattern=[[1, PAIR]], base=0, channel_multiplier=0, allow_small_or_imprecise_dtypes=True).then_inc(made, 1)
            nc.gpsimd.memset(env.ident[:], 0.0).then_inc(made, 1)
            pool.wait_ge(made, 10)
            nc.gpsimd.affine_select(out=env.ident[:], in_=env.ident[:], compare_op=ALU.not_equal, fill=one, base=0,
                                    pattern=[[-1, P]], channel_multiplier=1).then_inc(made, 1)
            nc.gpsimd.memset(env.eps[:, 0:1], RMS_EPS).then_inc(made, 1)
            nc.gpsimd.memset(env.eps[:, 1:2], LN_EPS).then_inc(made, 1)

        @block.tensor
        def _(pe):
            pe.wait_ge(made, 8)
            for w in range(2):
                pe.wait_ge(counted, w + 1)
                nc.tensor.matmul(base_ps[:, 0:TILES], before[:], count[:], start=True, stop=True)
                nc.tensor.matmul(total_ps[:, 0:TILES], ones[:], count[:], start=True, stop=True).then_inc(summed, 1)

        @block.vector
        def _(dve):
            v = nc.vector
            chain = Chain(stage, dve, "place_chain", 64)
            link = chain.link
            dve.wait_ge(edges_in, 32)
            dve.wait_ge(made, 13)
            link(v.tensor_copy(dst_f[:], dst_i[:]))
            for w, (width, tiles, n_items, row0) in enumerate(widths):
                link(v.tensor_scalar(tile_f[:], dst_f[:], -(width - 1) / 2.0, 1.0 / width, ALU.add, ALU.mult))
                link(v.tensor_scalar(tile_f[:], tile_f[:], MAGIC, MAGIC, ALU.add, ALU.subtract))
                hot = onehot[:, 0:tiles, :]
                rk = rank[:, 0:tiles, :]
                link(v.tensor_tensor(hot, tile_f[:].unsqueeze(1).broadcast_to([EP, tiles, EC]),
                                     tile_no[:, 0:tiles].unsqueeze(2).broadcast_to([EP, tiles, EC]), ALU.is_equal))
                link(v.tensor_tensor_scan(rk.rearrange("p t c -> p (t c)"), hot.rearrange("p t c -> p (t c)"),
                                          zeros[:, 0:tiles, :].rearrange("p t c -> p (t c)"), 0.0, ALU.add, ALU.add))
                if tiles < TILES:
                    link(v.memset(count[:, tiles:TILES], 0.0))
                link(v.tensor_copy(count[:, 0:1], rk[:, 0, EC - 1:EC]))
                link(v.tensor_tensor(count[:, 1:tiles], rk[:, 1:tiles, EC - 1], rk[:, 0:tiles - 1, EC - 1], ALU.subtract))
                v.tensor_copy(ones_t[:, 0:1], ones_t[:, 0:1]).then_inc(counted, 1)
                dve.wait_ge(summed, w + 1)
                link(v.tensor_scalar(total[:], total_ps[:, 0:TILES], P / 2.0 - 0.5, 1.0 / P, ALU.add, ALU.mult))
                link(v.tensor_scalar(items[:], total[:], MAGIC, MAGIC, ALU.add, ALU.subtract))
                link(v.tensor_tensor_scan(ends[:], ones_t[:], items[:], 0.0, ALU.mult, ALU.add))
                link(v.tensor_tensor(shift[:], ends[:], items[:], ALU.subtract))
                link(v.tensor_scalar(shift[:], shift[:], float(P), -1.0, ALU.mult, ALU.add))
                link(v.tensor_tensor(shift[:], base_ps[:, 0:TILES], shift[:], ALU.add))
                link(v.tensor_tensor(shift[0:EP, 1:tiles], shift[0:EP, 1:tiles], rk[:, 0:tiles - 1, EC - 1], ALU.subtract))
                link(v.tensor_tensor(rk, rk, shift[0:EP, 0:tiles].unsqueeze(2).broadcast_to([EP, tiles, EC]), ALU.add))
                link(v.tensor_tensor(rk, rk, hot, ALU.mult))
                link(v.tensor_reduce(position[:], rk.rearrange("p t c -> p c t"), AX.X, ALU.add))
                link(v.tensor_scalar(item_f[:], position[:], -(P - 1) / 2.0, 1.0 / P, ALU.add, ALU.mult))
                link(v.tensor_scalar(item_f[:], item_f[:], MAGIC, MAGIC, ALU.add, ALU.subtract))
                link(v.tensor_scalar(item_f[:], item_f[:], -float(P * n_items - 1), float(row0), ALU.mult, ALU.add))
                link(v.scalar_tensor_tensor(position[:], position[:], float(n_items), item_f[:], ALU.mult, ALU.add))
                mv = moves[:, w * EC:(w + 1) * EC, :]
                link(v.tensor_copy(mv[:, :, 0], position[:]))
                link(v.tensor_copy(mv[:, :, 1], src_i[:]))
                link(v.scalar_tensor_tensor(mv[:, :, 2].bitcast(F32), tile_f[:], -float(width), dst_f[:], ALU.mult, ALU.add))
                for c in range(2):
                    link(v.tensor_scalar(le_junk[:, 0:tiles], ends[:, 0:tiles], item_no[:, c:c + 1], None, ALU.is_le))
                    link(v.tensor_reduce(item_tile[:, w, c:c + 1], le_junk[:, 0:tiles], AX.X, ALU.add))
                link(v.tensor_scalar(item_tile[:, w, :], item_tile[:, w, :], float(tiles - 1), None, ALU.min))
                v.tensor_copy(item_tile_i[:, w, :], item_tile[:, w, :]).then_inc(placed, 1)


def attention_inputs(nc, env, x, W_down, Wl, Wr, rms_w, att, xl_dram, xr_dram, slots_dram, moves_dram):
    with ExitStack() as ctx:
        stage = Stage(nc, ctx, "pre")
        sb, ps, sem, done = stage.sb, stage.ps, stage.sem, stage.done
        wd = sb("wd", [P, KD, HID])
        rw = sb("rw", [P, KD])
        wlr = sb("wlr", [P, KH, 2 * HID])
        att_b = sb("att_b", [P, HID])
        moves = sb("moves_sb", [EP, 2 * EC, 3], I32)
        move_ring = sb("move_ring", [EP, 2, 3], I32)
        x_buf = sb("x_buf", [P, SUB, D])
        square = sb("square", [P, D])
        xT = sb("xT", [P, 2, KD, GROUP])
        yT = sb("yT", [P, KH, GROUP])
        xlr = sb("xlr", [P, SUB, 2 * HID])
        ms = sb("ms", [P, TILES])
        rstd = sb("rstd", [P, TILES])
        s_sum = sb("s_sum", [P, HID])
        s_leaky = sb("s_leaky", [P, HID])
        s_att = sb("s_att", [P, HID])
        tp = [ps(f"tp{i}", [P, KD, P]) for i in range(2)]
        y_ps = [ps(f"y_ps{i}", [P, GROUP]) for i in range(2)]
        xlr_ps = [ps(f"xlr_ps{i}", [P, 2 * HID]) for i in range(2)]

        weights_in = sem("weights_in")
        weights_scaled = sem("weights_scaled")
        den_set = sem("den_set")
        x_in = [sem(f"x_in{s}") for s in range(SUB)]
        xt_done = done("xt_done", SUB)
        sq_done = done("sq_done", SUB)
        rms_sqrt = done("rms_sqrt")
        rms_done = done("rms_done")
        tp_even = done("tp_even", 1)
        tp_odd = done("tp_odd", 1)
        y_done = done("y_done", per=1)
        y_out = done("y_out", 2)
        xlr_done = done("xlr_done")
        xlr_out = done("xlr_out", 2)
        self_done = done("self_done", SUB)
        acc_done = done("acc_done", SUB)
        stored = [sem(f"stored{s}") for s in range(SUB)]
        scattered = [stage.gpsimd_dma_sem(f"scattered{i}") for i in range(2)]

        ctx.callback(stage.clear)
        block = ctx.enter_context(nc.Block())
        last_group = GROUPS - 1

        @block.sync
        def _(sp):
            sp.dma_start(wd[:], W_down.rearrange("(k p) n -> p k n", p=P)).then_inc(weights_in, 16)
            with nc.allow_non_contiguous_dma("a column of weights"):
                sp.dma_start(rw[:], rms_w.rearrange("(k p) -> p k", p=P)).then_inc(weights_in, 16)
            sp.dma_start(wlr[:, :, 0:HID], Wl.rearrange("(k p) n -> p k n", p=P)).then_inc(weights_in, 16)
            sp.dma_start(wlr[:, :, HID:2 * HID], Wr.rearrange("(k p) n -> p k n", p=P)).then_inc(weights_in, 16)
            sp.dma_start(att_b[:], att.rearrange("h d -> (h d)").partition_broadcast(P)).then_inc(weights_in, 16)
            sp.dma_start(moves[:], moves_dram).then_inc(weights_in, 16)

            def load(g, s):
                t = g * SUB + s
                sp.wait_ge(xt_done.sem, xt_done.room(t))
                sp.wait_ge(sq_done.sem, sq_done.room(t))
                if not isinstance(g, int) or tile_rows(t) == P:
                    sp.dma_start(x_buf[:, s, :], x[bass.ds(t * P, P), :]).then_inc(x_in[s], 16)
                else:
                    n = tile_rows(t)
                    if n:
                        sp.dma_start(x_buf[0:n, s, :], x[t * P:t * P + n, :]).then_inc(x_in[s], 16)
                    sp.dma_start(x_buf[n:P, s, :], x[0:P - n, :]).then_inc(x_in[s], 16)

            with sp.Fori(0, last_group) as g:
                for s in range(SUB):
                    load(g, s)
            for s in range(SUB):
                load(last_group, s)

        def x_landed(s, g):
            t = g * SUB + s
            extra = 16 if isinstance(g, int) and g == last_group and 0 < tile_rows(t) < P else 0
            return g * 16 + 16 + extra

        @block.scalar
        def _(act):
            for c in (sq_done, tp_even, y_out, xlr_out):
                c.open(act)
            act.wait_ge(weights_in, 96)

            def square_up(g):
                for s in range(SUB):
                    act.wait_ge(x_in[s], x_landed(s, g))
                    act.wait_ge(sq_done.sem, sq_done.after(g * SUB + s - 1))
                    nc.scalar.activation(square[:], x_buf[:, s, :], ACT.Square,
                                         accum_out=ms[:, bass.ds(g * SUB + s, 1)]).then_inc(sq_done.sem, 1)
                act.wait_ge(sq_done.sem, sq_done.after(g * SUB + 3))
                nc.scalar.activation(rstd[:, bass.ds(g * SUB, SUB)], ms[:, bass.ds(g * SUB, SUB)], ACT.Sqrt,
                                     bias=env.eps[:, 0:1], scale=1.0 / D).then_inc(rms_sqrt.sem, 1)

            def copy_tp(g, u, s):
                act.wait_ge(xt_done.sem, xt_done.after(g * SUB + s))
                if inside(g - 2, GROUPS):
                    act.wait_ge(y_done.sem, y_done.after((g - 2) * KH + 1))
                nc.scalar.activation(xT[:, u % 2, :, s * P:(s + 1) * P], tp[0][:], ACT.Copy).then_inc(tp_even.sem, 1)

            def copy_y(g, m):
                act.wait_ge(y_done.sem, y_done.after(g * KH + m))
                if inside(g - 1, GROUPS):
                    act.wait_ge(xlr_done.sem, xlr_done.after(g * SUB - 1))
                nc.scalar.activation(yT[:, m, :], y_ps[m][:], ACT.Copy).then_inc(y_out.sem, 1)

            def scale_out(g, s):
                t = g * SUB + s
                act.wait_ge(xlr_done.sem, xlr_done.after(t))
                readers = [(self_done.sem, self_done.room(t)), (acc_done.sem, acc_done.room(t))]
                if inside(g - 1, GROUPS):
                    readers.append((stored[s], g * 32))
                wait_apart(act, (weights_in, 96), *readers)
                nc.scalar.activation(xlr[:, s, :], xlr_ps[s % 2][:], ACT.Copy,
                                     scale=rstd[:, bass.ds(t, 1)]).then_inc(xlr_out.sem, 1)
                act.wait_ge(xlr_out.sem, xlr_out.after(t))
                act.dma_start(xl_dram[bass.ds(t * P, P), :], xlr[:, s, 0:HID]).then_inc(stored[s], 16)
                act.dma_start(xr_dram[bass.ds(t * P, P), :], xlr[:, s, HID:2 * HID]).then_inc(stored[s], 16)

            def step(g, u, q):
                nxt = inside(g + 1, GROUPS)
                if isinstance(g, int) and g == 0:
                    square_up(0)
                    copy_tp(0, 0, 0)
                    copy_tp(0, 0, 2)
                act.wait_ge(rms_done.sem, rms_done.after(g))
                if nxt:
                    square_up(g + 1)
                    copy_tp(g + 1, u + 1, 0)
                copy_y(g, 0)
                copy_y(g, 1)
                if nxt:
                    copy_tp(g + 1, u + 1, 2)
                for s in range(SUB):
                    scale_out(g, s)

            run(act, GROUPS, 2, 0, step, last=2)
            for s in range(SUB):
                act.wait_ge(stored[s], GROUPS * 32)

        @block.vector
        def _(dve):
            v = nc.vector
            chain = Chain(stage, dve, "self_chain", 3 * SUB)
            tp_odd.open(dve)
            self_done.open(dve)
            dve.wait_ge(weights_in, 96)

            def copy_tp(g, u, s):
                dve.wait_ge(xt_done.sem, xt_done.after(g * SUB + s))
                if inside(g - 2, GROUPS):
                    dve.wait_ge(y_done.sem, y_done.after((g - 2) * KH + 1))
                v.tensor_copy(xT[:, u % 2, :, s * P:(s + 1) * P], tp[1][:]).then_inc(tp_odd.sem, 1)

            def recip(g):
                dve.wait_ge(rms_sqrt.sem, rms_sqrt.after(g))
                v.reciprocal(rstd[:, bass.ds(g * SUB, SUB)], rstd[:, bass.ds(g * SUB, SUB)]).then_inc(rms_done.sem, 1)

            def self_score(g, s):
                t = g * SUB + s
                dve.wait_ge(xlr_out.sem, xlr_out.after(t))
                dve.wait_ge(self_done.sem, self_done.after(t - 1))
                chain.link(v.tensor_tensor(s_sum[:], xlr[:, s, 0:HID], xlr[:, s, HID:2 * HID], ALU.add))
                chain.link(v.scalar_tensor_tensor(s_leaky[:], s_sum[:], NEG_SLOPE, s_sum[:], ALU.mult, ALU.max))
                chain.link(v.tensor_tensor(s_att[:], s_leaky[:], att_b[:], ALU.mult))
                v.tensor_reduce(env.nmax[:, bass.ds(t, 1), :].rearrange("p a h -> p (a h)"),
                                s_att[:].rearrange("p (h d) -> p h d", h=HEADS), AX.X, ALU.add,
                                negate=True).then_inc(self_done.sem, 1)

            def step(g, u, q):
                nxt = inside(g + 1, GROUPS)
                if isinstance(g, int) and g == 0:
                    recip(0)
                    copy_tp(0, 0, 1)
                    copy_tp(0, 0, 3)
                if nxt:
                    recip(g + 1)
                    copy_tp(g + 1, u + 1, 1)
                    copy_tp(g + 1, u + 1, 3)
                chain.start(g)
                for s in range(SUB):
                    self_score(g, s)

            run(dve, GROUPS, 2, 0, step, last=2)

        @block.tensor
        def _(pe):
            xt_done.open(pe)

            def turn(g, s):
                t = g * SUB + s
                pe.wait_ge(x_in[s], x_landed(s, g))
                evac = (tp_even, tp_odd)[s % 2]
                pe.wait_ge(evac.sem, evac.room(g * 2 + s // 2))
                for k in range(KD):
                    mm = nc.tensor.transpose(tp[s % 2][:, k, :], x_buf[:, s, k * P:(k + 1) * P], env.ident[:])
                mm.then_inc(xt_done.sem, 1)

            def down(g, u, m):
                if m == 0:
                    pe.wait_ge(tp_even.sem, tp_even.after(g * 2 + 1))
                    pe.wait_ge(tp_odd.sem, tp_odd.after(g * 2 + 1))
                pe.wait_ge(y_out.sem, y_out.room(g * KH + m))
                for k in range(KD):
                    mm = nc.tensor.matmul(y_ps[m][:], wd[:, k, m * P:(m + 1) * P], xT[:, u % 2, k, :],
                                          start=(k == 0), stop=(k == KD - 1))
                mm.then_inc(y_done.sem, 1)

            def left_right(g, s):
                t = g * SUB + s
                if s == 0:
                    pe.wait_ge(y_out.sem, y_out.after(g * KH + 1))
                pe.wait_ge(xlr_out.sem, xlr_out.room(t))
                for k in range(KH):
                    mm = nc.tensor.matmul(xlr_ps[s % 2][:], yT[:, k, s * P:(s + 1) * P], wlr[:, k, :],
                                          start=(k == 0), stop=(k == KH - 1))
                mm.then_inc(xlr_done.sem, 1)

            for s in range(SUB):
                turn(0, s)
            pe.wait_ge(weights_in, 96)
            pe.wait_ge(weights_scaled, KD)

            def step(g, u, q):
                nxt = inside(g + 1, GROUPS)
                if nxt:
                    turn(g + 1, 0)
                down(g, u, 0)
                if nxt:
                    turn(g + 1, 1)
                down(g, u, 1)
                if nxt:
                    turn(g + 1, 2)
                left_right(g, 0)
                left_right(g, 1)
                if nxt:
                    turn(g + 1, 3)
                left_right(g, 2)
                left_right(g, 3)

            run(pe, GROUPS, 2, 0, step, last=2)

        @block.gpsimd
        def _(pool):
            acc_done.open(pool)
            last_slot = pool.to_reg(SLOTS - 1)
            nc.gpsimd.memset(env.acc[:, :, :, HD:HDA], 1.0).then_inc(den_set, 1)
            pool.wait_ge(weights_in, 96)
            for k in range(KD):
                nc.gpsimd.tensor_scalar(wd[:, k, :], wd[:, k, :], rw[:, k:k + 1], None, ALU.mult).then_inc(weights_scaled, 1)
            pool.wait_ge(den_set, 1)
            chain = Chain(stage, pool, "move_chain", 10)
            per = 2 * EC // GROUPS

            def step(g, u, q):
                chain.start(g)
                for i in range(per):
                    if i < 2:
                        if inside(g - 1, GROUPS):
                            pool.wait_ge(scattered[i], g * (per // 2) * 16)
                    else:
                        pool.wait_ge(scattered[i % 2], g * (per // 2) * 16 + (i // 2) * 16)
                    v = chain.mark(nc.gpsimd.tensor_copy(move_ring[:, i % 2, :],
                                                         moves[:, bass.ds(g * per + i, 1), :].rearrange("p a c -> p (a c)")))
                    wait_apart(pool, (den_set, 1), (chain.sem, v))
                    pool.indirect_dma_start(
                        out=slots_dram, out_offset=bass.IndirectOffsetOnAxis(ap=move_ring[:, i % 2, 0:1], axis=0),
                        in_=move_ring[:, i % 2, 1:3], in_offset=None, bounds_check=last_slot,
                        oob_is_err=False).then_inc(scattered[i % 2], 16)
                for s in range(SUB):
                    t = g * SUB + s
                    pool.wait_ge(xlr_out.sem, xlr_out.after(t))
                    nc.gpsimd.tensor_copy(env.acc[:, bass.ds(t, 1), :, 0:HD].rearrange("p a h d -> p (a h) d"),
                                          xlr[:, s, 0:HID].rearrange("p (h d) -> p h d", h=HEADS)).then_inc(acc_done.sem, 1)

            run(pool, GROUPS, 1, 0, step)
            for i in range(2):
                pool.wait_ge(scattered[i], EC * 16)


def attention_edges(nc, env, att, xl_dram, xr_dram, slots_dram):
    with ExitStack() as ctx:
        stage = Stage(nc, ctx, "att")
        sb, ps, sem, done = stage.sb, stage.ps, stage.sem, stage.done
        R = UA
        att_b = sb("att_b2", [P, HID])
        index = sb("index", [P, R], I32)
        xl = sb("xl", [P, R, HID])
        xr = sb("xr", [P, R, HID])
        sel = sb("sel", [P, R, P])
        selT = sb("selT", [P, R, P])
        away = sb("away", [P, 4, P], BF16)
        message = sb("message", [P, 2, HID])
        leaky = sb("leaky", [P, HID])
        weighed = sb("weighed", [P, HID])
        score = sb("score", [P, R, HEADS])
        scoreT = sb("scoreT", [HEADS, 4, P])
        head_row = sb("head_row", [HEADS, HEADS, P])
        identb = sb("identb", [P, P], BF16)
        top = sb("top", [P, HEADS])
        nmax_new = sb("nmax_new", [P, R, HEADS])
        fall = sb("fall", [P, 2, HEADS])
        shrink = sb("shrink", [P, R, HEADS])
        under = sb("under", [P, 2, HEADS])
        part = sb("part", [P, 2, HEADS, HDA])

        selT_ps = ps("selT_ps", [P, 512])
        sum_ps = [ps(f"sum_ps{i}", [P, 512]) for i in range(2)]
        scoreT_ps = ps("scoreT_ps", [P, 512])
        wide_ps = [ps(f"wide_ps{i}", [P, HEADS, P]) for i in range(2)]
        under_ps = ps("under_ps", [P, 512])
        part_ps = ps("part_ps", [P, 512])

        tables_in = sem("tables_in")
        made = sem("made_c")
        xl_in = [stage.gpsimd_dma_sem(f"xl_in{u}") for u in range(R)]
        xr_in = [sem(f"xr_in{u}") for u in range(R)]
        index_done = done("index_done")
        sel_done = done("sel_done")
        selT_tp = done("selT_tp")
        selT_done = done("selT_done", 1)
        sum_done = done("sum_done", R)
        message_done = done("message_done", 2)
        score_done = done("score_done", 2)
        scoreT_tp = done("scoreT_tp")
        scoreT_done = done("scoreT_done", 1)
        wide_done = done("wide_done", 4)
        max_done = done("max_done", 2)
        shrink_done = done("shrink_done", 2)
        under_tp = done("under_tp")
        under_done = done("under_done", 1)
        prob_done = done("prob_done", 2)
        part_in = done("part_in", R)
        part_tp = done("part_tp", R)
        acc_done = done("acc_done2", 1)

        ctx.callback(stage.clear)
        block = ctx.enter_context(nc.Block())
        T = ITEMS_A

        @block.sync
        def _(sp):
            sp.dma_start(env.slots_a[:], slots_dram[0:P * ITEMS_A, :].rearrange("(p k) c -> p k c", p=P)).then_inc(tables_in, 16)
            sp.dma_start(env.slots_l[:], slots_dram[P * ITEMS_A:SLOTS, :].rearrange("(p k) c -> p k c", p=P)).then_inc(tables_in, 16)
            sp.dma_start(att_b[:], att.rearrange("h d -> (h d)").partition_broadcast(P)).then_inc(tables_in, 16)

            def step(i, u, q):
                j = sp.value_load(env.tile_a[0:1, bass.ds(i, 1)], min_val=0, max_val=NARROW_TILES - 1)
                sp.wait_ge(sum_done.sem, sum_done.room(i))
                sp.dma_start(xr[:, u, :], xr_dram[bass.ds(j * P, P), :]).then_inc(xr_in[u], 16)

            run(sp, T, R, 0, step)

        @block.gpsimd
        def _(pool):
            one = pool.to_reg(1.0)
            zero = pool.to_reg(0.0)
            last_row = pool.to_reg(ROWS - 1)
            nc.gpsimd.memset(xl[:], 0.0).then_inc(made, 1)
            nc.gpsimd.tensor_copy(identb[:], env.ident[:]).then_inc(made, 1)
            nc.gpsimd.memset(head_row[:], 1.0).then_inc(made, 1)
            pool.wait_ge(made, 3)
            nc.gpsimd.affine_select(out=head_row[:], in_=head_row[:], compare_op=ALU.is_equal, fill=zero, base=0,
                                    pattern=[[-1, HEADS], [0, P]], channel_multiplier=1).then_inc(made, 1)
            pool.wait_ge(made, 4)
            pool.wait_ge(tables_in, 48)

            def step(i, u, q):
                pool.wait_ge(part_in.sem, part_in.room(i))
                nc.gpsimd.tensor_copy(index[:, u:u + 1], env.slots_a[:, bass.ds(i, 1), 0]).then_inc(index_done.sem, 1)
                pool.wait_ge(tables_in, 48)
                pool.wait_ge(index_done.sem, index_done.after(i))
                pool.indirect_dma_start(out=xl[:, u, :], out_offset=None, in_=xl_dram,
                                        in_offset=bass.IndirectOffsetOnAxis(ap=index[:, u:u + 1], axis=0),
                                        bounds_check=last_row, oob_is_err=False).then_inc(xl_in[u], 16)

            run(pool, T, R, 0, step)

        @block.tensor
        def _(pe):
            for c in (sum_done, wide_done, part_tp):
                c.open(pe)
            pe.wait_ge(made, 4)

            def turn_sel(k, u):
                pe.wait_ge(sel_done.sem, sel_done.after(k))
                pe.wait_ge(selT_done.sem, selT_done.room(k))
                nc.tensor.transpose(selT_ps[:, 0:P], sel[:, u, :], env.ident[:]).then_inc(selT_tp.sem, 1)

            def turn_score(k, u):
                pe.wait_ge(score_done.sem, score_done.after(k))
                pe.wait_ge(scoreT_done.sem, scoreT_done.room(k))
                nc.tensor.transpose(scoreT_ps[0:HEADS, 0:P], score[:, u, :], env.ident[:]).then_inc(scoreT_tp.sem, 1)

            def sums(k, u, turn):
                pe.wait_ge(selT_done.sem, selT_done.after(k))
                pe.wait_ge(xl_in[u], turn * 16 + 16)
                pe.wait_ge(xr_in[u], turn * 16 + 16)
                pe.wait_ge(message_done.sem, message_done.room(k))
                nc.tensor.matmul(sum_ps[u % 2][:, 0:HID], selT[:, u, :], xr[:, u, :], start=True, stop=False)
                nc.tensor.matmul(sum_ps[u % 2][:, 0:HID], env.ident[:], xl[:, u, :], start=False,
                                 stop=True).then_inc(sum_done.sem, 1)

            def widen(k, u):
                pe.wait_ge(scoreT_done.sem, scoreT_done.after(k))
                pe.wait_ge(max_done.sem, max_done.room(k))
                nc.tensor.matmul(wide_ps[u % 2][:], identb[:], away[:, u % 4, :].unsqueeze(1).broadcast_to([P, HEADS, P]),
                                 start=True, stop=True)
                for h in range(HEADS):
                    mm = nc.tensor.matmul(wide_ps[u % 2][:, h, :], head_row[:, h, :], scoreT[:, u % 4, :],
                                          start=False, stop=True, skip_group_check=True)
                mm.then_inc(wide_done.sem, 1)

            def below(k, u):
                pe.wait_ge(max_done.sem, max_done.after(k))
                pe.wait_ge(under_done.sem, under_done.room(k))
                nc.tensor.matmul(under_ps[:, 0:HEADS], selT[:, u, :], nmax_new[:, u, :], start=True, stop=False)
                nc.tensor.matmul(under_ps[:, 0:HEADS], env.ident[:], score[:, u, :], start=False,
                                 stop=True).then_inc(under_tp.sem, 1)

            def gather_sum(k, u):
                pe.wait_ge(part_in.sem, part_in.after(k))
                pe.wait_ge(acc_done.sem, acc_done.room(k))
                nc.tensor.matmul(part_ps[:, 0:ACC], sel[:, u, :], part[:, u % 2].rearrange("p h d -> p (h d)"),
                                 start=True, stop=True).then_inc(part_tp.sem, 1)

            def step(i, u, q):
                if inside(i, T):
                    turn_sel(i, u)
                if inside(i - 2, T):
                    turn_score(i - 2, (u - 2) % R)
                if inside(i - 1, T):
                    k = i - 1
                    sums(k, (u - 1) % R, k // R if isinstance(k, int) else (q - 1 if u == 0 else q))
                if inside(i - 2, T):
                    widen(i - 2, (u - 2) % R)
                if inside(i - 3, T):
                    below(i - 3, (u - 3) % R)
                if inside(i - 4, T):
                    gather_sum(i - 4, (u - 4) % R)

            run(pe, T, R, 5, step)

        @block.scalar
        def _(act):
            for c in (selT_done, message_done, scoreT_done, shrink_done, prob_done):
                c.open(act)
            copied = done("selT_copied")

            def step(i, u, q):
                if inside(i, T):
                    act.wait_ge(selT_tp.sem, selT_tp.after(i))
                    act.wait_ge(part_tp.sem, part_tp.room(i))
                    act.wait_ge(wide_done.sem, wide_done.room(i))
                    nc.scalar.activation(selT[:, u, :], selT_ps[:, 0:P], ACT.Copy)
                    nc.scalar.activation(away[:, u % 4, :], selT_ps[:, 0:P], ACT.Copy, bias=-BIG,
                                         scale=BIG).then_inc(selT_done.sem, 1)
                if inside(i - 2, T):
                    k, w = i - 2, (u - 2) % 4
                    act.wait_ge(scoreT_tp.sem, scoreT_tp.after(k))
                    act.wait_ge(wide_done.sem, wide_done.room(k))
                    nc.scalar.activation(scoreT[:, w, :], scoreT_ps[0:HEADS, 0:P], ACT.Copy).then_inc(scoreT_done.sem, 1)
                if inside(i - 4, T):
                    k, w = i - 4, (u - 4) % 2
                    act.wait_ge(under_done.sem, under_done.after(k))
                    act.wait_ge(part_tp.sem, part_tp.after(k - 2))
                    nc.scalar.activation(part[:, w, :, HD], under[:, w, :], ACT.Exp).then_inc(prob_done.sem, 1)
                if inside(i - 1, T):
                    k, w = i - 1, (u - 1) % 2
                    act.wait_ge(sum_done.sem, sum_done.after(k))
                    act.wait_ge(score_done.sem, score_done.room(k))
                    nc.scalar.activation(message[:, w, :], sum_ps[w][:, 0:HID], ACT.Copy).then_inc(message_done.sem, 1)
                if inside(i - 3, T):
                    k, w = i - 3, (u - 3) % 2
                    act.wait_ge(max_done.sem, max_done.after(k))
                    nc.scalar.activation(shrink[:, (u - 3) % R, :], fall[:, w, :], ACT.Exp).then_inc(shrink_done.sem, 1)

            run(act, T, R, 5, step)

        @block.vector
        def _(dve):
            v = nc.vector
            for c in (score_done, max_done, under_done, part_in, acc_done):
                c.open(dve)
            dve.wait_ge(tables_in, 48)
            scored = done("scored", per=2)
            topped = done("topped", per=3)
            shrunk = done("shrunk")
            pointer = env.slots_a[:].bitcast(F32)

            def step(i, u, q):
                if inside(i, T):
                    dve.wait_ge(part_tp.sem, part_tp.room(i))
                    v.tensor_scalar(sel[:, u, :], env.iota_row[:, 0:P], pointer[:, bass.ds(i, 1), 1], None,
                                    ALU.is_equal).then_inc(sel_done.sem, 1)
                if inside(i - 3, T):
                    k, r, w = i - 3, (u - 3) % R, (u - 3) % 2
                    j = dve.value_load(env.tile_a[0:1, bass.ds(k, 1)], min_val=0, max_val=NARROW_TILES - 1)
                    mine = env.nmax[:, bass.ds(j, 1), :].rearrange("p a h -> p (a h)")
                    dve.wait_ge(wide_done.sem, wide_done.after(k))
                    dve.wait_ge(shrink_done.sem, shrink_done.room(k))
                    v.tensor_reduce(top[:], wide_ps[w][:], AX.X, ALU.max).then_inc(topped.sem, 1)
                    dve.wait_ge(topped.sem, k * 3 + 1)
                    v.scalar_tensor_tensor(nmax_new[:, r, :], top[:], -1.0, mine, ALU.mult, ALU.min).then_inc(topped.sem, 1)
                    dve.wait_ge(topped.sem, k * 3 + 2)
                    v.tensor_tensor(fall[:, w, :], nmax_new[:, r, :], mine, ALU.subtract).then_inc(topped.sem, 1)
                    wait_apart(dve, (tables_in, 48), (topped.sem, k * 3 + 3))
                    v.tensor_copy(mine, nmax_new[:, r, :]).then_inc(max_done.sem, 1)
                if inside(i - 4, T):
                    k, w = i - 4, (u - 4) % 2
                    dve.wait_ge(under_tp.sem, under_tp.after(k))
                    dve.wait_ge(prob_done.sem, prob_done.room(k))
                    v.tensor_scalar(under[:, w, :], under_ps[:, 0:HEADS], 0.0, None, ALU.min).then_inc(under_done.sem, 1)
                if inside(i - 5, T):
                    k, r = i - 5, (u - 5) % R
                    j = dve.value_load(env.tile_a[0:1, bass.ds(k, 1)], min_val=0, max_val=NARROW_TILES - 1)
                    mine = env.acc[:, bass.ds(j, 1)].rearrange("p a h d -> p (a h) d")
                    dve.wait_ge(shrink_done.sem, shrink_done.after(k))
                    dve.wait_ge(acc_done.sem, acc_done.room(k))
                    v.tensor_tensor(mine, mine, shrink[:, r, :].unsqueeze(2).broadcast_to([P, HEADS, HDA]),
                                    ALU.mult).then_inc(shrunk.sem, 1)
                    dve.wait_ge(part_tp.sem, part_tp.after(k))
                    dve.wait_ge(shrunk.sem, shrunk.after(k))
                    v.tensor_tensor(mine, part_ps[:, 0:ACC].rearrange("p (h d) -> p h d", h=HEADS), mine,
                                    ALU.add).then_inc(acc_done.sem, 1)
                if inside(i - 4, T):
                    k, r, w = i - 4, (u - 4) % R, (u - 4) % 2
                    dve.wait_ge(prob_done.sem, prob_done.after(k))
                    v.tensor_tensor(part[:, w, :, 0:HD], xl[:, r, :].rearrange("p (h d) -> p h d", h=HEADS),
                                    part[:, w, :, HD:HDA].broadcast_to([P, HEADS, HD]), ALU.mult).then_inc(part_in.sem, 1)
                if inside(i - 1, T):
                    k, r, w = i - 1, (u - 1) % R, (u - 1) % 2
                    dve.wait_ge(message_done.sem, message_done.after(k))
                    dve.wait_ge(score_done.sem, score_done.after(k - 1))
                    v.scalar_tensor_tensor(leaky[:], message[:, w, :], NEG_SLOPE, message[:, w, :], ALU.mult,
                                           ALU.max).then_inc(scored.sem, 1)
                    dve.wait_ge(scored.sem, k * 2 + 1)
                    v.tensor_tensor(weighed[:], leaky[:], att_b[:], ALU.mult).then_inc(scored.sem, 1)
                    dve.wait_ge(scored.sem, k * 2 + 2)
                    v.tensor_reduce(score[:, r, :], weighed[:].rearrange("p (h d) -> p h d", h=HEADS), AX.X,
                                    ALU.add).then_inc(score_done.sem, 1)

            run(dve, T, R, 5, step)


def network_inputs(nc, env, x, W_up, ln_g, ln_b, W1, b1, W2, b2, x1_dram, h_dram):
    with ExitStack() as ctx:
        stage = Stage(nc, ctx, "mid")
        sb, ps, sem, done = stage.sb, stage.ps, stage.sem, stage.done
        wup = sb("wup", [P, KH, D])
        w1 = sb("w1", [P, KD, MID])
        w2 = sb("w2", [P, KM, HID])
        g_col = sb("g_col", [P, KD])
        b_col = sb("b_col", [P, KD])
        b1_col = sb("b1_col", [P, KM])
        b2_b = sb("b2_b", [P, HID])
        x_buf = sb("x_buf3", [P, SUB, D])
        xn = sb("xn", [P, SUB, D])
        xnT = sb("xnT", [P, KD, GROUP])
        hidT = sb("hidT", [P, KM, GROUP])
        inv = sb("inv", [P, SUB, HEADS])
        out_a = sb("out_a", [P, 2, HID])
        oT = sb("oT", [P, 2, KH, P])
        h_row = sb("h_row", [P, SUB, HID])
        stats = sb("stats", [P, SUB, 2, 6])
        moments = sb("moments", [P, SUB, 2])
        rstd = sb("rstd3", [P, SUB])
        shift = sb("shift3", [P, SUB])
        var1 = sb("var1", [P, SUB])
        rstd1 = sb("rstd1", [P, SUB])
        turn_ps = [ps(f"turn_ps{i}", [P, 2 * KH, P]) for i in range(2)]
        up_ps = ps("up_ps", [P, D])
        xnT_ps = ps("xnT_ps", [P, KD, P])
        w_ps = [ps(f"w_ps{i}", [P, GROUP]) for i in range(2)]

        weights_in = sem("weights_in3")
        bias_done = sem("bias_done")
        bias_out = sem("bias_out")
        weights_scaled = sem("weights_scaled3")
        x_in = [sem(f"x3_in{s}") for s in range(SUB)]
        x1_out = [sem(f"x1_out{s}") for s in range(SUB)]
        h_out = [sem(f"h_out{s}") for s in range(SUB)]
        att_done = done("att_done", 2)
        oT_tp = done("oT_tp")
        oT_done = done("oT_done", 2)
        up_done = done("up_done", 2)
        v_done = done("v_done", 1)
        mom_done = done("mom_done")
        sqrt_done = done("sqrt_done")
        norm_done = done("norm_done")
        sqrt1_done = done("sqrt1_done")
        norm1_done = done("norm1_done")
        x1_done = done("x1_done")
        xn_done = done("xn_done", SUB)
        xn_tp = done("xn_tp", SUB)
        xnT_even = done("xnT_even")
        xnT_odd = done("xnT_odd")
        w1_done = done("w1_done")
        hid_done = done("hid_done", 2)
        h_tp_done = done("w2_done")
        h_done = done("h_done", 2)
        hT_tp = done("hT_tp")
        hT_done = done("hT_done", 1)

        ctx.callback(stage.clear)
        block = ctx.enter_context(nc.Block())
        last_group = GROUPS - 1
        T = GROUPS

        def x_landed(s, g):
            t = g * SUB + s
            extra = 16 if isinstance(g, int) and g == last_group and 0 < tile_rows(t) < P else 0
            return g * 16 + 16 + extra

        @block.sync
        def _(sp):
            sp.dma_start(wup[:], W_up.rearrange("(k p) n -> p k n", p=P)).then_inc(weights_in, 16)
            sp.dma_start(w1[:], W1.rearrange("(k p) n -> p k n", p=P)).then_inc(weights_in, 16)
            sp.dma_start(w2[:], W2.rearrange("(k p) n -> p k n", p=P)).then_inc(weights_in, 16)
            with nc.allow_non_contiguous_dma("columns of weights"):
                sp.dma_start(g_col[:], ln_g.rearrange("(k p) -> p k", p=P)).then_inc(weights_in, 16)
                sp.dma_start(b_col[:], ln_b.rearrange("(k p) -> p k", p=P)).then_inc(weights_in, 16)
                sp.dma_start(b1_col[:], b1.rearrange("(k p) -> p k", p=P)).then_inc(weights_in, 16)
            sp.dma_start(b2_b[:], b2.partition_broadcast(P)).then_inc(weights_in, 16)

            def load(g, s):
                t = g * SUB + s
                if not isinstance(g, int) or g > 0:
                    wait_apart(sp, (weights_in, 112), (xn_done.sem, xn_done.room(t)), (x1_out[s], g * 16))
                if not isinstance(g, int) or tile_rows(t) == P:
                    sp.dma_start(x_buf[:, s, :], x[bass.ds(t * P, P), :]).then_inc(x_in[s], 16)
                else:
                    n = tile_rows(t)
                    if n:
                        sp.dma_start(x_buf[0:n, s, :], x[t * P:t * P + n, :]).then_inc(x_in[s], 16)
                    sp.dma_start(x_buf[n:P, s, :], x[0:P - n, :]).then_inc(x_in[s], 16)

            def step(g, u, q):
                for s in range(SUB):
                    load(g, s)

            run(sp, T, 1, 0, step, last=1)

        @block.gpsimd
        def _(pool):
            xn_done.open(pool)
            pool.wait_ge(bias_done, 1)
            for k in range(KD):
                nc.gpsimd.tensor_scalar(w1[:, k, :], w1[:, k, :], g_col[:, k:k + 1], None, ALU.mult).then_inc(weights_scaled, 1)

            def step(g, u, q):
                for s in range(SUB):
                    t = g * SUB + s
                    wait_apart(pool, (bias_done, 1), (norm1_done.sem, norm1_done.after(g)),
                               (x1_done.sem, x1_done.after(t)), (xn_tp.sem, xn_tp.room(t)))
                    nc.gpsimd.tensor_scalar(xn[:, s, :], x_buf[:, s, :], rstd1[:, s:s + 1], None, ALU.mult).then_inc(xn_done.sem, 1)

            run(pool, T, 1, 0, step)

        @block.tensor
        def _(pe):
            up_done.open(pe)
            xn_tp.open(pe)
            pe.wait_ge(weights_in, 112)
            for m in range(KM):
                for k in range(KD):
                    mm = nc.tensor.matmul(w_ps[0][:, m:m + 1], w1[:, k, m * P:(m + 1) * P], b_col[:, k:k + 1],
                                          start=(k == 0), stop=(k == KD - 1))
            mm.then_inc(bias_done, 1)
            pe.wait_ge(bias_out, 1)
            pe.wait_ge(weights_scaled, KD)

            def turn_out(g, s):
                t = g * SUB + s
                pe.wait_ge(att_done.sem, att_done.after(t))
                pe.wait_ge(oT_done.sem, oT_done.after(t - 1))
                for k in range(KH):
                    mm = nc.tensor.transpose(turn_ps[0][:, k, :], out_a[:, s % 2, k * P:(k + 1) * P], env.ident[:])
                mm.then_inc(oT_tp.sem, 1)

            def up(g, s):
                t = g * SUB + s
                pe.wait_ge(oT_done.sem, oT_done.after(t))
                pe.wait_ge(v_done.sem, v_done.room(t))
                for n in range(2):
                    for k in range(KH):
                        mm = nc.tensor.matmul(up_ps[:, n * 512:(n + 1) * 512], oT[:, s % 2, k, :],
                                              wup[:, k, n * 512:(n + 1) * 512], start=(k == 0), stop=(k == KH - 1))
                mm.then_inc(up_done.sem, 1)

            def turn_x(g, s):
                t = g * SUB + s
                pe.wait_ge(xn_done.sem, xn_done.after(t))
                if s % 2:
                    pe.wait_ge(xnT_even.sem, xnT_even.after(g * 2 + s // 2))
                elif s or inside(g - 1, T):
                    pe.wait_ge(xnT_odd.sem, xnT_odd.after(g * 2 + s // 2 - 1))
                for k in range(KD):
                    mm = nc.tensor.transpose(xnT_ps[:, k, :], xn[:, s, k * P:(k + 1) * P], env.ident[:])
                mm.then_inc(xn_tp.sem, 1)

            def first(g, m):
                if m == 0:
                    pe.wait_ge(xnT_odd.sem, xnT_odd.after(g * 2 + 1))
                pe.wait_ge(hid_done.sem, hid_done.room(g * KM + m))
                pe.wait_ge(h_done.sem, h_done.after(g * SUB - 2 + m % 2))
                for k in range(KD):
                    mm = nc.tensor.matmul(w_ps[m % 2][:], w1[:, k, m * P:(m + 1) * P], xnT[:, k, :],
                                          start=(k == 0), stop=(k == KD - 1))
                mm.then_inc(w1_done.sem, 1)

            def second(g, s):
                t = g * SUB + s
                pe.wait_ge(hid_done.sem, hid_done.after(g * KM + KM - 1))
                pe.wait_ge(h_done.sem, h_done.room(t))
                for k in range(KM):
                    mm = nc.tensor.matmul(w_ps[s % 2][:, 0:HID], hidT[:, k, s * P:(s + 1) * P], w2[:, k, :],
                                          start=(k == 0), stop=(k == KM - 1))
                mm.then_inc(h_tp_done.sem, 1)

            def turn_h(g, s):
                t = g * SUB + s
                pe.wait_ge(h_done.sem, h_done.after(t))
                pe.wait_ge(hT_done.sem, hT_done.room(t))
                for k in range(KH):
                    mm = nc.tensor.transpose(turn_ps[1][:, k, :], h_row[:, s, k * P:(k + 1) * P], env.ident[:])
                mm.then_inc(hT_tp.sem, 1)

            def step(g, u, q):
                a, b = inside(g, T), inside(g - 1, T)
                if a:
                    turn_out(g, 0)
                for s in range(SUB):
                    if a and s + 1 < SUB:
                        turn_out(g, s + 1)
                    if a:
                        up(g, s)
                    if b:
                        turn_x(g - 1, s)
                if b:
                    for m in range(KM):
                        first(g - 1, m)
                    for s in range(SUB):
                        second(g - 1, s)
                        if s:
                            turn_h(g - 1, s - 1)
                    turn_h(g - 1, SUB - 1)

            run(pe, T, 1, 1, step)

        @block.scalar
        def _(act):
            oT_done.open(act)
            hid_done.open(act)
            hT_done.open(act)

            def copy_o(g, s):
                t = g * SUB + s
                act.wait_ge(oT_tp.sem, oT_tp.after(t))
                act.wait_ge(up_done.sem, up_done.room(t))
                nc.scalar.activation(oT[:, s % 2], turn_ps[0][:, 0:KH, :], ACT.Copy).then_inc(oT_done.sem, 1)

            def norm(g):
                act.wait_ge(mom_done.sem, mom_done.after(g))
                nc.scalar.activation(rstd[:], moments[:, :, 1], ACT.Sqrt, bias=env.eps[:, 1:2]).then_inc(sqrt_done.sem, 1)
                act.wait_ge(norm_done.sem, norm_done.after(g))
                act.wait_ge(xn_done.sem, xn_done.after(g * SUB - 1))
                nc.scalar.activation(rstd1[:], var1[:], ACT.Sqrt, bias=env.eps[:, 1:2]).then_inc(sqrt1_done.sem, 1)
                for s in range(SUB):
                    t = g * SUB + s
                    nc.scalar.activation(x_buf[:, s, :], x_buf[:, s, :], ACT.Identity, bias=shift[:, s:s + 1],
                                         scale=rstd[:, s:s + 1]).then_inc(x1_done.sem, 1)
                    act.wait_ge(x1_done.sem, x1_done.after(t))
                    act.dma_start(x1_dram[bass.ds(t * P, P), :], x_buf[:, s, :]).then_inc(x1_out[s], 16)

            def copy_x(g, s):
                t = g * SUB + s
                act.wait_ge(xn_tp.sem, xn_tp.after(t))
                if inside(g - 1, T):
                    act.wait_ge(w1_done.sem, w1_done.after(g * KM - 1))
                nc.scalar.activation(xnT[:, :, s * P:(s + 1) * P], xnT_ps[:], ACT.Copy).then_inc(xnT_even.sem, 1)

            def relu(g, m):
                act.wait_ge(w1_done.sem, w1_done.after(g * KM + m))
                if inside(g - 1, T):
                    act.wait_ge(h_tp_done.sem, h_tp_done.after(g * SUB - 1))
                nc.scalar.activation(hidT[:, m, :], w_ps[m % 2][:], ACT.Relu, bias=b1_col[:, m:m + 1]).then_inc(hid_done.sem, 1)

            def copy_h(g, s):
                t = g * SUB + s
                act.wait_ge(hT_tp.sem, hT_tp.after(t))
                nc.scalar.activation(env.featT[:, bass.ds(g * 2 + s // 2, 1), :, (s % 2) * P:(s % 2 + 1) * P]
                                     .rearrange("p a c n -> p (a c) n"), turn_ps[1][:, 0:KH, :], ACT.Copy).then_inc(hT_done.sem, 1)
                act.dma_start(h_dram[bass.ds(t * P, P), :], h_row[:, s, :]).then_inc(h_out[s], 16)

            def step(g, u, q):
                a, b = inside(g, T), inside(g - 1, T)
                if a:
                    copy_o(g, 0)
                for s in range(SUB):
                    if a and s + 1 < SUB:
                        copy_o(g, s + 1)
                    if b and s % 2 == 0:
                        copy_x(g - 1, s)
                if a:
                    norm(g)
                if b:
                    for m in range(KM):
                        relu(g - 1, m)
                    for s in range(SUB):
                        copy_h(g - 1, s)

            run(act, T, 1, 1, step)
            for s in range(SUB):
                act.wait_ge(x1_out[s], GROUPS * 16)
                act.wait_ge(h_out[s], GROUPS * 16)

        @block.vector
        def _(dve):
            v = nc.vector
            for c in (att_done, v_done, h_done):
                c.open(dve)
            dve.wait_ge(weights_in, 112)
            dve.wait_ge(bias_done, 1)
            v.tensor_tensor(b1_col[:], w_ps[0][:, 0:KM], b1_col[:], ALU.add).then_inc(bias_out, 1)

            chain = Chain(stage, dve, "input_chain", 3 * SUB + 5)

            def attended(g):
                den = env.acc[:, bass.ds(g * SUB, SUB), :, HD]
                chain.link(v.tensor_scalar(inv[:], den, DEN_EPS, None, ALU.add))
                chain.link(v.reciprocal(inv[:], inv[:]))

            def divide(g, s):
                t = g * SUB + s
                dve.wait_ge(oT_tp.sem, oT_tp.after(t - 2)) if inside(t - 2, TILES) else None
                v.tensor_tensor(out_a[:, s % 2, :].rearrange("p (h d) -> p h d", h=HEADS),
                                env.acc[:, bass.ds(t, 1), :, 0:HD].rearrange("p a h d -> p (a h) d"),
                                inv[:, s, :].unsqueeze(2).broadcast_to([P, HEADS, HD]), ALU.mult).then_inc(att_done.sem, 1)

            def residual(g, s):
                t = g * SUB + s
                dve.wait_ge(x_in[s], x_landed(s, g))
                dve.wait_ge(up_done.sem, up_done.after(t))
                v.tensor_tensor(x_buf[:, s, :], up_ps[:], x_buf[:, s, :], ALU.add).then_inc(v_done.sem, 1)
                dve.wait_ge(v_done.sem, v_done.after(t))
                for n in range(2):
                    m = chain.mark(v.bn_stats(stats[:, s, n, :], x_buf[:, s, n * 512:(n + 1) * 512]))
                wait_apart(dve, (weights_in, 112), (chain.sem, m))
                chain.link(v.bn_aggr(moments[:, s, :], stats[:, s].rearrange("p n c -> p (n c)")))

            def norm(g):
                v.tensor_copy(var1[:], moments[:, :, 1]).then_inc(mom_done.sem, 1)
                dve.wait_ge(sqrt_done.sem, sqrt_done.after(g))
                chain.link(v.reciprocal(rstd[:], rstd[:]))
                chain.link(v.scalar_tensor_tensor(shift[:], moments[:, :, 0], -1.0, rstd[:], ALU.mult, ALU.mult))
                chain.link(v.tensor_tensor(var1[:], var1[:], rstd[:], ALU.mult))
                v.tensor_tensor(var1[:], var1[:], rstd[:], ALU.mult).then_inc(norm_done.sem, 1)
                dve.wait_ge(sqrt1_done.sem, sqrt1_done.after(g))
                v.reciprocal(rstd1[:], rstd1[:]).then_inc(norm1_done.sem, 1)

            def copy_x(g, s):
                t = g * SUB + s
                dve.wait_ge(xn_tp.sem, xn_tp.after(t))
                if inside(g - 1, T):
                    dve.wait_ge(w1_done.sem, w1_done.after(g * KM - 1))
                v.tensor_copy(xnT[:, :, s * P:(s + 1) * P], xnT_ps[:]).then_inc(xnT_odd.sem, 1)

            def bias(g, s):
                t = g * SUB + s
                dve.wait_ge(h_tp_done.sem, h_tp_done.after(t))
                if inside(g - 1, T):
                    dve.wait_ge(h_out[s], g * 16)
                v.tensor_tensor(h_row[:, s, :], w_ps[s % 2][:, 0:HID], b2_b[:], ALU.add).then_inc(h_done.sem, 1)

            def step(g, u, q):
                a, b = inside(g, T), inside(g - 1, T)
                chain.start(g)
                if a:
                    attended(g)
                    divide(g, 0)
                for s in range(SUB):
                    if a and s + 1 < SUB:
                        divide(g, s + 1)
                    if a:
                        residual(g, s)
                    if b and s % 2 == 1:
                        copy_x(g - 1, s)
                if a:
                    norm(g)
                if b:
                    for s in range(SUB):
                        bias(g - 1, s)

            run(dve, T, 1, 1, step, last=1)


def add_neighbours(nc, env, number, h_dram):
    with ExitStack() as ctx:
        stage = Stage(nc, ctx, f"sum{number}")
        sb, ps, sem, done = stage.sb, stage.ps, stage.sem, stage.done
        R = UL
        T = ITEMS_L
        index = sb("index_l", [P, R], I32)
        h_src = sb("h_src", [P, R, HID])
        sel = sb("sel_l", [P, R, PAIR])
        sum_ps = [ps(f"nb_ps{i}", [P, KH, PAIR]) for i in range(R)]
        cleared = sem("cleared")
        index_done = done("index_done_l")
        h_in = [stage.gpsimd_dma_sem(f"h_in{u}") for u in range(R)]
        sel_done = done("sel_done_l")
        sum_done = done("sum_done_l", R)
        add_done = done("add_done", R)
        ctx.callback(stage.clear)
        block = ctx.enter_context(nc.Block())

        @block.gpsimd
        def _(pool):
            last_row = pool.to_reg(ROWS - 1)
            nc.gpsimd.memset(h_src[:], 0.0).then_inc(cleared, 1)
            pool.wait_ge(cleared, 1)

            def step(i, u, q):
                pool.wait_ge(sum_done.sem, sum_done.room(i))
                nc.gpsimd.tensor_copy(index[:, u:u + 1], env.slots_l[:, bass.ds(i, 1), 0]).then_inc(index_done.sem, 1)
                pool.wait_ge(cleared, 1)
                pool.wait_ge(index_done.sem, index_done.after(i))
                pool.indirect_dma_start(out=h_src[:, u, :], out_offset=None, in_=h_dram,
                                        in_offset=bass.IndirectOffsetOnAxis(ap=index[:, u:u + 1], axis=0),
                                        bounds_check=last_row, oob_is_err=False).then_inc(h_in[u], 16)

            run(pool, T, R, 0, step)

        @block.tensor
        def _(pe):
            sum_done.open(pe)

            def step(i, u, q):
                pe.wait_ge(sel_done.sem, sel_done.after(i))
                pe.wait_ge(h_in[u], q * 16 + 16)
                pe.wait_ge(add_done.sem, add_done.room(i))
                for c in range(KH):
                    mm = nc.tensor.matmul(sum_ps[u][:, c, :], h_src[:, u, c * P:(c + 1) * P], sel[:, u, :],
                                          start=True, stop=True)
                mm.then_inc(sum_done.sem, 1)

            run(pe, T, R, 0, step)

        @block.vector
        def _(dve):
            v = nc.vector
            add_done.open(dve)
            pointer = env.slots_l[:].bitcast(F32)

            def step(i, u, q):
                if inside(i, T):
                    dve.wait_ge(sum_done.sem, sum_done.room(i))
                    v.tensor_scalar(sel[:, u, :], env.iota_row[:], pointer[:, bass.ds(i, 1), 1], None,
                                    ALU.is_equal).then_inc(sel_done.sem, 1)
                if inside(i - 2, T):
                    k, r = i - 2, (u - 2) % R
                    j = dve.value_load(env.tile_l[0:1, bass.ds(k, 1)], min_val=0, max_val=WIDE_TILES - 1)
                    mine = env.featT[:, bass.ds(j, 1), :, :].rearrange("p a c n -> p (a c) n")
                    dve.wait_ge(sum_done.sem, sum_done.after(k))
                    dve.wait_ge(add_done.sem, add_done.after(k - 1))
                    v.tensor_tensor(mine, sum_ps[r][:], mine, ALU.add).then_inc(add_done.sem, 1)

            run(dve, T, R, 2, step)


def layer(nc, env, number, Wa, ba, Wb, bb, ng, nb, h_dram):
    with ExitStack() as ctx:
        stage = Stage(nc, ctx, f"layer{number}")
        sb, ps, sem, done = stage.sb, stage.ps, stage.sem, stage.done
        wa = sb("wa", [P, KH, HID])
        wb = sb("wb", [P, KH, HID])
        ba_col = sb("ba_col", [P, KH])
        bb_b = sb("bb_b", [P, HID])
        ng_b = sb("ng_b", [P, HID])
        nb_b = sb("nb_b", [P, HID])
        aT = sb("aT", [P, 2, KH, GROUP])
        h_row = sb("h_row4", [P, 2, SUB, HID])
        z = sb("z", [P, 2, SUB, HID])
        stats = sb("stats4", [P, SUB, 6])
        moments = sb("moments4", [P, SUB, 2])
        rstd = sb("rstd4", [P, SUB])
        a_ps = [ps(f"a_ps{i}", [P, GROUP]) for i in range(2)]
        z_ps = [ps(f"z_ps{i}", [P, 512]) for i in range(2)]
        hT_ps = [ps(f"hT_ps{i}", [P, SUB, P]) for i in range(4)]

        weights_in = sem("weights_in4")
        h_in = [sem(f"h4_in{u}") for u in range(2)]
        h_out = [sem(f"h4_out{u}") for u in range(2)]
        a_done = done("a_done")
        aT_done = done("aT_done", 2)
        z_done = done("z_done")
        zb_done = done("zb_done", 2)
        mom_done = done("mom_done4")
        sqrt_done = done("sqrt_done4")
        norm_done = done("norm_done4")
        gain_done = done("gain_done")
        affine_done = done("affine_done")
        h_done = done("h_done4")
        hT_tp = done("hT_tp4")
        hT_done = done("hT_done4", 2)
        ctx.callback(stage.clear)
        block = ctx.enter_context(nc.Block())
        T = GROUPS

        @block.sync
        def _(sp):
            sp.dma_start(wa[:], Wa.rearrange("(k p) n -> p k n", p=P)).then_inc(weights_in, 16)
            sp.dma_start(wb[:], Wb.rearrange("(k p) n -> p k n", p=P)).then_inc(weights_in, 16)
            with nc.allow_non_contiguous_dma("a column of weights"):
                sp.dma_start(ba_col[:], ba.rearrange("(k p) -> p k", p=P)).then_inc(weights_in, 16)
            for to, of in ((bb_b, bb), (ng_b, ng), (nb_b, nb)):
                sp.dma_start(to[:], of.partition_broadcast(P)).then_inc(weights_in, 16)

            def rows(g):
                return h_dram[bass.ds(g * GROUP, GROUP), :].rearrange("(s p) d -> p s d", p=P)

            def step(g, u, q):
                if inside(g, T):
                    if inside(g - 2, T):
                        sp.wait_ge(h_out[u], q * 16)
                        sp.wait_ge(hT_tp.sem, hT_tp.after((g - 2) * 2 + 1))
                    sp.dma_start(h_row[:, u], rows(g)).then_inc(h_in[u], 16)
                if inside(g - 1, T):
                    sp.wait_ge(h_done.sem, h_done.after(g - 1))
                    sp.dma_start(rows(g - 1), h_row[:, 1 - u]).then_inc(h_out[1 - u], 16)

            run(sp, T, 2, 1, step)
            for u in range(2):
                sp.wait_ge(h_out[u], GROUPS * 8)

        @block.tensor
        def _(pe):
            pe.wait_ge(weights_in, 96)

            def first(g, u):
                for m in range(KH):
                    pe.wait_ge(aT_done.sem, aT_done.room(g * KH + m))
                    for k in range(KH):
                        mm = nc.tensor.matmul(a_ps[m][:], wa[:, k, m * P:(m + 1) * P], env.featT[:, bass.ds(g * 2, 2), k, :],
                                              start=(k == 0), stop=(k == KH - 1))
                    mm.then_inc(a_done.sem, 1)

            def second(g, u, s):
                t = g * SUB + s
                if s == 0:
                    pe.wait_ge(aT_done.sem, aT_done.after(g * KH + 1))
                pe.wait_ge(zb_done.sem, zb_done.room(t))
                for k in range(KH):
                    mm = nc.tensor.matmul(z_ps[s % 2][:, 0:HID], aT[:, u, k, s * P:(s + 1) * P], wb[:, k, :],
                                          start=(k == 0), stop=(k == KH - 1))
                mm.then_inc(z_done.sem, 1)

            def turn(g, u, c):
                if c == 0:
                    pe.wait_ge(h_done.sem, h_done.after(g))
                pe.wait_ge(hT_done.sem, hT_done.room(g * KH + c))
                for s in range(SUB):
                    mm = nc.tensor.transpose(hT_ps[c][:, s, :], h_row[:, u, s, c * P:(c + 1) * P], env.ident[:])
                mm.then_inc(hT_tp.sem, 1)

            first(0, 0)

            def step(g, u, q):
                if inside(g + 1, T) and inside(g, T):
                    first(g + 1, 1 - u)
                if inside(g, T):
                    for s in range(SUB):
                        second(g, u, s)
                if inside(g - 1, T):
                    for c in range(KH):
                        turn(g - 1, 1 - u, c)

            run(pe, T, 2, 1, step, last=2)

        @block.scalar
        def _(act):
            aT_done.open(act)
            hT_done.open(act)
            act.wait_ge(weights_in, 96)

            def relu(g, u):
                for m in range(KH):
                    act.wait_ge(a_done.sem, a_done.after(g * KH + m))
                    if inside(g - 2, T):
                        act.wait_ge(z_done.sem, z_done.after((g - 2) * SUB + 3))
                    nc.scalar.activation(aT[:, u, m, :], a_ps[m][:], ACT.Relu, bias=ba_col[:, m:m + 1]).then_inc(aT_done.sem, 1)

            relu(0, 0)

            def step(g, u, q):
                if inside(g + 1, T) and inside(g, T):
                    relu(g + 1, 1 - u)
                if inside(g - 1, T):
                    for c in range(KH):
                        k = (g - 1) * KH + c
                        act.wait_ge(hT_tp.sem, hT_tp.after(k))
                        nc.scalar.activation(env.featT[:, bass.ds((g - 1) * 2, 2), c, :],
                                             hT_ps[c][:].rearrange("p (w t) n -> p w (t n)", w=2), ACT.Copy).then_inc(hT_done.sem, 1)
                if inside(g, T):
                    act.wait_ge(mom_done.sem, mom_done.after(g))
                    nc.scalar.activation(rstd[:], moments[:, :, 1], ACT.Sqrt, bias=env.eps[:, 1:2]).then_inc(sqrt_done.sem, 1)

            run(act, T, 2, 1, step, last=2)

        @block.gpsimd
        def _(pool):
            pool.wait_ge(weights_in, 96)

            def step(g, u, q):
                pool.wait_ge(norm_done.sem, norm_done.after(g))
                nc.gpsimd.tensor_tensor(z[:, u], z[:, u], ng_b[:].unsqueeze(1).broadcast_to([P, SUB, HID]),
                                        ALU.mult).then_inc(gain_done.sem, 1)
                pool.wait_ge(gain_done.sem, gain_done.after(g))
                nc.gpsimd.tensor_tensor(z[:, u], z[:, u], nb_b[:].unsqueeze(1).broadcast_to([P, SUB, HID]),
                                        ALU.add).then_inc(affine_done.sem, 1)

            run(pool, T, 2, 0, step)

        @block.vector
        def _(dve):
            v = nc.vector
            zb_done.open(dve)
            dve.wait_ge(weights_in, 96)
            chain = Chain(stage, dve, "layer_chain", 2 * SUB + 1)

            def step(g, u, q):
                chain.start(g)
                if inside(g, T):
                    for s in range(SUB):
                        t = g * SUB + s
                        dve.wait_ge(z_done.sem, z_done.after(t))
                        v.tensor_tensor(z[:, u, s, :], z_ps[s % 2][:, 0:HID], bb_b[:], ALU.add).then_inc(zb_done.sem, 1)
                        dve.wait_ge(zb_done.sem, zb_done.after(t))
                        m = chain.mark(v.bn_stats(stats[:, s, :], z[:, u, s, :]))
                        wait_apart(dve, (weights_in, 96), (chain.sem, m))
                        m = chain.mark(v.bn_aggr(moments[:, s, :], stats[:, s, :]))
                    dve.wait_ge(chain.sem, m)
                    v.tensor_copy(stats[:, 0, 0:1], moments[:, 0, 0:1]).then_inc(mom_done.sem, 1)
                if inside(g - 1, T):
                    w = 1 - u
                    dve.wait_ge(affine_done.sem, affine_done.after(g - 1))
                    dve.wait_ge(h_in[w], (q if u else q - 1) * 16 + 16) if not isinstance(g, int) else dve.wait_ge(h_in[w], ((g - 1) // 2) * 16 + 16)
                    v.scalar_tensor_tensor(h_row[:, w], z[:, w], 0.0, h_row[:, w], ALU.max, ALU.add).then_inc(h_done.sem, 1)
                if inside(g, T):
                    dve.wait_ge(sqrt_done.sem, sqrt_done.after(g))
                    chain.link(v.reciprocal(rstd[:], rstd[:]))
                    for s in range(SUB):
                        ins = v.tensor_scalar(z[:, u, s, :], z[:, u, s, :], moments[:, s, 0:1], rstd[:, s:s + 1],
                                              ALU.subtract, ALU.mult)
                    ins.then_inc(norm_done.sem, 1)

            run(dve, T, 2, 1, step)


def network_outputs(nc, env, Wd1, bd1, Wd2, bd2, out_g, out_b, x1_dram, out):
    with ExitStack() as ctx:
        stage = Stage(nc, ctx, "post")
        sb, ps, sem, done = stage.sb, stage.ps, stage.sem, stage.done
        R = 4
        wd1 = sb("wd1", [P, KH, MID])
        wd2 = sb("wd2", [P, KM, D])
        bd1_col = sb("bd1_col", [P, KM])
        bd2_b = sb("bd2_b", [P, D])
        g_b = sb("g_b", [P, D])
        b_b = sb("b_b", [P, D])
        dT = sb("dT", [P, 2, KM, GROUP])
        x1 = sb("x1", [P, R, D])
        x1b = sb("x1b", [P, 2, D])
        x1o = sb("x1o", [P, 2, D])
        y = sb("y", [P, R, D])
        stats = sb("stats5", [P, 2, 2, 6])
        moments = sb("moments5", [P, 2, 2, 2])
        rstd = sb("rstd5", [P, 2, 2])
        shift = sb("shift5", [P, 2, 2])
        d_ps = [ps(f"d_ps{i}", [P, GROUP]) for i in range(2)]
        delta_ps = [ps(f"delta_ps{i}", [P, D]) for i in range(3)]

        weights_in = sem("weights_in5")
        x1_in = [sem(f"x1_in{u}") for u in range(R)]
        out_done = [sem(f"out_done{u}") for u in range(R)]
        d_done = done("d_done")
        dT_done = done("dT_done", 2)
        delta_done = done("delta_done")
        x1b_done = done("x1b_done")
        x1o_done = done("x1o_done", R)
        v_done = done("v_done5", 2)
        mom_done = [done(f"mom5_{i}") for i in range(2)]
        sqrt_done = [done(f"sqrt5_{i}") for i in range(2)]
        norm_done = [done(f"norm5_{i}") for i in range(2)]
        y_done = done("y_done5")
        w_done = done("w_done5", 2)
        z_done = done("z_done5")
        ctx.callback(stage.clear)
        block = ctx.enter_context(nc.Block())
        T = TILES
        U = 2 * SUB

        @block.sync
        def _(sp):
            sp.dma_start(wd1[:], Wd1.rearrange("(k p) n -> p k n", p=P)).then_inc(weights_in, 16)
            with nc.allow_non_contiguous_dma("a column of weights"):
                sp.dma_start(bd1_col[:], bd1.rearrange("(k p) -> p k", p=P)).then_inc(weights_in, 16)
            sp.dma_start(wd2[:], Wd2.rearrange("(k p) n -> p k n", p=P)).then_inc(weights_in, 16)
            for to, of in ((bd2_b, bd2), (g_b, out_g), (b_b, out_b)):
                sp.dma_start(to[:], of.partition_broadcast(P)).then_inc(weights_in, 16)

            def step(t, u, q):
                if inside(t, T):
                    sp.wait_ge(x1o_done.sem, x1o_done.room(t))
                    sp.dma_start(x1[:, u % R, :], x1_dram[bass.ds(t * P, P), :]).then_inc(x1_in[u % R], 16)

            run(sp, T, R, 0, step)

        @block.gpsimd
        def _(pool):
            x1o_done.open(pool)
            pool.wait_ge(weights_in, 96)

            def step(t, u, q):
                pool.wait_ge(x1_in[u], q * 16 + 16)
                pool.wait_ge(v_done.sem, v_done.room(t))
                nc.gpsimd.tensor_tensor(x1b[:, u % 2, :], x1[:, u, :], bd2_b[:], ALU.add).then_inc(x1b_done.sem, 1)
                pool.wait_ge(w_done.sem, w_done.room(t))
                nc.gpsimd.tensor_tensor(x1o[:, u % 2, :], x1[:, u, :], b_b[:], ALU.add).then_inc(x1o_done.sem, 1)

            run(pool, T, R, 0, step)

        @block.tensor
        def _(pe):
            pe.wait_ge(weights_in, 96)

            def first(g, w, m):
                pe.wait_ge(dT_done.sem, dT_done.room(g * KM + m))
                for k in range(KH):
                    mm = nc.tensor.matmul(d_ps[m % 2][:], wd1[:, k, m * P:(m + 1) * P], env.featT[:, bass.ds(g * 2, 2), k, :],
                                          start=(k == 0), stop=(k == KH - 1))
                mm.then_inc(d_done.sem, 1)

            for m in range(KM):
                first(0, 0, m)

            def step(t, u, q):
                w, s = u // SUB, u % SUB
                g = q * 2 + w
                pe.wait_ge(dT_done.sem, dT_done.after(g * KM + KM - 1))
                pe.wait_ge(v_done.sem, v_done.after(t - 2)) if inside(t - 2, T) else None
                for n in range(2):
                    for k in range(KM):
                        mm = nc.tensor.matmul(delta_ps[u % 2][:, n * 512:(n + 1) * 512], dT[:, w, k, s * P:(s + 1) * P],
                                              wd2[:, k, n * 512:(n + 1) * 512], start=(k == 0), stop=(k == KM - 1))
                mm.then_inc(delta_done.sem, 1)
                if inside(g + 1, GROUPS):
                    first(g + 1, 1 - w, s)

            run(pe, T, U, 0, step, last=U)

        @block.scalar
        def _(act):
            dT_done.open(act)
            act.wait_ge(weights_in, 96)

            def relu(g, w, m):
                act.wait_ge(d_done.sem, d_done.after(g * KM + m))
                if inside(g - 2, GROUPS):
                    act.wait_ge(delta_done.sem, delta_done.after((g - 2) * SUB + 3))
                nc.scalar.activation(dT[:, w, m, :], d_ps[m % 2][:], ACT.Relu, bias=bd1_col[:, m:m + 1]).then_inc(dT_done.sem, 1)

            def root(t, i):
                scaled = (y_done, z_done)[i]
                if inside(t - 1, T):
                    act.wait_ge(scaled.sem, scaled.after(t - 1))
                act.wait_ge(mom_done[i].sem, mom_done[i].after(t))
                nc.scalar.activation(rstd[:, i, 0:1], moments[:, i, 0, 1:2], ACT.Sqrt, bias=env.eps[:, 1:2]).then_inc(sqrt_done[i].sem, 1)

            def scale(t, r, i, to):
                act.wait_ge(norm_done[i].sem, norm_done[i].after(t))
                nc.scalar.activation(y[:, r, :], y[:, r, :], ACT.Identity, bias=shift[:, i, 0:1],
                                     scale=rstd[:, i, 0:1]).then_inc(to.sem, 1)

            for m in range(KM):
                relu(0, 0, m)

            def step(t, u, q):
                w, s = u // SUB, u % SUB
                if inside(t, T):
                    root(t, 0)
                if inside(t - 1, T):
                    root(t - 1, 1)
                if inside(t, T):
                    scale(t, u % R, 0, y_done)
                    g = q * 2 + w
                    if inside(g + 1, GROUPS):
                        relu(g + 1, 1 - w, s)
                if inside(t - 1, T):
                    k, r = t - 1, (u - 1) % R
                    scale(k, r, 1, z_done)
                    act.wait_ge(z_done.sem, z_done.after(k))
                    if not isinstance(k, int) or tile_rows(k) == P:
                        act.dma_start(out[bass.ds(k * P, P), :], y[:, r, :]).then_inc(out_done[r], 16)
                    elif tile_rows(k):
                        n = tile_rows(k)
                        act.dma_start(out[k * P:k * P + n, :], y[0:n, r, :]).then_inc(out_done[r], 16)

            run(act, T, U, 1, step, last=U)
            for r in range(R):
                act.wait_ge(out_done[r], 16 * sum(1 for t in range(r, T, R) if tile_rows(t)))

        @block.vector
        def _(dve):
            v = nc.vector
            v_done.open(dve)
            w_done.open(dve)
            dve.wait_ge(weights_in, 96)
            chains = (Chain(stage, dve, "inner_chain", 3), Chain(stage, dve, "outer_chain", 4))

            def spread(t, r, i):
                chain = chains[i]
                for n in range(2):
                    m = chain.mark(v.bn_stats(stats[:, i, n, :], y[:, r, n * 512:(n + 1) * 512]))
                wait_apart(dve, (weights_in, 96), (chain.sem, m))
                v.bn_aggr(moments[:, i, 0, :], stats[:, i].rearrange("p n c -> p (n c)")).then_inc(mom_done[i].sem, 1)

            def norm(t, i):
                dve.wait_ge(sqrt_done[i].sem, sqrt_done[i].after(t))
                chains[i].link(v.reciprocal(rstd[:, i, 0:1], rstd[:, i, 0:1]))
                v.scalar_tensor_tensor(shift[:, i, 0:1], moments[:, i, 0, 0:1], -1.0, rstd[:, i, 0:1], ALU.mult,
                                       ALU.mult).then_inc(norm_done[i].sem, 1)

            def step(t, u, q):
                r = u % R
                chains[0].start(t)
                chains[1].start(t - 1)
                if inside(t, T):
                    dve.wait_ge(delta_done.sem, delta_done.after(t))
                    dve.wait_ge(x1b_done.sem, x1b_done.after(t))
                    if not isinstance(t, int) or t >= R:
                        dve.wait_ge(out_done[r], (q * 2 + u // R) * 16 if not isinstance(t, int) else t // R * 16)
                    v.tensor_tensor(y[:, r, :], delta_ps[u % 2][:], x1b[:, u % 2, :], ALU.add).then_inc(v_done.sem, 1)
                    dve.wait_ge(v_done.sem, v_done.after(t))
                    spread(t, r, 0)
                if inside(t - 1, T):
                    k, p = t - 1, (u - 1) % R
                    dve.wait_ge(y_done.sem, y_done.after(k))
                    chains[1].link(v.tensor_tensor(y[:, p, :], y[:, p, :], g_b[:], ALU.mult))
                    dve.wait_ge(x1o_done.sem, x1o_done.after(k))
                    v.tensor_tensor(y[:, p, :], y[:, p, :], x1o[:, p % 2, :], ALU.add).then_inc(w_done.sem, 1)
                    dve.wait_ge(w_done.sem, w_done.after(k))
                    spread(k, p, 1)
                if inside(t, T):
                    norm(t, 0)
                if inside(t - 1, T):
                    norm(t - 1, 1)

            run(dve, T, U, 1, step)


def build(nc, x, src, dst, L0_gnn_rms_w, L0_gnn_W_down, L0_gnn_Wl, L0_gnn_Wr, L0_gnn_att, L0_gnn_W_up, L1_gnn_ln_in_g,
          L1_gnn_ln_in_b, L1_gnn_W1, L1_gnn_b1, L1_gnn_W2, L1_gnn_b2, L1_gnn_layer_Wa, L1_gnn_layer_ba,
          L1_gnn_layer_Wb, L1_gnn_layer_bb, L1_gnn_layer_ng, L1_gnn_layer_nb, L1_gnn_Wd1, L1_gnn_bd1, L1_gnn_Wd2,
          L1_gnn_bd2, L1_gnn_out_g, L1_gnn_out_b, out):
    slots = nc.dram_tensor("slots", (SLOTS, 2), I32, kind="Internal").ap()
    item_tiles = nc.dram_tensor("item_tiles", (2, 2 * P), I32, kind="Internal").ap()
    moves = nc.dram_tensor("moves", (EP, 2 * EC, 3), I32, kind="Internal").ap()
    xl = nc.dram_tensor("xl_rows", (ROWS, HID), F32, kind="Internal").ap()
    xr = nc.dram_tensor("xr_rows", (ROWS, HID), F32, kind="Internal").ap()
    x1 = nc.dram_tensor("x1_rows", (ROWS, D), F32, kind="Internal").ap()
    h = nc.dram_tensor("h_rows", (ROWS, HID), F32, kind="Internal").ap()
    with ExitStack() as ctx:
        env = consts(nc, ctx)
        place_edges(nc, env, src, dst, slots, item_tiles, moves)
        attention_inputs(nc, env, x, L0_gnn_W_down, L0_gnn_Wl, L0_gnn_Wr, L0_gnn_rms_w, L0_gnn_att, xl, xr, slots, moves)
        attention_edges(nc, env, L0_gnn_att, xl, xr, slots)
        network_inputs(nc, env, x, L0_gnn_W_up, L1_gnn_ln_in_g, L1_gnn_ln_in_b, L1_gnn_W1, L1_gnn_b1, L1_gnn_W2,
                       L1_gnn_b2, x1, h)
        for i in range(LAYERS):
            add_neighbours(nc, env, i, h)
            layer(nc, env, i, L1_gnn_layer_Wa[i], L1_gnn_layer_ba[i], L1_gnn_layer_Wb[i], L1_gnn_layer_bb[i],
                  L1_gnn_layer_ng[i], L1_gnn_layer_nb[i], h)
        network_outputs(nc, env, L1_gnn_Wd1, L1_gnn_bd1, L1_gnn_Wd2, L1_gnn_bd2, L1_gnn_out_g, L1_gnn_out_b, x1, out)


_INS = ['x', 'src', 'dst', 'L0_gnn_rms_w', 'L0_gnn_W_down', 'L0_gnn_Wl', 'L0_gnn_Wr', 'L0_gnn_att', 'L0_gnn_W_up',
        'L1_gnn_ln_in_g', 'L1_gnn_ln_in_b', 'L1_gnn_W1', 'L1_gnn_b1', 'L1_gnn_W2', 'L1_gnn_b2', 'L1_gnn_layer_Wa',
        'L1_gnn_layer_ba', 'L1_gnn_layer_Wb', 'L1_gnn_layer_bb', 'L1_gnn_layer_ng', 'L1_gnn_layer_nb', 'L1_gnn_Wd1',
        'L1_gnn_bd1', 'L1_gnn_Wd2', 'L1_gnn_bd2', 'L1_gnn_out_g', 'L1_gnn_out_b']


def kernel(**inputs):
    import numpy as _np
    import concourse.bacc as _bacc
    from concourse import mybir as _mybir
    from concourse.bass_utils import run_bass_kernel_spmd as _run

    nc = _bacc.Bacc("TRN2", target_bir_lowering=False, num_devices=1)
    arrays, args = {}, []
    for name in _INS:
        a = _np.ascontiguousarray(inputs[name])
        arrays[f"in_{name}_dram"] = a
        args.append(nc.dram_tensor(f"in_{name}_dram", a.shape, _mybir.dt.from_np(a.dtype), kind="ExternalInput").ap())
    args.append(nc.dram_tensor("out_0_dram", (N_NODES, D), F32, kind="ExternalOutput").ap())
    build(nc, *args)
    r = _run(nc, [arrays], core_ids=[0])
    return r.results[0]["out_0_dram"]
```

```python
from contextlib import ExitStack

import concourse.bass as bass
from concourse import mybir

ALU = mybir.AluOpType
ACT = mybir.ActivationFunctionType
AX = mybir.AxisListType
F32 = mybir.dt.float32
BF16 = mybir.dt.bfloat16
I32 = mybir.dt.int32
F32R = mybir.dt.float32r

P = 128
N_NODES = 10000
D = 1024
HID = 256
MID = 512
HEADS = 4
HD = HID // HEADS
HDA = HD + 1
EDGES = 12500
LAYERS = 3
RMS_EPS = 1e-6
LN_EPS = 1e-5
NEG_SLOPE = 0.2
DEN_EPS = 1e-16

GROUP = 512
SUB = GROUP // P
GROUPS = -(-N_NODES // GROUP)
TILES = GROUPS * SUB
ROWS = GROUPS * GROUP
KD = D // P
KH = HID // P
KM = MID // P
PAIR = 2 * P
WIDE = TILES // 2
ACC = HEADS * HDA
STRIDE = 2 * ACC

EP = 125
EC = EDGES // EP


def items_for(tiles, unroll):
    return -(-((EDGES + tiles * (P - 1)) // P) // unroll) * unroll


UA = 8
UL = 7
NARROW_TILES = -(-N_NODES // P)
WIDE_TILES = -(-N_NODES // PAIR)
ITEMS_A = items_for(NARROW_TILES, UA)
ITEMS_L = items_for(WIDE_TILES, UL)
SLOTS = P * (ITEMS_A + ITEMS_L)
MAGIC = 12582912.0
BIG = float(2.0 ** 100)
FIRST_SEM = 160
PAD_SRC = ROWS


class Done:

    def __init__(self, stage, name, slots=0, per=1):
        self.sem = stage.sem(name)
        self.slots, self.per = slots, per

    def open(self, eng):
        eng.sem_inc(self.sem, self.slots * self.per)

    def after(self, k):
        return k * self.per + (1 + self.slots) * self.per

    def room(self, k):
        return k * self.per + self.per


class Chain:

    def __init__(self, stage, eng, name, per):
        self.sem = stage.sem(name)
        self.eng, self.per, self.base, self.n = eng, per, 0, 0

    def start(self, k):
        self.base, self.n = k * self.per, 0

    def link(self, ins):
        ins.then_inc(self.sem, 1)
        self.n += 1
        assert self.n <= self.per
        self.eng.wait_ge(self.sem, self.base + self.n)

    def mark(self, ins):
        ins.then_inc(self.sem, 1)
        self.n += 1
        assert self.n <= self.per
        return self.base + self.n


def run(eng, total, unroll, skew, step, last=0):
    for i in range(unroll):
        step(i, i, 0)
    with eng.Fori(1, (total - last) // unroll) as q:
        for u in range(unroll):
            step(eng.snap(q * unroll + u), u, q)
    for i in range(total - last, total + skew):
        step(i, i % unroll, i // unroll)


def wait_apart(eng, reached, *waits):
    waits = [(sem, value if isinstance(value, int) else eng.to_reg(value)) for sem, value in waits]
    eng.wait_ge(*reached)
    for sem, value in waits:
        eng.wait_ge(sem, value)


def inside(k, total):
    return not isinstance(k, int) or 0 <= k < total


def tile_rows(t):
    return max(0, min(P, N_NODES - t * P))


class Env:
    pass


class Stage:

    def __init__(self, nc, ctx, name):
        self.nc, self.ctx, self.name = nc, ctx, name
        self.sems = []

    def sb(self, name, shape, dt=F32):
        return self.ctx.enter_context(self.nc.sbuf_tensor(f"{self.name}_{name}", shape, dt))

    def ps(self, name, shape):
        return self.ctx.enter_context(self.nc.psum_tensor(f"{self.name}_{name}", shape, F32))

    def sem(self, name):
        number = FIRST_SEM + len(self.sems)
        self.sems.append(number)
        return self.ctx.enter_context(self.nc.semaphore(f"{self.name}_{name}", num=number))

    def gpsimd_dma_sem(self, name):
        return self.ctx.enter_context(self.nc.semaphore(f"{self.name}_{name}"))

    def clear(self):
        self.nc.all_engine_barrier(sems_to_clear=range(FIRST_SEM, FIRST_SEM + len(self.sems)))

    def done(self, name, slots=0, per=1):
        return Done(self, name, slots, per)


def consts(nc, ctx):
    env = Env()

    def sb(name, shape, dt=F32):
        return ctx.enter_context(nc.sbuf_tensor(name, shape, dt))

    env.state = sb("state", [P, WIDE, STRIDE])
    env.acc = env.state[:].rearrange("p w (t h d) -> p (w t) h d", t=2, h=HEADS)
    env.featT = env.state[:, :, 0:2 * PAIR].rearrange("p w (c n) -> p w c n", c=KH)
    env.ident = sb("ident", [P, P])
    env.iota_row = sb("iota_row", [P, PAIR])
    env.nmax = sb("nmax", [P, TILES, HEADS])
    env.slots_a = sb("slots_a", [P, ITEMS_A, 2], I32)
    env.slots_l = sb("slots_l", [P, ITEMS_L, 2], I32)
    env.tile_a = sb("tile_a", [1, 2 * P], I32)
    env.tile_l = sb("tile_l", [1, 2 * P], I32)
    env.eps = sb("eps", [P, 2])
    return env


def place_edges(nc, env, src, dst, slots_dram, item_tiles_dram, moves_dram):
    with ExitStack() as ctx:
        stage = Stage(nc, ctx, "place")
        sb, ps, sem, done = stage.sb, stage.ps, stage.sem, stage.done
        src_i = sb("src_i", [EP, EC], I32)
        dst_i = sb("dst_i", [EP, EC], I32)
        dst_f = sb("dst_f", [EP, EC])
        tile_f = sb("tile_f", [EP, EC])
        tile_no = sb("tile_no", [EP, TILES])
        onehot = sb("onehot", [EP, TILES, EC])
        rank = sb("rank", [EP, TILES, EC])
        zeros = sb("zeros", [EP, TILES, EC], BF16)
        count = sb("count", [EP, TILES])
        total = sb("total", [P, TILES])
        items = sb("items", [P, TILES])
        ends = sb("ends", [P, TILES])
        shift = sb("shift", [P, TILES])
        ones_t = sb("ones_t", [P, TILES])
        position = sb("position", [EP, EC])
        item_f = sb("item_f", [EP, EC])
        before = sb("before", [EP, P])
        ones = sb("ones", [EP, P])
        item_no = sb("item_no", [P, 2])
        item_tile = sb("item_tile", [P, 2, 2])
        item_tile_i = sb("item_tile_i", [P, 2, 2], I32)
        le_junk = sb("le_junk", [P, TILES])
        moves = sb("moves", [EP, 2 * EC, 3], I32)
        blank = sb("blank", [P, ITEMS_A + ITEMS_L, 2], I32)
        base_ps = ps("base_ps", [P, 512])
        total_ps = ps("total_ps", [P, 512])
        edges_in = sem("edges_in")
        made = sem("made")
        counted = sem("counted")
        summed = sem("summed")
        placed = sem("placed")
        blank_out = sem("blank_out")
        out_done = sem("out_done")
        widths = ((P, NARROW_TILES, ITEMS_A, 0), (PAIR, WIDE_TILES, ITEMS_L, P * ITEMS_A))

        ctx.callback(stage.clear)
        block = ctx.enter_context(nc.Block())

        @block.sync
        def _(sp):
            sp.dma_start(src_i[:], src.rearrange("(p c) -> p c", p=EP)).then_inc(edges_in, 16)
            sp.dma_start(dst_i[:], dst.rearrange("(p c) -> p c", p=EP)).then_inc(edges_in, 16)
            sp.wait_ge(made, 8)
            sp.dma_start(slots_dram.rearrange("(p k) c -> p k c", p=P), blank[:]).then_inc(blank_out, 16)
            sp.wait_ge(placed, 2)
            sp.dma_start(moves_dram, moves[:]).then_inc(out_done, 16)
            for w in range(2):
                sp.dma_start(item_tiles_dram[w].rearrange("(p c) -> p c", p=P), item_tile_i[:, w, :]).then_inc(out_done, 16)
            sp.wait_ge(out_done, 48)
            sp.wait_ge(blank_out, 16)
            for w, t in enumerate((env.tile_a, env.tile_l)):
                sp.dma_start(t[:], item_tiles_dram[w:w + 1, :]).then_inc(out_done, 16)
            sp.wait_ge(out_done, 80)

        @block.gpsimd
        def _(pool):
            one = pool.to_reg(1.0)
            zero = pool.to_reg(0.0)
            nc.gpsimd.iota(tile_no[:], pattern=[[1, TILES]], base=0, channel_multiplier=0, allow_small_or_imprecise_dtypes=True).then_inc(made, 1)
            nc.gpsimd.iota(item_no[:], pattern=[[1, 2]], base=0, channel_multiplier=2, allow_small_or_imprecise_dtypes=True).then_inc(made, 1)
            nc.gpsimd.memset(ones[:], 1.0).then_inc(made, 1)
            pool.wait_ge(made, 3)
            nc.gpsimd.affine_select(out=before[:], in_=ones[:], compare_op=ALU.is_gt, fill=zero, base=0,
                                    pattern=[[1, P]], channel_multiplier=-1).then_inc(made, 1)
            nc.gpsimd.memset(ones_t[:], 1.0).then_inc(made, 1)
            nc.gpsimd.memset(zeros[:], 0.0).then_inc(made, 1)
            nc.gpsimd.memset(blank[:, :, 0:1], PAD_SRC).then_inc(made, 1)
            nc.gpsimd.memset(blank[:, :, 1:2].bitcast(F32), -1.0).then_inc(made, 1)
            nc.gpsimd.iota(env.iota_row[:], pattern=[[1, PAIR]], base=0, channel_multiplier=0, allow_small_or_imprecise_dtypes=True).then_inc(made, 1)
            nc.gpsimd.memset(env.ident[:], 0.0).then_inc(made, 1)
            pool.wait_ge(made, 10)
            nc.gpsimd.affine_select(out=env.ident[:], in_=env.ident[:], compare_op=ALU.not_equal, fill=one, base=0,
                                    pattern=[[-1, P]], channel_multiplier=1).then_inc(made, 1)
            nc.gpsimd.memset(env.eps[:, 0:1], RMS_EPS).then_inc(made, 1)
            nc.gpsimd.memset(env.eps[:, 1:2], LN_EPS).then_inc(made, 1)

        @block.tensor
        def _(pe):
            pe.wait_ge(made, 8)
            for w in range(2):
                pe.wait_ge(counted, w + 1)
                nc.tensor.matmul(base_ps[:, 0:TILES], before[:], count[:], start=True, stop=True)
                nc.tensor.matmul(total_ps[:, 0:TILES], ones[:], count[:], start=True, stop=True).then_inc(summed, 1)

        @block.vector
        def _(dve):
            v = nc.vector
            chain = Chain(stage, dve, "place_chain", 64)
            link = chain.link
            dve.wait_ge(edges_in, 32)
            dve.wait_ge(made, 13)
            link(v.tensor_copy(dst_f[:], dst_i[:]))
            for w, (width, tiles, n_items, row0) in enumerate(widths):
                link(v.tensor_scalar(tile_f[:], dst_f[:], -(width - 1) / 2.0, 1.0 / width, ALU.add, ALU.mult))
                link(v.tensor_scalar(tile_f[:], tile_f[:], MAGIC, MAGIC, ALU.add, ALU.subtract))
                hot = onehot[:, 0:tiles, :]
                rk = rank[:, 0:tiles, :]
                link(v.tensor_tensor(hot, tile_f[:].unsqueeze(1).broadcast_to([EP, tiles, EC]),
                                     tile_no[:, 0:tiles].unsqueeze(2).broadcast_to([EP, tiles, EC]), ALU.is_equal))
                link(v.tensor_tensor_scan(rk.rearrange("p t c -> p (t c)"), hot.rearrange("p t c -> p (t c)"),
                                          zeros[:, 0:tiles, :].rearrange("p t c -> p (t c)"), 0.0, ALU.add, ALU.add))
                if tiles < TILES:
                    link(v.memset(count[:, tiles:TILES], 0.0))
                link(v.tensor_copy(count[:, 0:1], rk[:, 0, EC - 1:EC]))
                link(v.tensor_tensor(count[:, 1:tiles], rk[:, 1:tiles, EC - 1], rk[:, 0:tiles - 1, EC - 1], ALU.subtract))
                v.tensor_copy(ones_t[:, 0:1], ones_t[:, 0:1]).then_inc(counted, 1)
                dve.wait_ge(summed, w + 1)
                link(v.tensor_scalar(total[:], total_ps[:, 0:TILES], P / 2.0 - 0.5, 1.0 / P, ALU.add, ALU.mult))
                link(v.tensor_scalar(items[:], total[:], MAGIC, MAGIC, ALU.add, ALU.subtract))
                link(v.tensor_tensor_scan(ends[:], ones_t[:], items[:], 0.0, ALU.mult, ALU.add))
                link(v.tensor_tensor(shift[:], ends[:], items[:], ALU.subtract))
                link(v.tensor_scalar(shift[:], shift[:], float(P), -1.0, ALU.mult, ALU.add))
                link(v.tensor_tensor(shift[:], base_ps[:, 0:TILES], shift[:], ALU.add))
                link(v.tensor_tensor(shift[0:EP, 1:tiles], shift[0:EP, 1:tiles], rk[:, 0:tiles - 1, EC - 1], ALU.subtract))
                link(v.tensor_tensor(rk, rk, shift[0:EP, 0:tiles].unsqueeze(2).broadcast_to([EP, tiles, EC]), ALU.add))
                link(v.tensor_tensor(rk, rk, hot, ALU.mult))
                link(v.tensor_reduce(position[:], rk.rearrange("p t c -> p c t"), AX.X, ALU.add))
                link(v.tensor_scalar(item_f[:], position[:], -(P - 1) / 2.0, 1.0 / P, ALU.add, ALU.mult))
                link(v.tensor_scalar(item_f[:], item_f[:], MAGIC, MAGIC, ALU.add, ALU.subtract))
                link(v.tensor_scalar(item_f[:], item_f[:], -float(P * n_items - 1), float(row0), ALU.mult, ALU.add))
                link(v.scalar_tensor_tensor(position[:], position[:], float(n_items), item_f[:], ALU.mult, ALU.add))
                mv = moves[:, w * EC:(w + 1) * EC, :]
                link(v.tensor_copy(mv[:, :, 0], position[:]))
                link(v.tensor_copy(mv[:, :, 1], src_i[:]))
                link(v.scalar_tensor_tensor(mv[:, :, 2].bitcast(F32), tile_f[:], -float(width), dst_f[:], ALU.mult, ALU.add))
                for c in range(2):
                    link(v.tensor_scalar(le_junk[:, 0:tiles], ends[:, 0:tiles], item_no[:, c:c + 1], None, ALU.is_le))
                    link(v.tensor_reduce(item_tile[:, w, c:c + 1], le_junk[:, 0:tiles], AX.X, ALU.add))
                link(v.tensor_scalar(item_tile[:, w, :], item_tile[:, w, :], float(tiles - 1), None, ALU.min))
                v.tensor_copy(item_tile_i[:, w, :], item_tile[:, w, :]).then_inc(placed, 1)


def attention_inputs(nc, env, x, W_down, Wl, Wr, rms_w, att, xl_dram, xr_dram, slots_dram, moves_dram):
    with ExitStack() as ctx:
        stage = Stage(nc, ctx, "pre")
        sb, ps, sem, done = stage.sb, stage.ps, stage.sem, stage.done
        wd = [sb(f"wd_{n}", [P, KD, HID], F32R) for n in ("hi", "lo")]
        wlr = [sb(f"wlr_{n}", [P, KH, 2 * HID], F32R) for n in ("hi", "lo")]
        xT = [sb(f"xT_{n}", [P, 2, KD, PAIR], F32R) for n in ("hi", "lo")]
        yT = [sb(f"yT_{n}", [P, 2, KH, PAIR], F32R) for n in ("hi", "lo")]
        wd_whole = sb("wd_whole", [P, KD, HID])
        wlr_whole = sb("wlr_whole", [P, KH, 2 * HID])
        rw = sb("rw", [P, KD])
        att_b = sb("att_b", [P, HID])
        moves = sb("moves_sb", [EP, 2 * EC, 3], I32)
        move_ring = sb("move_ring", [EP, 2, 3], I32)
        x_buf = sb("x_buf", [P, 4, D])
        square = sb("square", [P, D])
        xlr = sb("xlr", [P, 4, 2 * HID])
        ms = sb("ms", [P, TILES])
        rstd = sb("rstd", [P, TILES])
        s_sum = sb("s_sum", [P, HID])
        s_leaky = sb("s_leaky", [P, HID])
        s_att = sb("s_att", [P, HID])
        xT_ps = [ps(f"xT_ps{j}", [P, KD, P]) for j in range(2)]
        y_ps = [ps(f"y_ps{u}", [P, KH, PAIR]) for u in range(2)]
        xlr_ps = [ps(f"xlr_ps{j}", [P, 2 * HID]) for j in range(2)]

        weights_in = sem("weights_in")
        split = sem("split")
        den_set = sem("den_set")
        x_in = [sem(f"x_in{s}") for s in range(4)]
        xt_tp = done("xt_tp", 4)
        x_hi = done("x_hi1")
        x_lo = done("x_lo1")
        sq_done = done("sq_done", 4)
        rms_sqrt = done("rms_sqrt")
        rms_done = done("rms_done")
        y_done = done("y_done")
        y_hi = done("y_hi")
        y_lo = done("y_lo")
        xlr_done = done("xlr_done")
        xlr_out = done("xlr_out", 2)
        self_done = done("self_done", 4)
        acc_done = done("acc_done", 4)
        stored = [sem(f"stored{s}") for s in range(4)]
        scattered = [stage.gpsimd_dma_sem(f"scattered{i}") for i in range(2)]

        ctx.callback(stage.clear)
        block = ctx.enter_context(nc.Block())
        T = WIDE
        SPLITS = 4 + KD

        def products(out, lhs, rhs, n_k):
            for a, b in ((0, 0), (0, 1), (1, 0)):
                for k in range(n_k):
                    mm = nc.tensor.matmul(out, lhs(a, k), rhs(b, k), start=(a == b == 0 and k == 0),
                                          stop=(a == 1 and k == n_k - 1))
            return mm

        @block.sync
        def _(sp):
            sp.dma_start(wd_whole[:], W_down.rearrange("(k p) n -> p k n", p=P)).then_inc(weights_in, 16)
            with nc.allow_non_contiguous_dma("a column of weights"):
                sp.dma_start(rw[:], rms_w.rearrange("(k p) -> p k", p=P)).then_inc(weights_in, 16)

            def load(p, u, j):
                t, s = p * 2 + j, u * 2 + j
                if inside(p - 2, T):
                    sp.wait_ge(xt_tp.sem, xt_tp.room(t))
                    sp.wait_ge(sq_done.sem, sq_done.room(t))
                if not isinstance(p, int) or tile_rows(t) == P:
                    sp.dma_start(x_buf[:, s, :], x[bass.ds(t * P, P), :]).then_inc(x_in[s], 16)
                else:
                    n = tile_rows(t)
                    if n:
                        sp.dma_start(x_buf[0:n, s, :], x[t * P:t * P + n, :]).then_inc(x_in[s], 16)
                    sp.dma_start(x_buf[n:P, s, :], x[0:P - n, :]).then_inc(x_in[s], 16)

            def step(p, u, q):
                load(p, u, 0)
                load(p, u, 1)
                if isinstance(p, int) and p == 0:
                    sp.dma_start(wlr_whole[:, :, 0:HID], Wl.rearrange("(k p) n -> p k n", p=P)).then_inc(weights_in, 16)
                    sp.dma_start(wlr_whole[:, :, HID:2 * HID], Wr.rearrange("(k p) n -> p k n", p=P)).then_inc(weights_in, 16)
                    sp.dma_start(att_b[:], att.rearrange("h d -> (h d)").partition_broadcast(P)).then_inc(weights_in, 16)
                    sp.dma_start(moves[:], moves_dram).then_inc(weights_in, 16)

            run(sp, T, 2, 0, step, last=2)

        def landed(p, q, j):
            extra = 16 if isinstance(p, int) and 0 < tile_rows(p * 2 + j) < P else 0
            return q * 16 + 16 + extra

        @block.tensor
        def _(pe):
            xt_tp.open(pe)

            def turn(p, u, q, j):
                t, s = p * 2 + j, u * 2 + j
                pe.wait_ge(x_in[s], landed(p, q, j))
                if inside(p - 1, T):
                    pe.wait_ge(x_lo.sem, x_lo.after(t - 2))
                for k in range(KD):
                    mm = nc.tensor.transpose(xT_ps[j][:, k, :], x_buf[:, s, k * P:(k + 1) * P], env.ident[:])
                mm.then_inc(xt_tp.sem, 1)

            def down(p, u, m):
                if m == 0:
                    pe.wait_ge(x_lo.sem, x_lo.after(p * 2 + 1))
                    if inside(p - 2, T):
                        pe.wait_ge(y_lo.sem, y_lo.after(p - 2))
                mm = products(y_ps[u][:, m, :], lambda a, k: wd[a][:, k, m * P:(m + 1) * P], lambda b, k: xT[b][:, u, k, :], KD)
                if m == KH - 1:
                    mm.then_inc(y_done.sem, 1)

            def left_right(p, u, j):
                t = p * 2 + j
                if j == 0:
                    pe.wait_ge(y_lo.sem, y_lo.after(p))
                pe.wait_ge(xlr_out.sem, xlr_out.room(t))
                mm = products(xlr_ps[j][:], lambda a, k: yT[a][:, u, k, j * P:(j + 1) * P], lambda b, k: wlr[b][:, k, :], KH)
                mm.then_inc(xlr_done.sem, 1)

            turn(0, 0, 0, 0)
            turn(0, 0, 0, 1)
            pe.wait_ge(split, SPLITS)

            def step(p, u, q):
                nxt = inside(p + 1, T) and inside(p, T)
                for j in range(2):
                    if nxt:
                        turn(p + 1, 1 - u, q + u, j)
                    if inside(p, T):
                        down(p, u, j)
                for j in range(2):
                    if inside(p - 1, T):
                        left_right(p - 1, 1 - u, j)

            run(pe, T, 2, 1, step, last=2)

        @block.scalar
        def _(act):
            sq_done.open(act)
            xlr_out.open(act)

            def part_x(p, u, j):
                t = p * 2 + j
                act.wait_ge(xt_tp.sem, xt_tp.after(t))
                if inside(p - 2, T):
                    act.wait_ge(y_done.sem, y_done.after(p - 2))
                nc.scalar.activation(xT[0][:, u, :, j * P:(j + 1) * P], xT_ps[j][:], ACT.Copy).then_inc(x_hi.sem, 1)

            def square_up(p, u, q, j):
                t, s = p * 2 + j, u * 2 + j
                act.wait_ge(x_in[s], landed(p, q, j))
                act.wait_ge(sq_done.sem, sq_done.after(t - 1))
                nc.scalar.activation(square[:], x_buf[:, s, :], ACT.Square, accum_out=ms[:, bass.ds(t, 1)]).then_inc(sq_done.sem, 1)

            def root(p):
                act.wait_ge(sq_done.sem, sq_done.after(p * 2 + 1))
                nc.scalar.activation(rstd[:, bass.ds(p * 2, 2)], ms[:, bass.ds(p * 2, 2)], ACT.Sqrt,
                                     bias=env.eps[:, 0:1], scale=1.0 / D).then_inc(rms_sqrt.sem, 1)

            def part_y(p, u):
                act.wait_ge(y_done.sem, y_done.after(p))
                if inside(p - 2, T):
                    act.wait_ge(xlr_done.sem, xlr_done.after(p * 2 - 3))
                nc.scalar.activation(yT[0][:, u], y_ps[u][:], ACT.Copy).then_inc(y_hi.sem, 1)

            def scale_out(p, u, q, j):
                t, s = p * 2 + j, u * 2 + j
                act.wait_ge(xlr_done.sem, xlr_done.after(t))
                readers = [(rms_done.sem, rms_done.after(p)), (self_done.sem, self_done.room(t)), (acc_done.sem, acc_done.room(t))]
                if inside(p - 2, T):
                    readers.append((stored[s], q * 32))
                wait_apart(act, (weights_in, 96), *readers)
                nc.scalar.activation(xlr[:, s, :], xlr_ps[j][:], ACT.Copy, scale=rstd[:, bass.ds(t, 1)]).then_inc(xlr_out.sem, 1)
                act.wait_ge(xlr_out.sem, xlr_out.after(t))
                act.dma_start(xl_dram[bass.ds(t * P, P), :], xlr[:, s, 0:HID]).then_inc(stored[s], 16)
                act.dma_start(xr_dram[bass.ds(t * P, P), :], xlr[:, s, HID:2 * HID]).then_inc(stored[s], 16)

            part_x(0, 0, 0)
            part_x(0, 0, 1)
            square_up(0, 0, 0, 0)
            square_up(0, 0, 0, 1)
            root(0)
            act.wait_ge(weights_in, 96)

            def step(p, u, q):
                nxt = inside(p + 1, T) and inside(p, T)
                if nxt:
                    part_x(p + 1, 1 - u, 0)
                    square_up(p + 1, 1 - u, q + u, 0)
                    square_up(p + 1, 1 - u, q + u, 1)
                    part_x(p + 1, 1 - u, 1)
                    root(p + 1)
                if inside(p, T):
                    part_y(p, u)
                if inside(p - 1, T):
                    for j in range(2):
                        scale_out(p - 1, 1 - u, q - 1 + u, j)

            run(act, T, 2, 1, step, last=2)
            for s in range(4):
                act.wait_ge(stored[s], T // 2 * 32)

        @block.vector
        def _(dve):
            v = nc.vector
            self_done.open(dve)
            chain = Chain(stage, dve, "self_chain", 6)

            def rest_x(p, u, j):
                dve.wait_ge(x_hi.sem, x_hi.after(p * 2 + j))
                v.tensor_tensor(xT[1][:, u, :, j * P:(j + 1) * P], xT_ps[j][:],
                                xT[0][:, u, :, j * P:(j + 1) * P].bitcast(F32), ALU.subtract).then_inc(x_lo.sem, 1)

            def recip(p):
                dve.wait_ge(rms_sqrt.sem, rms_sqrt.after(p))
                v.reciprocal(rstd[:, bass.ds(p * 2, 2)], rstd[:, bass.ds(p * 2, 2)]).then_inc(rms_done.sem, 1)

            def rest_y(p, u):
                dve.wait_ge(y_hi.sem, y_hi.after(p))
                v.tensor_tensor(yT[1][:, u], y_ps[u][:], yT[0][:, u].bitcast(F32), ALU.subtract).then_inc(y_lo.sem, 1)

            def self_score(p, u, j):
                t, s = p * 2 + j, u * 2 + j
                dve.wait_ge(xlr_out.sem, xlr_out.after(t))
                dve.wait_ge(self_done.sem, self_done.after(t - 1))
                chain.link(v.tensor_tensor(s_sum[:], xlr[:, s, 0:HID], xlr[:, s, HID:2 * HID], ALU.add))
                chain.link(v.scalar_tensor_tensor(s_leaky[:], s_sum[:], NEG_SLOPE, s_sum[:], ALU.mult, ALU.max))
                chain.link(v.tensor_tensor(s_att[:], s_leaky[:], att_b[:], ALU.mult))
                v.tensor_reduce(env.nmax[:, bass.ds(t, 1), :].rearrange("p a h -> p (a h)"),
                                s_att[:].rearrange("p (h d) -> p h d", h=HEADS), AX.X, ALU.add,
                                negate=True).then_inc(self_done.sem, 1)

            rest_x(0, 0, 0)
            rest_x(0, 0, 1)
            dve.wait_ge(weights_in, 96)
            for k in range(KD):
                v.tensor_scalar(wd_whole[:, k, :], wd_whole[:, k, :], rw[:, k:k + 1], None, ALU.mult).then_inc(split, 1)
            dve.wait_ge(split, KD)
            for i, (w, whole) in enumerate(((wd, wd_whole), (wlr, wlr_whole))):
                v.tensor_copy(w[0][:], whole[:]).then_inc(split, 1)
                dve.wait_ge(split, KD + 2 * i + 1)
                v.tensor_tensor(w[1][:], whole[:], w[0][:].bitcast(F32), ALU.subtract).then_inc(split, 1)
            recip(0)

            def step(p, u, q):
                nxt = inside(p + 1, T) and inside(p, T)
                chain.start(p - 2)
                for j in range(2):
                    if nxt:
                        rest_x(p + 1, 1 - u, j)
                    if inside(p - 2, T):
                        self_score(p - 2, u, j)
                if nxt:
                    recip(p + 1)
                if inside(p, T):
                    rest_y(p, u)

            run(dve, T, 2, 2, step, last=2)

        @block.gpsimd
        def _(pool):
            acc_done.open(pool)
            last_slot = pool.to_reg(SLOTS - 1)
            nc.gpsimd.memset(env.acc[:, :, :, HD:HDA], 1.0).then_inc(den_set, 1)
            pool.wait_ge(weights_in, 96)
            pool.wait_ge(den_set, 1)
            chain = Chain(stage, pool, "move_chain", 10)
            per = 2 * EC // GROUPS
            copies = {2: 0, 4: 1, 7: 2, 9: 3}

            def step(g, u, q):
                chain.start(g)
                for i in range(per):
                    if i < 2:
                        if inside(g - 1, GROUPS):
                            pool.wait_ge(scattered[i], g * (per // 2) * 16)
                    else:
                        pool.wait_ge(scattered[i % 2], g * (per // 2) * 16 + (i // 2) * 16)
                    v = chain.mark(nc.gpsimd.tensor_copy(move_ring[:, i % 2, :],
                                                         moves[:, bass.ds(g * per + i, 1), :].rearrange("p a c -> p (a c)")))
                    wait_apart(pool, (den_set, 1), (chain.sem, v))
                    pool.indirect_dma_start(
                        out=slots_dram, out_offset=bass.IndirectOffsetOnAxis(ap=move_ring[:, i % 2, 0:1], axis=0),
                        in_=move_ring[:, i % 2, 1:3], in_offset=None, bounds_check=last_slot,
                        oob_is_err=False).then_inc(scattered[i % 2], 16)
                    if i in copies:
                        s = copies[i]
                        t = g * SUB + s
                        pool.wait_ge(xlr_out.sem, xlr_out.after(t))
                        nc.gpsimd.tensor_copy(env.acc[:, bass.ds(t, 1), :, 0:HD].rearrange("p a h d -> p (a h) d"),
                                              xlr[:, s, 0:HID].rearrange("p (h d) -> p h d", h=HEADS)).then_inc(acc_done.sem, 1)

            run(pool, GROUPS, 1, 0, step)
            for i in range(2):
                pool.wait_ge(scattered[i], EC * 16)


def attention_edges(nc, env, att, xl_dram, xr_dram, slots_dram):
    with ExitStack() as ctx:
        stage = Stage(nc, ctx, "att")
        sb, ps, sem, done = stage.sb, stage.ps, stage.sem, stage.done
        R = UA
        att_b = sb("att_b2", [P, HID])
        index = sb("index", [P, R], I32)
        xl = sb("xl", [P, R, HID])
        xr = sb("xr", [P, R, HID])
        sel = sb("sel", [P, R, P])
        selT = sb("selT", [P, R, P])
        away = sb("away", [P, 4, P], BF16)
        message = sb("message", [P, 2, HID])
        leaky = sb("leaky", [P, HID])
        weighed = sb("weighed", [P, HID])
        score = sb("score", [P, R, HEADS])
        parts = sb("parts", [P, 2, 2, HEADS], F32R)
        scoreT = sb("scoreT", [2 * HEADS, 4, HEADS, P], F32R)
        head_col = sb("head_col", [2 * HEADS, HEADS])
        ones_row = sb("ones_row", [2 * HEADS, P])
        ones_r = sb("ones_r", [2 * HEADS, P], F32R)
        identb = sb("identb", [P, P], BF16)
        top = sb("top", [P, HEADS])
        nmax_new = sb("nmax_new", [P, R, HEADS])
        fall = sb("fall", [P, 2, HEADS])
        shrink = sb("shrink", [P, R, HEADS])
        under = sb("under", [P, 2, HEADS])
        part = sb("part", [P, 2, HEADS, HDA])
        added = sb("added", [P, 2, HEADS, HDA])

        selT_ps = ps("selT_ps", [P, 512])
        sum_ps = [ps(f"sum_ps{i}", [P, 512]) for i in range(2)]
        scoreT_ps = ps("scoreT_ps", [P, 512])
        wide_ps = [ps(f"wide_ps{i}", [P, HEADS, P]) for i in range(2)]
        under_ps = ps("under_ps", [P, 512])
        part_ps = ps("part_ps", [P, 512])

        tables_in = sem("tables_in")
        made = sem("made_c")
        xl_in = [stage.gpsimd_dma_sem(f"xl_in{u}") for u in range(R)]
        xr_in = [sem(f"xr_in{u}") for u in range(R)]
        index_done = done("index_done")
        sel_done = done("sel_done")
        selT_tp = done("selT_tp")
        selT_done = done("selT_done", 1)
        sum_done = done("sum_done", R)
        message_done = done("message_done", 2)
        score_done = done("score_done", 2)
        scoreT_tp = done("scoreT_tp")
        parts_done = done("parts_done", per=2)
        scoreT_done = done("scoreT_done", 1)
        wide_done = done("wide_done", 4)
        topped = done("topped", per=3)
        max_done = done("max_done", 2)
        shrink_done = done("shrink_done", 2)
        under_tp = done("under_tp")
        gap_done = done("gap_done")
        under_done = done("under_done", 2)
        prob_done = done("prob_done", 2)
        part_in = done("part_in", R)
        part_tp = done("part_tp", R)
        copied = done("part_copied", 1)
        acc_done = done("acc_done2", 2)

        ctx.callback(stage.clear)
        block = ctx.enter_context(nc.Block())
        T = ITEMS_A

        @block.sync
        def _(sp):
            sp.dma_start(env.slots_a[:], slots_dram[0:P * ITEMS_A, :].rearrange("(p k) c -> p k c", p=P)).then_inc(tables_in, 16)
            sp.dma_start(env.slots_l[:], slots_dram[P * ITEMS_A:SLOTS, :].rearrange("(p k) c -> p k c", p=P)).then_inc(tables_in, 16)
            sp.dma_start(att_b[:], att.rearrange("h d -> (h d)").partition_broadcast(P)).then_inc(tables_in, 16)

            def step(i, u, q):
                j = sp.value_load(env.tile_a[0:1, bass.ds(i, 1)], min_val=0, max_val=NARROW_TILES - 1)
                sp.wait_ge(sum_done.sem, sum_done.room(i))
                sp.dma_start(xr[:, u, :], xr_dram[bass.ds(j * P, P), :]).then_inc(xr_in[u], 16)

            run(sp, T, R, 0, step)

        @block.gpsimd
        def _(pool):
            one = pool.to_reg(1.0)
            last_row = pool.to_reg(ROWS - 1)
            nc.gpsimd.memset(xl[:], 0.0).then_inc(made, 1)
            nc.gpsimd.tensor_copy(identb[:], env.ident[:]).then_inc(made, 1)
            nc.gpsimd.memset(ones_row[:], 1.0).then_inc(made, 1)
            nc.gpsimd.memset(head_col[:], 0.0).then_inc(made, 1)
            pool.wait_ge(made, 4)
            nc.gpsimd.tensor_copy(ones_r[:], ones_row[:]).then_inc(made, 1)
            for n in range(2):
                nc.gpsimd.affine_select(out=head_col[:], in_=head_col[:], compare_op=ALU.not_equal, fill=one, base=-n * HEADS,
                                        pattern=[[-1, HEADS]], channel_multiplier=1).then_inc(made, 1)
                pool.wait_ge(made, 6 + n)
            pool.wait_ge(tables_in, 48)

            acc_done.open(pool)
            part_in.open(pool)
            shrunk = done("shrunk")

            def step(i, u, q):
                if inside(i, T):
                    pool.wait_ge(part_in.sem, part_in.room(i))
                    nc.gpsimd.tensor_copy(index[:, u:u + 1], env.slots_a[:, bass.ds(i, 1), 0]).then_inc(index_done.sem, 1)
                    pool.wait_ge(tables_in, 48)
                    pool.wait_ge(index_done.sem, index_done.after(i))
                    pool.indirect_dma_start(out=xl[:, u, :], out_offset=None, in_=xl_dram,
                                            in_offset=bass.IndirectOffsetOnAxis(ap=index[:, u:u + 1], axis=0),
                                            bounds_check=last_row, oob_is_err=False).then_inc(xl_in[u], 16)
                if inside(i - 6, T):
                    k, r, w = i - 6, (u - 6) % R, (u - 6) % 2
                    pool.wait_ge(prob_done.sem, prob_done.after(k))
                    nc.gpsimd.tensor_tensor(part[:, w, :, 0:HD], xl[:, r, :].rearrange("p (h d) -> p h d", h=HEADS),
                                            part[:, w, :, HD:HDA].broadcast_to([P, HEADS, HD]), ALU.mult).then_inc(part_in.sem, 1)
                if inside(i - 8, T):
                    k, r = i - 8, (u - 8) % R
                    j = pool.value_load(env.tile_a[0:1, bass.ds(k, 1)], min_val=0, max_val=NARROW_TILES - 1)
                    mine = env.acc[:, bass.ds(j, 1)].rearrange("p a h d -> p (a h) d")
                    before = [(acc_done.sem, acc_done.after(k - 1))] if inside(k - 1, T) else []
                    wait_apart(pool, (tables_in, 48), (shrink_done.sem, shrink_done.after(k)), *before)
                    nc.gpsimd.tensor_tensor(mine, mine, shrink[:, r, :].unsqueeze(2).broadcast_to([P, HEADS, HDA]),
                                            ALU.mult).then_inc(shrunk.sem, 1)
                    wait_apart(pool, (tables_in, 48), (copied.sem, copied.after(k)), (shrunk.sem, shrunk.after(k)))
                    nc.gpsimd.tensor_tensor(mine, added[:, r % 2], mine,
                                            ALU.add).then_inc(acc_done.sem, 1)

            run(pool, T, R, 8, step)

        @block.tensor
        def _(pe):
            for c in (sum_done, wide_done, part_tp):
                c.open(pe)
            pe.wait_ge(made, 7)

            def turn_sel(k, u):
                pe.wait_ge(sel_done.sem, sel_done.after(k))
                pe.wait_ge(selT_done.sem, selT_done.room(k))
                nc.tensor.transpose(selT_ps[:, 0:P], sel[:, u, :], env.ident[:]).then_inc(selT_tp.sem, 1)

            def turn_score(k, u):
                pe.wait_ge(parts_done.sem, parts_done.after(k))
                pe.wait_ge(scoreT_done.sem, scoreT_done.room(k))
                nc.tensor.transpose(scoreT_ps[0:2 * HEADS, 0:P], parts[:, u % 2].bitcast(F32).rearrange("p n h -> p (n h)"),
                                    env.ident[:]).then_inc(scoreT_tp.sem, 1)

            def sums(k, u, turn):
                pe.wait_ge(selT_done.sem, selT_done.after(k))
                pe.wait_ge(xr_in[u], turn * 16 + 16)
                pe.wait_ge(message_done.sem, message_done.room(k))
                nc.tensor.matmul(sum_ps[u % 2][:, 0:HID], selT[:, u, :], xr[:, u, :], start=True,
                                 stop=True).then_inc(sum_done.sem, 1)

            def widen(k, u):
                pe.wait_ge(scoreT_done.sem, scoreT_done.after(k))
                pe.wait_ge(max_done.sem, max_done.room(k))
                nc.tensor.matmul(wide_ps[u % 2][:], identb[:], away[:, u % 4, :].unsqueeze(1).broadcast_to([P, HEADS, P]),
                                 start=True, stop=True)
                mm = nc.tensor.matmul(wide_ps[u % 2][:], ones_r[:], scoreT[:, u % 4], start=False, stop=True,
                                      skip_group_check=True)
                mm.then_inc(wide_done.sem, 1)

            def below(k, u):
                pe.wait_ge(topped.sem, k * 3 + 2)
                if inside(k - 1, T):
                    pe.wait_ge(gap_done.sem, gap_done.after(k - 1))
                nc.tensor.matmul(under_ps[:, 0:HEADS], selT[:, u, :], nmax_new[:, u, :], start=True,
                                 stop=True).then_inc(under_tp.sem, 1)

            def gather_sum(k, u):
                pe.wait_ge(part_in.sem, part_in.after(k))
                pe.wait_ge(copied.sem, copied.room(k))
                nc.tensor.matmul(part_ps[:, 0:ACC], sel[:, u, :], part[:, u % 2].rearrange("p h d -> p (h d)"),
                                 start=True, stop=True).then_inc(part_tp.sem, 1)

            def step(i, u, q):
                if inside(i, T):
                    turn_sel(i, u)
                if inside(i - 2, T):
                    turn_score(i - 2, (u - 2) % R)
                if inside(i - 1, T):
                    k = i - 1
                    sums(k, (u - 1) % R, k // R if isinstance(k, int) else (q - 1 if u == 0 else q))
                if inside(i - 3, T):
                    below(i - 3, (u - 3) % R)
                if inside(i - 5, T):
                    gather_sum(i - 5, (u - 5) % R)
                if inside(i - 2, T):
                    widen(i - 2, (u - 2) % R)

            run(pe, T, R, 5, step)

        @block.scalar
        def _(act):
            for c in (selT_done, scoreT_done, shrink_done, prob_done, copied):
                c.open(act)

            def step(i, u, q):
                if inside(i, T):
                    act.wait_ge(selT_tp.sem, selT_tp.after(i))
                    act.wait_ge(part_tp.sem, part_tp.room(i))
                    act.wait_ge(wide_done.sem, wide_done.room(i))
                    nc.scalar.activation(selT[:, u, :], selT_ps[:, 0:P], ACT.Copy)
                    nc.scalar.activation(away[:, u % 4, :], selT_ps[:, 0:P], ACT.Copy, bias=-BIG,
                                         scale=BIG).then_inc(selT_done.sem, 1)
                if inside(i - 6, T):
                    k, w = i - 6, (u - 6) % 2
                    act.wait_ge(part_tp.sem, part_tp.after(k))
                    act.wait_ge(acc_done.sem, acc_done.room(k))
                    nc.scalar.activation(added[:, w].rearrange("p h d -> p (h d)"), part_ps[:, 0:ACC], ACT.Copy).then_inc(copied.sem, 1)
                if inside(i - 2, T):
                    k, w = i - 2, (u - 2) % 4
                    act.wait_ge(scoreT_tp.sem, scoreT_tp.after(k))
                    act.wait_ge(wide_done.sem, wide_done.room(k))
                    for h in range(HEADS):
                        ins = nc.scalar.activation(scoreT[:, w, h, :], scoreT_ps[0:2 * HEADS, 0:P], ACT.Copy,
                                                   scale=head_col[:, h:h + 1])
                    ins.then_inc(scoreT_done.sem, 1)
                if inside(i - 4, T):
                    k, w = i - 4, (u - 4) % 2
                    act.wait_ge(under_done.sem, under_done.after(k))
                    act.wait_ge(part_tp.sem, part_tp.after(k - 2))
                    nc.scalar.activation(part[:, w, :, HD], under[:, w, :], ACT.Exp).then_inc(prob_done.sem, 1)
                if inside(i - 3, T):
                    k, w = i - 3, (u - 3) % 2
                    act.wait_ge(max_done.sem, max_done.after(k))
                    nc.scalar.activation(shrink[:, (u - 3) % R, :], fall[:, w, :], ACT.Exp).then_inc(shrink_done.sem, 1)

            run(act, T, R, 6, step)

        @block.vector
        def _(dve):
            v = nc.vector
            for c in (message_done, score_done, max_done, under_done):
                c.open(dve)
            dve.wait_ge(tables_in, 48)
            scored = done("scored", per=2)
            pointer = env.slots_a[:].bitcast(F32)

            def choose(k, u):
                wait_apart(dve, (tables_in, 48), (part_tp.sem, part_tp.room(k)))
                v.tensor_scalar(sel[:, u, :], env.iota_row[:, 0:P], pointer[:, bass.ds(k, 1), 1], None,
                                ALU.is_equal).then_inc(sel_done.sem, 1)

            def step(i, u, q):
                new, max_, gap = inside(i - 1, T), inside(i - 3, T), inside(i - 4, T)
                kn, rn, wn = i - 1, (u - 1) % R, (u - 1) % 2
                km, rm, wm = i - 3, (u - 3) % R, (u - 3) % 2
                kg, rg, wg = i - 4, (u - 4) % R, (u - 4) % 2
                if gap:
                    dve.wait_ge(under_tp.sem, under_tp.after(kg))
                    dve.wait_ge(prob_done.sem, prob_done.room(kg))
                    v.tensor_tensor(under[:, wg, :], under_ps[:, 0:HEADS], score[:, rg, :], ALU.add).then_inc(gap_done.sem, 1)
                if max_:
                    dve.wait_ge(wide_done.sem, wide_done.after(km))
                    v.tensor_reduce(top[:], wide_ps[wm][:], AX.X, ALU.max).then_inc(topped.sem, 1)
                    j = dve.value_load(env.tile_a[0:1, bass.ds(km, 1)], min_val=0, max_val=NARROW_TILES - 1)
                    mine = env.nmax[:, bass.ds(j, 1), :].rearrange("p a h -> p (a h)")
                if gap:
                    dve.wait_ge(gap_done.sem, gap_done.after(kg))
                    v.tensor_scalar(under[:, wg, :], under[:, wg, :], 0.0, None, ALU.min).then_inc(under_done.sem, 1)
                if max_:
                    dve.wait_ge(shrink_done.sem, shrink_done.room(km))
                    dve.wait_ge(topped.sem, km * 3 + 1)
                    v.scalar_tensor_tensor(nmax_new[:, rm, :], top[:], -1.0, mine, ALU.mult, ALU.min).then_inc(topped.sem, 1)
                if new:
                    dve.wait_ge(sum_done.sem, sum_done.after(kn))
                    dve.wait_ge(xl_in[rn], (kn // R if isinstance(kn, int) else (q - 1 if u == 0 else q)) * 16 + 16)
                    dve.wait_ge(score_done.sem, score_done.after(kn - 1))
                    v.tensor_tensor(message[:, wn, :], sum_ps[wn][:, 0:HID], xl[:, rn, :], ALU.add).then_inc(message_done.sem, 1)
                if max_:
                    dve.wait_ge(topped.sem, km * 3 + 2)
                    v.tensor_tensor(fall[:, wm, :], nmax_new[:, rm, :], mine, ALU.subtract).then_inc(topped.sem, 1)
                if new:
                    dve.wait_ge(message_done.sem, message_done.after(kn))
                    v.scalar_tensor_tensor(leaky[:], message[:, wn, :], NEG_SLOPE, message[:, wn, :], ALU.mult,
                                           ALU.max).then_inc(scored.sem, 1)
                if max_:
                    wait_apart(dve, (tables_in, 48), (topped.sem, km * 3 + 3))
                    v.tensor_copy(mine, nmax_new[:, rm, :]).then_inc(max_done.sem, 1)
                if new:
                    dve.wait_ge(scored.sem, kn * 2 + 1)
                    v.tensor_tensor(weighed[:], leaky[:], att_b[:], ALU.mult).then_inc(scored.sem, 1)
                if inside(i, T) and inside(i + 1, T):
                    choose(i + 1, (u + 1) % R)
                if new:
                    dve.wait_ge(scored.sem, kn * 2 + 2)
                    v.tensor_reduce(score[:, rn, :], weighed[:].rearrange("p (h d) -> p h d", h=HEADS), AX.X,
                                    ALU.add).then_inc(score_done.sem, 1)
                    dve.wait_ge(score_done.sem, score_done.after(kn))
                    if inside(kn - 2, T):
                        dve.wait_ge(scoreT_tp.sem, scoreT_tp.after(kn - 2))
                    v.tensor_copy(parts[:, wn, 0, :], score[:, rn, :]).then_inc(parts_done.sem, 1)
                    dve.wait_ge(parts_done.sem, kn * 2 + 1)
                    v.tensor_tensor(parts[:, wn, 1, :], score[:, rn, :], parts[:, wn, 0, :].bitcast(F32),
                                    ALU.subtract).then_inc(parts_done.sem, 1)

            choose(0, 0)
            run(dve, T, R, 4, step, last=R)


def network_inputs(nc, env, x, W_up, ln_g, ln_b, W1, b1, W2, b2, x1_dram, h_dram):
    with ExitStack() as ctx:
        stage = Stage(nc, ctx, "mid")
        sb, ps, sem, done = stage.sb, stage.ps, stage.sem, stage.done
        wup = [sb(f"wup_{n}", [P, KH, D], F32R) for n in ("hi", "lo")]
        w1 = [sb(f"w1_{n}", [P, KD, MID], F32R) for n in ("hi", "lo")]
        w2 = [sb(f"w2_{n}", [P, KM, HID], F32R) for n in ("hi", "lo")]
        xnT = [sb(f"xnT_{n}", [P, KD, PAIR], F32R) for n in ("hi", "lo")]
        hidT = [sb(f"hidT_{n}", [P, KM, PAIR], F32R) for n in ("hi", "lo")]
        oT = [sb(f"oT_{n}", [P, 2, KH, P], F32R) for n in ("hi", "lo")]
        g_col = sb("g_col", [P, KD])
        b_col = sb("b_col", [P, KD])
        b1_col = sb("b1_col", [P, KM])
        b2_b = sb("b2_b", [P, HID])
        x_buf = sb("x_buf3", [P, 4, D])
        xn = sb("xn", [P, 2, D])
        hid = sb("hid", [P, 2, PAIR])
        rows = sb("rows3", [P, 4, HID])
        out_a = rows[:, 0:2, :]
        h_row = rows[:, 2:4, :]
        inv = sb("inv", [P, 2, HEADS])
        stats = sb("stats", [P, 2, 2, 6])
        moments = sb("moments", [P, 2, 2])
        rstd = sb("rstd3", [P, 2])
        shift = sb("shift3", [P, 2])
        var1 = sb("var1", [P, 2])
        rstd1 = sb("rstd1", [P, 2])
        out_ps = ps("out_ps", [P, 2 * KH, P])
        hT_ps = ps("hT_ps3", [P, 2, KH, P])
        up_ps = ps("up_ps", [P, D])
        xnT_ps = ps("xnT_ps", [P, KD, P])
        w_ps = [ps(f"w_ps{i}", [P, GROUP]) for i in range(2)]

        weights_in = sem("weights_in3")
        bias_done = sem("bias_done")
        gained = sem("gained")
        split = sem("split3")
        x_in = [sem(f"x3_in{s}") for s in range(4)]
        x1_out = [sem(f"x1_out{s}") for s in range(4)]
        h_out = [sem(f"h_out{s}") for s in range(2)]
        att_done = done("att_done")
        out_tp = done("out_tp")
        o_hi = done("o_hi")
        o_lo = done("o_lo")
        up_done = done("up_done")
        v_done = done("v_done", 1)
        mom_done = done("mom_done")
        sqrt_done = done("sqrt_done")
        norm_done = done("norm_done")
        sqrt1_done = done("sqrt1_done")
        norm1_done = done("norm1_done")
        x1_done = done("x1_done")
        xn_done = done("xn_done", 4)
        xn_tp = done("xn_tp")
        x_hi = done("x_hi")
        x_lo = done("x_lo")
        w1_done = done("w1_done")
        relu_done = done("relu_done")
        hid_hi = done("hid_hi", 2)
        hid_lo = done("hid_lo")
        w2_done = done("w2_done")
        h_done = done("h_done", 2)
        hT_tp = done("hT_tp")
        hT_done = done("hT_done", 1)

        ctx.callback(stage.clear)
        block = ctx.enter_context(nc.Block())
        T = WIDE
        LOADS = 7 * 16

        def products(out, lhs, rhs, n_k):
            for a, b in ((0, 0), (0, 1), (1, 0)):
                for k in range(n_k):
                    mm = nc.tensor.matmul(out, lhs(a, k), rhs(b, k), start=(a == b == 0 and k == 0),
                                          stop=(a == 1 and k == n_k - 1))
            return mm

        @block.sync
        def _(sp):
            sp.dma_start(x_buf[:].rearrange("p s d -> p (s d)"), W1.rearrange("(k p) n -> p k n", p=P)).then_inc(weights_in, 16)
            sp.dma_start(xn[:], W_up.rearrange("(k p) n -> p k n", p=P)).then_inc(weights_in, 16)
            sp.dma_start(rows[:], W2.rearrange("(k p) n -> p k n", p=P)).then_inc(weights_in, 16)
            with nc.allow_non_contiguous_dma("columns of weights"):
                sp.dma_start(g_col[:], ln_g.rearrange("(k p) -> p k", p=P)).then_inc(weights_in, 16)
                sp.dma_start(b_col[:], ln_b.rearrange("(k p) -> p k", p=P)).then_inc(weights_in, 16)
                sp.dma_start(b1_col[:], b1.rearrange("(k p) -> p k", p=P)).then_inc(weights_in, 16)
            sp.dma_start(b2_b[:], b2.partition_broadcast(P)).then_inc(weights_in, 16)
            sp.wait_ge(split, 7)

            def step(p, u, q):
                for j in range(2):
                    t, s = p * 2 + j, u * 2 + j
                    if inside(p - 2, T):
                        wait_apart(sp, (split, 7), (xn_done.sem, xn_done.room(t)), (x1_out[s], q * 16))
                    if not isinstance(p, int) or tile_rows(t) == P:
                        sp.dma_start(x_buf[:, s, :], x[bass.ds(t * P, P), :]).then_inc(x_in[s], 16)
                    else:
                        n = tile_rows(t)
                        if n:
                            sp.dma_start(x_buf[0:n, s, :], x[t * P:t * P + n, :]).then_inc(x_in[s], 16)
                        sp.dma_start(x_buf[n:P, s, :], x[0:P - n, :]).then_inc(x_in[s], 16)

            run(sp, T, 2, 0, step, last=2)

        @block.gpsimd
        def _(pool):
            pool.wait_ge(bias_done, 1)
            for k in range(KD):
                w = x_buf[:].rearrange("p s d -> p (s d)")[:, k * MID:(k + 1) * MID]
                nc.gpsimd.tensor_scalar(w, w, g_col[:, k:k + 1], None, ALU.mult).then_inc(gained, 1)

        @block.tensor
        def _(pe):
            pe.wait_ge(weights_in, LOADS)
            whole = x_buf[:].rearrange("p s d -> p (s d)")
            for m in range(KM):
                for k in range(KD):
                    mm = nc.tensor.matmul(w_ps[0][:, m:m + 1], whole[:, k * MID + m * P:k * MID + (m + 1) * P],
                                          b_col[:, k:k + 1], start=(k == 0), stop=(k == KD - 1))
            mm.then_inc(bias_done, 1)
            pe.wait_ge(split, 7)

            def turn_out(p):
                pe.wait_ge(att_done.sem, att_done.after(p * 2 + 1))
                if inside(p - 1, T):
                    pe.wait_ge(o_lo.sem, o_lo.after(p - 1))
                for j in range(2):
                    for k in range(KH):
                        mm = nc.tensor.transpose(out_ps[:, j * KH + k, :], out_a[:, j, k * P:(k + 1) * P], env.ident[:])
                mm.then_inc(out_tp.sem, 1)

            def up(p, j):
                t = p * 2 + j
                if j == 0:
                    pe.wait_ge(o_lo.sem, o_lo.after(p))
                pe.wait_ge(v_done.sem, v_done.room(t))
                for n in range(2):
                    mm = products(up_ps[:, n * 512:(n + 1) * 512], lambda a, k: oT[a][:, j, k, :],
                                  lambda b, k: wup[b][:, k, n * 512:(n + 1) * 512], KH)
                mm.then_inc(up_done.sem, 1)

            def turn_x(p, j):
                t = p * 2 + j
                pe.wait_ge(xn_done.sem, xn_done.after(t))
                if j or inside(p - 1, T):
                    pe.wait_ge(x_lo.sem, x_lo.after(t - 1))
                for k in range(KD):
                    mm = nc.tensor.transpose(xnT_ps[:, k, :], xn[:, j, k * P:(k + 1) * P], env.ident[:])
                mm.then_inc(xn_tp.sem, 1)

            def first(p, m):
                if m == 0:
                    pe.wait_ge(x_lo.sem, x_lo.after(p * 2 + 1))
                if m < 2:
                    pe.wait_ge(h_done.sem, h_done.after(p * 2 - 2 + m))
                pe.wait_ge(hid_hi.sem, hid_hi.room(p * KM + m))
                mm = products(w_ps[m % 2][:, 0:PAIR], lambda a, k: w1[a][:, k, m * P:(m + 1) * P],
                              lambda b, k: xnT[b][:, k, :], KD)
                mm.then_inc(w1_done.sem, 1)

            def second(p, j):
                t = p * 2 + j
                if j == 0:
                    pe.wait_ge(hid_lo.sem, hid_lo.after(p * KM + KM - 1))
                pe.wait_ge(h_done.sem, h_done.room(t))
                mm = products(w_ps[j][:, 0:HID], lambda a, k: hidT[a][:, k, j * P:(j + 1) * P],
                              lambda b, k: w2[b][:, k, :], KM)
                mm.then_inc(w2_done.sem, 1)

            def turn_h(p, j):
                t = p * 2 + j
                pe.wait_ge(h_done.sem, h_done.after(t))
                pe.wait_ge(hT_done.sem, hT_done.room(t))
                for k in range(KH):
                    mm = nc.tensor.transpose(hT_ps[:, j, k, :], h_row[:, j, k * P:(k + 1) * P], env.ident[:])
                mm.then_inc(hT_tp.sem, 1)

            turn_out(0)

            def step(p, u, q):
                a, b, c = inside(p, T), inside(p - 1, T), inside(p - 2, T)
                for j in range(2):
                    if b:
                        turn_x(p - 1, j)
                    if a:
                        up(p, j)
                    if c:
                        second(p - 2, j)
                if c:
                    turn_h(p - 2, 0)
                for m in range(KM):
                    if b:
                        first(p - 1, m)
                    if m == 0 and c:
                        turn_h(p - 2, 1)
                    if m == 2 and a and inside(p + 1, T):
                        turn_out(p + 1)

            run(pe, T, 2, 2, step, last=2)

        @block.scalar
        def _(act):
            for c in (xn_done, hid_hi, hT_done):
                c.open(act)

            def part_o(p):
                act.wait_ge(out_tp.sem, out_tp.after(p))
                if inside(p - 1, T):
                    act.wait_ge(up_done.sem, up_done.after(p * 2 - 1))
                nc.scalar.activation(oT[0][:].rearrange("p j k n -> p (j k) n"), out_ps[:], ACT.Copy).then_inc(o_hi.sem, 1)

            def part_x(p, j):
                t = p * 2 + j
                act.wait_ge(xn_tp.sem, xn_tp.after(t))
                if inside(p - 1, T):
                    act.wait_ge(w1_done.sem, w1_done.after(p * KM - 1))
                nc.scalar.activation(xnT[0][:, :, j * P:(j + 1) * P], xnT_ps[:], ACT.Copy).then_inc(x_hi.sem, 1)

            def copy_h(p, j):
                t = p * 2 + j
                act.wait_ge(hT_tp.sem, hT_tp.after(t))
                nc.scalar.activation(env.featT[:, bass.ds(p, 1), :, j * P:(j + 1) * P].rearrange("p a c n -> p (a c) n"),
                                     hT_ps[:, j], ACT.Copy).then_inc(hT_done.sem, 1)
                act.dma_start(h_dram[bass.ds(t * P, P), :], h_row[:, j, :]).then_inc(h_out[j], 16)

            def roots(p):
                act.wait_ge(mom_done.sem, mom_done.after(p))
                if inside(p - 1, T):
                    act.wait_ge(x1_done.sem, x1_done.after(p * 2 - 1))
                nc.scalar.activation(rstd[:], moments[:, :, 1], ACT.Sqrt, bias=env.eps[:, 1:2]).then_inc(sqrt_done.sem, 1)
                act.wait_ge(norm_done.sem, norm_done.after(p))
                if inside(p - 1, T):
                    act.wait_ge(xn_done.sem, xn_done.after(p * 2 - 1))
                nc.scalar.activation(rstd1[:], var1[:], ACT.Sqrt, bias=env.eps[:, 1:2]).then_inc(sqrt1_done.sem, 1)

            def scale_x1(p, u, j):
                t, s = p * 2 + j, u * 2 + j
                nc.scalar.activation(x_buf[:, s, :], x_buf[:, s, :], ACT.Identity, bias=shift[:, j:j + 1],
                                     scale=rstd[:, j:j + 1]).then_inc(x1_done.sem, 1)

            def scale_xn(p, u, j):
                t, s = p * 2 + j, u * 2 + j
                act.wait_ge(norm1_done.sem, norm1_done.after(p))
                act.wait_ge(x1_done.sem, x1_done.after(t))
                if inside(p - 1, T):
                    act.wait_ge(xn_tp.sem, xn_tp.after(t - 2))
                nc.scalar.activation(xn[:, j, :], x_buf[:, s, :], ACT.Copy, scale=rstd1[:, j:j + 1]).then_inc(xn_done.sem, 1)
                act.dma_start(x1_dram[bass.ds(t * P, P), :], x_buf[:, s, :]).then_inc(x1_out[s], 16)

            def relu(p, m):
                k = p * KM + m
                act.wait_ge(w1_done.sem, w1_done.after(k))
                if m > 1 or inside(p - 1, T):
                    act.wait_ge(hid_lo.sem, hid_lo.after(k - 2))
                nc.scalar.activation(hid[:, m % 2, :], w_ps[m % 2][:, 0:PAIR], ACT.Relu, bias=b1_col[:, m:m + 1]).then_inc(relu_done.sem, 1)
                if inside(p - 1, T):
                    act.wait_ge(w2_done.sem, w2_done.after(p * 2 - 1))
                nc.scalar.activation(hidT[0][:, m, :], w_ps[m % 2][:, 0:PAIR], ACT.Relu, bias=b1_col[:, m:m + 1]).then_inc(hid_hi.sem, 1)

            act.wait_ge(split, 7)
            part_o(0)

            def step(p, u, q):
                a, b, c = inside(p, T), inside(p - 1, T), inside(p - 2, T)
                for j in range(2):
                    if b:
                        part_x(p - 1, j)
                for j in range(2):
                    if c and j == 0:
                        copy_h(p - 2, j)
                if a:
                    roots(p)
                    scale_x1(p, u, 0)
                if b:
                    relu(p - 1, 0)
                if c:
                    copy_h(p - 2, 1)
                if a:
                    scale_x1(p, u, 1)
                if b:
                    relu(p - 1, 1)
                if a:
                    scale_xn(p, u, 0)
                if b:
                    relu(p - 1, 2)
                if a and inside(p + 1, T):
                    part_o(p + 1)
                if a:
                    scale_xn(p, u, 1)
                if b:
                    relu(p - 1, 3)

            run(act, T, 2, 2, step, last=2)
            for s in range(4):
                act.wait_ge(x1_out[s], TILES // 4 * 16)
            for j in range(2):
                act.wait_ge(h_out[j], WIDE * 16)

        @block.vector
        def _(dve):
            v = nc.vector
            v_done.open(dve)
            h_done.open(dve)
            dve.wait_ge(weights_in, LOADS)
            parts = ((wup, xn[:]), (w2, rows[:]), (w1, x_buf[:].rearrange("p s (k n) -> p (s k) n", n=MID)))
            for i, (w, whole) in enumerate(parts):
                if w is w1:
                    dve.wait_ge(gained, KD)
                v.tensor_copy(w[0][:], whole).then_inc(split, 1)
                dve.wait_ge(split, 2 * i + 1)
                v.tensor_tensor(w[1][:], whole, w[0][:].bitcast(F32), ALU.subtract).then_inc(split, 1)
            dve.wait_ge(bias_done, 1)
            v.tensor_tensor(b1_col[:], w_ps[0][:, 0:KM], b1_col[:], ALU.add).then_inc(split, 1)
            dve.wait_ge(split, 7)

            chain = Chain(stage, dve, "input_chain", 10)

            def divide(p):
                den = env.acc[:, bass.ds(p * 2, 2), :, HD]
                chain.link(v.tensor_scalar(inv[:], den, DEN_EPS, None, ALU.add))
                chain.link(v.reciprocal(inv[:], inv[:]))
                for j in range(2):
                    if inside(p - 1, T):
                        dve.wait_ge(out_tp.sem, out_tp.after(p - 1))
                    v.tensor_tensor(out_a[:, j, :].rearrange("p (h d) -> p h d", h=HEADS),
                                    env.acc[:, bass.ds(p * 2 + j, 1), :, 0:HD].rearrange("p a h d -> p (a h) d"),
                                    inv[:, j, :].unsqueeze(2).broadcast_to([P, HEADS, HD]), ALU.mult).then_inc(att_done.sem, 1)

            def rest_o(p):
                dve.wait_ge(o_hi.sem, o_hi.after(p))
                v.tensor_tensor(oT[1][:].rearrange("p j k n -> p (j k) n"), out_ps[:],
                                oT[0][:].bitcast(F32).rearrange("p j k n -> p (j k) n"), ALU.subtract).then_inc(o_lo.sem, 1)

            def rest_x(p, j):
                dve.wait_ge(x_hi.sem, x_hi.after(p * 2 + j))
                v.tensor_tensor(xnT[1][:, :, j * P:(j + 1) * P], xnT_ps[:],
                                xnT[0][:, :, j * P:(j + 1) * P].bitcast(F32), ALU.subtract).then_inc(x_lo.sem, 1)

            def residual(p, u, q, j):
                t, s = p * 2 + j, u * 2 + j
                extra = 16 if isinstance(p, int) and 0 < tile_rows(t) < P else 0
                dve.wait_ge(x_in[s], q * 16 + 16 + extra)
                dve.wait_ge(up_done.sem, up_done.after(t))
                v.tensor_tensor(x_buf[:, s, :], up_ps[:], x_buf[:, s, :], ALU.add).then_inc(v_done.sem, 1)

            def spread(p, u, j):
                t, s = p * 2 + j, u * 2 + j
                dve.wait_ge(v_done.sem, v_done.after(t))
                for n in range(2):
                    m = chain.mark(v.bn_stats(stats[:, j, n, :], x_buf[:, s, n * 512:(n + 1) * 512]))
                wait_apart(dve, (split, 7), (chain.sem, m))
                ins = v.bn_aggr(moments[:, j, :], stats[:, j].rearrange("p n c -> p (n c)"))
                if j == 0:
                    chain.link(ins)
                else:
                    ins.then_inc(mom_done.sem, 1)

            def norm(p):
                dve.wait_ge(sqrt_done.sem, sqrt_done.after(p))
                chain.link(v.reciprocal(rstd[:], rstd[:]))
                chain.mark(v.scalar_tensor_tensor(shift[:], moments[:, :, 0], -1.0, rstd[:], ALU.mult, ALU.mult))
                chain.link(v.tensor_tensor(var1[:], moments[:, :, 1], rstd[:], ALU.mult))
                v.tensor_tensor(var1[:], var1[:], rstd[:], ALU.mult).then_inc(norm_done.sem, 1)
                dve.wait_ge(sqrt1_done.sem, sqrt1_done.after(p))
                v.reciprocal(rstd1[:], rstd1[:]).then_inc(norm1_done.sem, 1)

            def rest_hid(p, m):
                k = p * KM + m
                dve.wait_ge(relu_done.sem, relu_done.after(k))
                dve.wait_ge(hid_hi.sem, hid_hi.after(k))
                v.tensor_tensor(hidT[1][:, m, :], hid[:, m % 2, :], hidT[0][:, m, :].bitcast(F32),
                                ALU.subtract).then_inc(hid_lo.sem, 1)

            def bias(p, j):
                t = p * 2 + j
                dve.wait_ge(w2_done.sem, w2_done.after(t))
                if inside(p - 1, T):
                    dve.wait_ge(h_out[j], p * 16)
                v.tensor_tensor(h_row[:, j, :], w_ps[j][:, 0:HID], b2_b[:], ALU.add).then_inc(h_done.sem, 1)

            chain.start(0)
            divide(0)
            rest_o(0)

            def step(p, u, q):
                a, b, c = inside(p, T), inside(p - 1, T), inside(p - 2, T)
                chain.start(p)
                chain.n = 2
                for j in range(2):
                    if b:
                        rest_x(p - 1, j)
                    if a:
                        residual(p, u, q, j)
                    if c:
                        bias(p - 2, j)
                    if a:
                        spread(p, u, j)
                if a:
                    norm(p)
                if b:
                    rest_hid(p - 1, 0)
                if a and inside(p + 1, T):
                    chain.start(p + 1)
                    divide(p + 1)
                if b:
                    rest_hid(p - 1, 1)
                if b:
                    rest_hid(p - 1, 2)
                if a and inside(p + 1, T):
                    rest_o(p + 1)
                if b:
                    rest_hid(p - 1, 3)

            run(dve, T, 2, 2, step, last=2)


def add_neighbours(nc, env, number, h_dram):
    with ExitStack() as ctx:
        stage = Stage(nc, ctx, f"sum{number}")
        sb, ps, sem, done = stage.sb, stage.ps, stage.sem, stage.done
        R = UL
        T = ITEMS_L
        index = sb("index_l", [P, R], I32)
        h_src = sb("h_src", [P, R, HID])
        sel = sb("sel_l", [P, R, PAIR])
        sum_ps = [ps(f"nb_ps{i}", [P, KH, PAIR]) for i in range(R)]
        cleared = sem("cleared")
        opened = sem("opened")
        index_ready = sem("index_ready")
        index_done = done("index_done_l")
        h_in = [stage.gpsimd_dma_sem(f"h_in{u}") for u in range(R)]
        sel_done = done("sel_done_l")
        sum_done = done("sum_done_l", R)
        add_done = done("add_done", R)
        ctx.callback(stage.clear)
        block = ctx.enter_context(nc.Block())

        @block.gpsimd
        def _(pool):
            last_row = pool.to_reg(ROWS - 1)
            nc.gpsimd.memset(h_src[:], 0.0).then_inc(cleared, 1)
            pool.wait_ge(cleared, 1)

            def step(i, u, q):
                wait_apart(pool, (cleared, 1), (index_done.sem, index_done.after(i)),
                           (sum_done.sem, sum_done.room(i)))
                pool.indirect_dma_start(out=h_src[:, u, :], out_offset=None, in_=h_dram,
                                        in_offset=bass.IndirectOffsetOnAxis(ap=index[:, u:u + 1], axis=0),
                                        bounds_check=last_row, oob_is_err=False).then_inc(h_in[u], 16)

            run(pool, T, R, 0, step)

        @block.tensor
        def _(pe):
            sum_done.open(pe)

            def step(i, u, q):
                pe.wait_ge(sel_done.sem, sel_done.after(i))
                pe.wait_ge(h_in[u], q * 16 + 16)
                pe.wait_ge(add_done.sem, add_done.room(i))
                for c in range(KH):
                    mm = nc.tensor.matmul(sum_ps[u][:, c, :], h_src[:, u, c * P:(c + 1) * P], sel[:, u, :],
                                          start=True, stop=True)
                mm.then_inc(sum_done.sem, 1)

            run(pe, T, R, 0, step)

        @block.scalar
        def _(act):
            act.sem_inc(index_ready, 1)
            act.wait_ge(index_ready, 1)

            def step(i, u, q):
                wait_apart(act, (index_ready, 1), (sum_done.sem, sum_done.room(i)))
                nc.scalar.activation(index[:, u:u + 1], env.slots_l[:, bass.ds(i, 1), 0], ACT.Copy).then_inc(index_done.sem, 1)

            run(act, T, R, 0, step)

        @block.vector
        def _(dve):
            v = nc.vector
            add_done.open(dve)
            dve.sem_inc(opened, 1)
            dve.wait_ge(opened, 1)
            pointer = env.slots_l[:].bitcast(F32)

            tile = [None]

            def tile_of(k):
                return dve.value_load(env.tile_l[0:1, bass.ds(k, 1)], min_val=0, max_val=WIDE_TILES - 1)

            def step(i, u, q):
                if u == 0 and inside(i - 5, T):
                    tile[0] = tile_of(i - 5)
                if inside(i, T):
                    wait_apart(dve, (opened, 1), (sum_done.sem, sum_done.room(i)))
                    v.tensor_scalar(sel[:, u, :], env.iota_row[:], pointer[:, bass.ds(i, 1), 1], None,
                                    ALU.is_equal).then_inc(sel_done.sem, 1)
                if inside(i - 5, T):
                    k, r = i - 5, (u - 5) % R
                    j = tile[0] if tile[0] is not None else tile_of(k)
                    mine = env.featT[:, bass.ds(j, 1), :, :].rearrange("p a c n -> p (a c) n")
                    dve.wait_ge(sum_done.sem, sum_done.after(k))
                    dve.wait_ge(add_done.sem, add_done.after(k - 1))
                    v.tensor_tensor(mine, sum_ps[r][:], mine, ALU.add).then_inc(add_done.sem, 1)
                    tile[0] = tile_of(k + 1) if u < R - 1 and inside(k + 1, T) else None

            run(dve, T, R, 5, step)


def layer(nc, env, number, Wa, ba, Wb, bb, ng, nb, h_dram):
    with ExitStack() as ctx:
        stage = Stage(nc, ctx, f"layer{number}")
        sb, ps, sem, done = stage.sb, stage.ps, stage.sem, stage.done
        R = 4
        wa = sb("wa", [P, KH, HID])
        wb = sb("wb", [P, KH, HID])
        ba_col = sb("ba_col", [P, KH])
        bb_b = sb("bb_b", [P, HID])
        ng_b = sb("ng_b", [P, HID])
        nb_b = sb("nb_b", [P, HID])
        aT = sb("aT", [P, 2, KH, GROUP])
        h_row = sb("h_row4", [P, R, SUB, HID])
        z = sb("z", [P, R, SUB, HID])
        stats = sb("stats4", [P, SUB, 6])
        moments = sb("moments4", [P, SUB, 2])
        rstd = sb("rstd4", [P, SUB])
        a_ps = [ps(f"a_ps{i}", [P, GROUP]) for i in range(2)]
        z_ps = [ps(f"z_ps{i}", [P, 512]) for i in range(2)]
        hT_ps = [ps(f"hT_ps{i}", [P, SUB, P]) for i in range(4)]

        weights_in = sem("weights_in4")
        h_in = [sem(f"h4_in{u}") for u in range(R)]
        h_out = [sem(f"h4_out{u}") for u in range(R)]
        a_done = done("a_done")
        aT_done = done("aT_done", 2)
        z_done = done("z_done")
        zb_done = done("zb_done", 2)
        mom_done = done("mom_done4")
        sqrt_done = done("sqrt_done4")
        norm_done = done("norm_done4")
        gain_done = done("gain_done")
        affine_done = done("affine_done")
        h_done = done("h_done4")
        hT_tp = done("hT_tp4")
        hT_done = done("hT_done4", 2)
        ctx.callback(stage.clear)
        block = ctx.enter_context(nc.Block())
        T = GROUPS

        @block.sync
        def _(sp):
            sp.dma_start(wa[:], Wa.rearrange("(k p) n -> p k n", p=P)).then_inc(weights_in, 16)
            sp.dma_start(wb[:], Wb.rearrange("(k p) n -> p k n", p=P)).then_inc(weights_in, 16)
            with nc.allow_non_contiguous_dma("a column of weights"):
                sp.dma_start(ba_col[:], ba.rearrange("(k p) -> p k", p=P)).then_inc(weights_in, 16)
            for to, of in ((bb_b, bb), (ng_b, ng), (nb_b, nb)):
                sp.dma_start(to[:], of.partition_broadcast(P)).then_inc(weights_in, 16)

            def rows(g):
                return h_dram[bass.ds(g * GROUP, GROUP), :].rearrange("(s p) d -> p s d", p=P)

            def step(g, u, q):
                if inside(g, T):
                    if inside(g - R, T):
                        sp.wait_ge(h_out[u], q * 16)
                        sp.wait_ge(hT_tp.sem, hT_tp.after((g - R) * 2 + 1))
                    sp.dma_start(h_row[:, u], rows(g)).then_inc(h_in[u], 16)
                if inside(g - 3, T):
                    r = (u - 3) % R
                    sp.wait_ge(h_done.sem, h_done.after(g - 3))
                    sp.dma_start(rows(g - 3), h_row[:, r]).then_inc(h_out[r], 16)

            run(sp, T, R, 3, step)
            for u in range(R):
                sp.wait_ge(h_out[u], GROUPS // R * 16)

        @block.tensor
        def _(pe):
            pe.wait_ge(weights_in, 96)

            def first(g, u):
                for m in range(KH):
                    pe.wait_ge(aT_done.sem, aT_done.room(g * KH + m))
                    for k in range(KH):
                        mm = nc.tensor.matmul(a_ps[m][:], wa[:, k, m * P:(m + 1) * P], env.featT[:, bass.ds(g * 2, 2), k, :],
                                              start=(k == 0), stop=(k == KH - 1))
                    mm.then_inc(a_done.sem, 1)

            def second(g, u, s):
                t = g * SUB + s
                if s == 0:
                    pe.wait_ge(aT_done.sem, aT_done.after(g * KH + 1))
                pe.wait_ge(zb_done.sem, zb_done.room(t))
                for k in range(KH):
                    mm = nc.tensor.matmul(z_ps[s % 2][:, 0:HID], aT[:, u % 2, k, s * P:(s + 1) * P], wb[:, k, :],
                                          start=(k == 0), stop=(k == KH - 1))
                mm.then_inc(z_done.sem, 1)

            def turn(g, u, c):
                if c == 0:
                    pe.wait_ge(h_done.sem, h_done.after(g))
                pe.wait_ge(hT_done.sem, hT_done.room(g * KH + c))
                for s in range(SUB):
                    mm = nc.tensor.transpose(hT_ps[c][:, s, :], h_row[:, u, s, c * P:(c + 1) * P], env.ident[:])
                mm.then_inc(hT_tp.sem, 1)

            first(0, 0)

            def step(g, u, q):
                if inside(g + 1, T) and inside(g, T):
                    first(g + 1, u + 1)
                if inside(g, T):
                    for s in range(SUB):
                        second(g, u, s)
                if inside(g - 3, T):
                    for c in range(KH):
                        turn(g - 3, (u - 3) % R, c)

            run(pe, T, R, 3, step, last=R)

        @block.scalar
        def _(act):
            aT_done.open(act)
            hT_done.open(act)
            act.wait_ge(weights_in, 96)

            def relu(g, u):
                for m in range(KH):
                    act.wait_ge(a_done.sem, a_done.after(g * KH + m))
                    if inside(g - 2, T):
                        act.wait_ge(z_done.sem, z_done.after((g - 2) * SUB + 3))
                    nc.scalar.activation(aT[:, u % 2, m, :], a_ps[m][:], ACT.Relu, bias=ba_col[:, m:m + 1]).then_inc(aT_done.sem, 1)

            relu(0, 0)

            def step(g, u, q):
                if inside(g + 1, T) and inside(g, T):
                    relu(g + 1, u + 1)
                if inside(g, T):
                    act.wait_ge(mom_done.sem, mom_done.after(g))
                    nc.scalar.activation(rstd[:], moments[:, :, 1], ACT.Sqrt, bias=env.eps[:, 1:2]).then_inc(sqrt_done.sem, 1)
                if inside(g - 3, T):
                    for c in range(KH):
                        k = (g - 3) * KH + c
                        act.wait_ge(hT_tp.sem, hT_tp.after(k))
                        nc.scalar.activation(env.featT[:, bass.ds((g - 3) * 2, 2), c, :],
                                             hT_ps[c][:].rearrange("p (w t) n -> p w (t n)", w=2), ACT.Copy).then_inc(hT_done.sem, 1)

            run(act, T, R, 3, step, last=R)

        @block.gpsimd
        def _(pool):
            pool.wait_ge(weights_in, 96)

            def step(g, u, q):
                pool.wait_ge(norm_done.sem, norm_done.after(g))
                nc.gpsimd.tensor_tensor(z[:, u], z[:, u], ng_b[:].unsqueeze(1).broadcast_to([P, SUB, HID]),
                                        ALU.mult).then_inc(gain_done.sem, 1)
                pool.wait_ge(gain_done.sem, gain_done.after(g))
                nc.gpsimd.tensor_tensor(z[:, u], z[:, u], nb_b[:].unsqueeze(1).broadcast_to([P, SUB, HID]),
                                        ALU.add).then_inc(affine_done.sem, 1)

            run(pool, T, R, 0, step)

        @block.vector
        def _(dve):
            v = nc.vector
            zb_done.open(dve)
            dve.wait_ge(weights_in, 96)
            chain = Chain(stage, dve, "layer_chain", 2 * SUB + 1)

            def step(g, u, q):
                chain.start(g)
                if inside(g, T):
                    for s in range(SUB):
                        t = g * SUB + s
                        dve.wait_ge(z_done.sem, z_done.after(t))
                        v.tensor_tensor(z[:, u, s, :], z_ps[s % 2][:, 0:HID], bb_b[:], ALU.add).then_inc(zb_done.sem, 1)
                        dve.wait_ge(zb_done.sem, zb_done.after(t))
                        m = chain.mark(v.bn_stats(stats[:, s, :], z[:, u, s, :]))
                        wait_apart(dve, (weights_in, 96), (chain.sem, m))
                        m = chain.mark(v.bn_aggr(moments[:, s, :], stats[:, s, :]))
                    dve.wait_ge(chain.sem, m)
                    v.tensor_copy(stats[:, 0, 0:1], moments[:, 0, 0:1]).then_inc(mom_done.sem, 1)
                if inside(g, T):
                    dve.wait_ge(sqrt_done.sem, sqrt_done.after(g))
                    chain.link(v.reciprocal(rstd[:], rstd[:]))
                    for s in range(SUB):
                        ins = v.tensor_scalar(z[:, u, s, :], z[:, u, s, :], moments[:, s, 0:1], rstd[:, s:s + 1],
                                              ALU.subtract, ALU.mult)
                    ins.then_inc(norm_done.sem, 1)
                if inside(g - 2, T):
                    k, w = g - 2, (u - 2) % R
                    dve.wait_ge(affine_done.sem, affine_done.after(k))
                    dve.wait_ge(h_in[w], (q if u >= 2 else q - 1) * 16 + 16)
                    v.scalar_tensor_tensor(h_row[:, w], z[:, w], 0.0, h_row[:, w], ALU.max, ALU.add).then_inc(h_done.sem, 1)

            run(dve, T, R, 2, step)


def network_outputs(nc, env, Wd1, bd1, Wd2, bd2, out_g, out_b, x1_dram, out):
    with ExitStack() as ctx:
        stage = Stage(nc, ctx, "post")
        sb, ps, sem, done = stage.sb, stage.ps, stage.sem, stage.done
        R = 8
        wd1 = [sb(f"wd1_{n}", [P, KH, MID], F32R) for n in ("hi", "lo")]
        wd2 = [sb(f"wd2_{n}", [P, KM, D], F32R) for n in ("hi", "lo")]
        hT = [sb(f"hT_{n}", [P, 2, KH, PAIR], F32R) for n in ("hi", "lo")]
        dT = [sb(f"dT_{n}", [P, 2, KM, PAIR], F32R) for n in ("hi", "lo")]
        bd1_col = sb("bd1_col", [P, KM])
        bd2_b = sb("bd2_b", [P, D])
        g_b = sb("g_b", [P, D])
        b_b = sb("b_b", [P, D])
        hidden = sb("hidden", [P, 2, PAIR])
        x1 = sb("x1", [P, R, D])
        x1o = sb("x1o", [P, 2, D])
        total = sb("total5", [P, 2, 2])
        away = sb("away5", [P, 2, 2])
        square = sb("square5", [P, 2, 2])
        rstd = sb("rstd5", [P, 2, 2])
        shift = sb("shift5", [P, 2])
        d_ps = [ps(f"d_ps{i}", [P, 512]) for i in range(2)]
        delta_ps = [ps(f"delta_ps{i}", [P, D]) for i in range(2)]
        unread = ps("unread", [P, D])

        weights_in = sem("weights_in5")
        split = sem("split5")
        x1_in = [sem(f"x1_in{u}") for u in range(R)]
        out_done = [sem(f"out_done{u}") for u in range(R)]
        h_hi = done("h_hi")
        h_lo = done("h_lo")
        d_done = done("d_done")
        relu_done = done("relu_done5")
        d_hi = done("d_hi", 2)
        d_lo = done("d_lo")
        delta_done = done("delta_done")
        x1o_done = done("x1o_done")
        x1b_done = done("x1b_done")
        v_done = done("v_done5", 2)
        away_done = [done(f"away5_{i}") for i in range(2)]
        square_done = [done(f"square5_{i}") for i in range(2)]
        sqrt_done = [done(f"sqrt5_{i}") for i in range(2)]
        w_done = done("w_done5", 2)
        shift_done = done("shift_done5")
        z_done = done("z_done5")
        ctx.callback(stage.clear)
        block = ctx.enter_context(nc.Block())
        T = TILES
        U = R
        LOADS = 6 * 16
        WHOLE = 4

        def products(out, lhs, rhs, n_k):
            for a, b in ((0, 0), (0, 1), (1, 0)):
                for k in range(n_k):
                    mm = nc.tensor.matmul(out, lhs(a, k), rhs(b, k), start=(a == b == 0 and k == 0),
                                          stop=(a == 1 and k == n_k - 1))
            return mm

        @block.sync
        def _(sp):
            sp.dma_start(x1[:, 4:6, :].rearrange("p s d -> p (s d)")[:, 0:KH * MID], Wd1.rearrange("(k p) n -> p k n", p=P)).then_inc(weights_in, 16)
            sp.dma_start(x1[:, 0:4, :], Wd2.rearrange("(k p) n -> p k n", p=P)).then_inc(weights_in, 16)
            with nc.allow_non_contiguous_dma("a column of weights"):
                sp.dma_start(bd1_col[:], bd1.rearrange("(k p) -> p k", p=P)).then_inc(weights_in, 16)
            for to, of in ((bd2_b, bd2), (g_b, out_g), (b_b, out_b)):
                sp.dma_start(to[:], of.partition_broadcast(P)).then_inc(weights_in, 16)
            sp.wait_ge(split, WHOLE)

            def step(t, u, q):
                if not isinstance(t, int) or t >= R:
                    sp.wait_ge(out_done[u], q * 16)
                sp.dma_start(x1[:, u, :], x1_dram[bass.ds(t * P, P), :]).then_inc(x1_in[u], 16)

            run(sp, T, U, 0, step)

        @block.gpsimd
        def _(pool):
            pool.wait_ge(weights_in, LOADS)

            def step(t, u, q):
                pool.wait_ge(x1_in[u], q * 16 + 16)
                pool.wait_ge(w_done.sem, w_done.room(t))
                nc.gpsimd.tensor_tensor(x1o[:, u % 2, :], x1[:, u, :], b_b[:], ALU.add).then_inc(x1o_done.sem, 1)
                pool.wait_ge(x1o_done.sem, x1o_done.after(t))
                nc.gpsimd.tensor_tensor(x1[:, u, :], x1[:, u, :], bd2_b[:], ALU.add).then_inc(x1b_done.sem, 1)

            run(pool, T, U, 0, step)

        @block.tensor
        def _(pe):
            def first(p, w, m):
                if m == 0:
                    pe.wait_ge(h_lo.sem, h_lo.after(p))
                pe.wait_ge(d_hi.sem, d_hi.room(p * KM + m))
                mm = products(d_ps[m % 2][:, 0:PAIR], lambda a, k: wd1[a][:, k, m * P:(m + 1) * P],
                              lambda b, k: hT[b][:, w, k, :], KH)
                mm.then_inc(d_done.sem, 1)

            def second(t, w, j):
                if j == 0:
                    pe.wait_ge(d_lo.sem, d_lo.after(t // 2 * KM + KM - 1) if isinstance(t, int) else d_lo.after(t * 2 + KM - 1))
                pe.wait_ge(v_done.sem, v_done.room(t))
                for n in range(2):
                    mm = products(delta_ps[j][:, n * 512:(n + 1) * 512], lambda a, k: dT[a][:, w, k, j * P:(j + 1) * P],
                                  lambda b, k: wd2[b][:, k, n * 512:(n + 1) * 512], KM)
                mm.then_inc(delta_done.sem, 1)

            pe.wait_ge(split, WHOLE)
            for m in range(KM):
                first(0, 0, m)

            def step(t, u, q):
                j, w = u % 2, u // 2 % 2
                p = q * (U // 2) + u // 2
                if inside(p + 1, WIDE):
                    first(p + 1, 1 - w, 2 * j)
                    first(p + 1, 1 - w, 2 * j + 1)
                second(t, w, j)

            run(pe, T, U, 0, step, last=U)

        @block.scalar
        def _(act):
            d_hi.open(act)

            def part_h(p, w):
                if inside(p - 2, WIDE):
                    act.wait_ge(d_done.sem, d_done.after((p - 2) * KM + KM - 1))
                nc.scalar.activation(hT[0][:, w].rearrange("p k n -> p (k n)"),
                                     env.featT[:, bass.ds(p, 1)].rearrange("p a c n -> p (a c n)"), ACT.Copy).then_inc(h_hi.sem, 1)

            def relu(p, w, m):
                k = p * KM + m
                act.wait_ge(d_done.sem, d_done.after(k))
                if m > 1 or inside(p - 1, WIDE):
                    act.wait_ge(d_lo.sem, d_lo.after(k - 2))
                nc.scalar.activation(hidden[:, m % 2, :], d_ps[m % 2][:, 0:PAIR], ACT.Relu, bias=bd1_col[:, m:m + 1]).then_inc(relu_done.sem, 1)
                if inside(p - 2, WIDE):
                    act.wait_ge(delta_done.sem, delta_done.after((p - 2) * 2 + 1))
                nc.scalar.activation(dT[0][:, w, m, :], d_ps[m % 2][:, 0:PAIR], ACT.Relu, bias=bd1_col[:, m:m + 1]).then_inc(d_hi.sem, 1)

            def spread(t, s, i):
                act.wait_ge(away_done[i].sem, away_done[i].after(t))
                if i == 1:
                    act.wait_ge(square_done[0].sem, square_done[0].after(t))
                elif inside(t - 1, T):
                    act.wait_ge(square_done[1].sem, square_done[1].after(t - 1))
                if inside(t - 2, T):
                    reader, value = ((w_done, w_done.after(t - 2)), (z_done, z_done.after(t - 2)))[i]
                    act.wait_ge(reader.sem, value)
                nc.scalar.activation(unread[:], x1[:, s, :], ACT.Square, bias=away[:, i, s % 2:s % 2 + 1],
                                     accum_out=square[:, i, s % 2:s % 2 + 1]).then_inc(square_done[i].sem, 1)
                act.wait_ge(square_done[i].sem, square_done[i].after(t))
                nc.scalar.activation(rstd[:, i, s % 2:s % 2 + 1], square[:, i, s % 2:s % 2 + 1], ACT.Sqrt, bias=env.eps[:, 1:2],
                                     scale=1.0 / D).then_inc(sqrt_done[i].sem, 1)

            act.wait_ge(weights_in, LOADS)
            part_h(0, 0)
            part_h(1, 1)
            for m in range(KM):
                relu(0, 0, m)

            def step(t, u, q):
                j, w = u % 2, u // 2 % 2
                p = q * (U // 2) + u // 2
                nxt = inside(t, T) and inside(p + 1, WIDE)
                if nxt:
                    relu(p + 1, 1 - w, 2 * j)
                if inside(t - 1, T):
                    spread(t - 1, (u - 1) % R, 0)
                if nxt:
                    relu(p + 1, 1 - w, 2 * j + 1)
                if j == 0 and inside(t, T) and inside(p + 2, WIDE):
                    part_h(p + 2, w)
                if inside(t - 3, T):
                    k, r = t - 3, (u - 3) % R
                    act.wait_ge(shift_done.sem, shift_done.after(k))
                    nc.scalar.activation(x1[:, r, :], x1[:, r, :], ACT.Identity, bias=shift[:, r % 2:r % 2 + 1],
                                         scale=rstd[:, 1, r % 2:r % 2 + 1]).then_inc(z_done.sem, 1)
                    act.wait_ge(z_done.sem, z_done.after(k))
                    if not isinstance(k, int) or tile_rows(k) == P:
                        act.dma_start(out[bass.ds(k * P, P), :], x1[:, r, :]).then_inc(out_done[r], 16)
                    elif tile_rows(k):
                        n = tile_rows(k)
                        act.dma_start(out[k * P:k * P + n, :], x1[0:n, r, :]).then_inc(out_done[r], 16)
                if inside(t - 1, T):
                    spread(t - 1, (u - 1) % R, 1)

            run(act, T, U, 3, step, last=U)
            for r in range(R):
                act.wait_ge(out_done[r], 16 * sum(1 for t in range(r, T, R) if tile_rows(t)))

        @block.vector
        def _(dve):
            v = nc.vector
            v_done.open(dve)
            w_done.open(dve)
            dve.wait_ge(weights_in, LOADS)
            parts = ((wd1, x1[:, 4:6, :].rearrange("p s (k n) -> p (s k) n", n=MID)[:, 0:KH, :]), (wd2, x1[:, 0:4, :]))
            for i, (w, whole) in enumerate(parts):
                v.tensor_copy(w[0][:], whole).then_inc(split, 1)
                dve.wait_ge(split, 2 * i + 1)
                v.tensor_tensor(w[1][:], whole, w[0][:].bitcast(F32), ALU.subtract).then_inc(split, 1)
            inner = Chain(stage, dve, "inner_chain", 2)
            outer = Chain(stage, dve, "outer_chain", 1)

            def rest_h(p, w):
                dve.wait_ge(h_hi.sem, h_hi.after(p))
                v.tensor_tensor(hT[1][:, w].rearrange("p k n -> p (k n)"),
                                env.featT[:, bass.ds(p, 1)].rearrange("p a c n -> p (a c n)"),
                                hT[0][:, w].bitcast(F32).rearrange("p k n -> p (k n)"), ALU.subtract).then_inc(h_lo.sem, 1)

            def rest_d(p, w, m):
                k = p * KM + m
                dve.wait_ge(relu_done.sem, relu_done.after(k))
                dve.wait_ge(d_hi.sem, d_hi.after(k))
                v.tensor_tensor(dT[1][:, w, m, :], hidden[:, m % 2, :], dT[0][:, w, m, :].bitcast(F32),
                                ALU.subtract).then_inc(d_lo.sem, 1)

            rest_h(0, 0)
            rest_h(1, 1)
            for m in range(KM):
                rest_d(0, 0, m)

            def step(t, u, q):
                j, w = u % 2, u // 2 % 2
                p = q * (U // 2) + u // 2
                inner.start(t - 1)
                outer.start(t - 2)
                if inside(t, T) and inside(p + 1, WIDE):
                    rest_d(p + 1, 1 - w, 2 * j)
                if inside(t - 1, T):
                    k, r = t - 1, (u - 1) % R
                    i = 1 - j
                    dve.wait_ge(sqrt_done[0].sem, sqrt_done[0].after(k))
                    inner.link(v.reciprocal(rstd[:, 0, i:i + 1], rstd[:, 0, i:i + 1]))
                    inner.link(v.scalar_tensor_tensor(x1[:, r, :], x1[:, r, :], away[:, 0, i:i + 1], g_b[:], ALU.add, ALU.mult))
                    dve.wait_ge(x1o_done.sem, x1o_done.after(k))
                    v.scalar_tensor_tensor(x1[:, r, :], x1[:, r, :], rstd[:, 0, i:i + 1], x1o[:, i, :], ALU.mult, ALU.add,
                                           accum_out=total[:, 1, i:i + 1]).then_inc(w_done.sem, 1)
                    dve.wait_ge(w_done.sem, w_done.after(k))
                    v.tensor_scalar(away[:, 1, i:i + 1], total[:, 1, i:i + 1], -1.0 / D, None, ALU.mult).then_inc(away_done[1].sem, 1)
                if inside(t, T) and inside(p + 1, WIDE):
                    rest_d(p + 1, 1 - w, 2 * j + 1)
                if j == 0 and inside(t, T) and inside(p + 2, WIDE):
                    rest_h(p + 2, w)
                if inside(t - 2, T):
                    dve.wait_ge(sqrt_done[1].sem, sqrt_done[1].after(t - 2))
                    outer.link(v.reciprocal(rstd[:, 1, j:j + 1], rstd[:, 1, j:j + 1]))
                    if inside(t - 4, T):
                        dve.wait_ge(z_done.sem, z_done.after(t - 4))
                    v.tensor_tensor(shift[:, j:j + 1], away[:, 1, j:j + 1], rstd[:, 1, j:j + 1], ALU.mult).then_inc(shift_done.sem, 1)
                if inside(t, T):
                    dve.wait_ge(delta_done.sem, delta_done.after(t))
                    dve.wait_ge(x1b_done.sem, x1b_done.after(t))
                    v.scalar_tensor_tensor(x1[:, u, :], delta_ps[j][:], 0.0, x1[:, u, :], ALU.add, ALU.add,
                                           accum_out=total[:, 0, j:j + 1]).then_inc(v_done.sem, 1)
                    dve.wait_ge(v_done.sem, v_done.after(t))
                    v.tensor_scalar(away[:, 0, j:j + 1], total[:, 0, j:j + 1], -1.0 / D, None, ALU.mult).then_inc(away_done[0].sem, 1)

            run(dve, T, U, 2, step, last=U)


def build(nc, x, src, dst, L0_gnn_rms_w, L0_gnn_W_down, L0_gnn_Wl, L0_gnn_Wr, L0_gnn_att, L0_gnn_W_up, L1_gnn_ln_in_g,
          L1_gnn_ln_in_b, L1_gnn_W1, L1_gnn_b1, L1_gnn_W2, L1_gnn_b2, L1_gnn_layer_Wa, L1_gnn_layer_ba,
          L1_gnn_layer_Wb, L1_gnn_layer_bb, L1_gnn_layer_ng, L1_gnn_layer_nb, L1_gnn_Wd1, L1_gnn_bd1, L1_gnn_Wd2,
          L1_gnn_bd2, L1_gnn_out_g, L1_gnn_out_b, out):
    slots = nc.dram_tensor("slots", (SLOTS, 2), I32, kind="Internal").ap()
    item_tiles = nc.dram_tensor("item_tiles", (2, 2 * P), I32, kind="Internal").ap()
    moves = nc.dram_tensor("moves", (EP, 2 * EC, 3), I32, kind="Internal").ap()
    xl = nc.dram_tensor("xl_rows", (ROWS, HID), F32, kind="Internal").ap()
    xr = nc.dram_tensor("xr_rows", (ROWS, HID), F32, kind="Internal").ap()
    x1 = nc.dram_tensor("x1_rows", (ROWS, D), F32, kind="Internal").ap()
    h = nc.dram_tensor("h_rows", (ROWS, HID), F32, kind="Internal").ap()
    with ExitStack() as ctx:
        env = consts(nc, ctx)
        place_edges(nc, env, src, dst, slots, item_tiles, moves)
        attention_inputs(nc, env, x, L0_gnn_W_down, L0_gnn_Wl, L0_gnn_Wr, L0_gnn_rms_w, L0_gnn_att, xl, xr, slots, moves)
        attention_edges(nc, env, L0_gnn_att, xl, xr, slots)
        network_inputs(nc, env, x, L0_gnn_W_up, L1_gnn_ln_in_g, L1_gnn_ln_in_b, L1_gnn_W1, L1_gnn_b1, L1_gnn_W2,
                       L1_gnn_b2, x1, h)
        for i in range(LAYERS):
            add_neighbours(nc, env, i, h)
            layer(nc, env, i, L1_gnn_layer_Wa[i], L1_gnn_layer_ba[i], L1_gnn_layer_Wb[i], L1_gnn_layer_bb[i],
                  L1_gnn_layer_ng[i], L1_gnn_layer_nb[i], h)
        network_outputs(nc, env, L1_gnn_Wd1, L1_gnn_bd1, L1_gnn_Wd2, L1_gnn_bd2, L1_gnn_out_g, L1_gnn_out_b, x1, out)


_INS = ['x', 'src', 'dst', 'L0_gnn_rms_w', 'L0_gnn_W_down', 'L0_gnn_Wl', 'L0_gnn_Wr', 'L0_gnn_att', 'L0_gnn_W_up',
        'L1_gnn_ln_in_g', 'L1_gnn_ln_in_b', 'L1_gnn_W1', 'L1_gnn_b1', 'L1_gnn_W2', 'L1_gnn_b2', 'L1_gnn_layer_Wa',
        'L1_gnn_layer_ba', 'L1_gnn_layer_Wb', 'L1_gnn_layer_bb', 'L1_gnn_layer_ng', 'L1_gnn_layer_nb', 'L1_gnn_Wd1',
        'L1_gnn_bd1', 'L1_gnn_Wd2', 'L1_gnn_bd2', 'L1_gnn_out_g', 'L1_gnn_out_b']


def kernel(**inputs):
    import numpy as _np
    import concourse.bacc as _bacc
    from concourse import mybir as _mybir
    from concourse.bass_utils import run_bass_kernel_spmd as _run

    nc = _bacc.Bacc("TRN2", target_bir_lowering=False, num_devices=1)
    arrays, args = {}, []
    for name in _INS:
        a = _np.ascontiguousarray(inputs[name])
        arrays[f"in_{name}_dram"] = a
        args.append(nc.dram_tensor(f"in_{name}_dram", a.shape, _mybir.dt.from_np(a.dtype), kind="ExternalInput").ap())
    args.append(nc.dram_tensor("out_0_dram", (N_NODES, D), F32, kind="ExternalOutput").ap())
    build(nc, *args)
    r = _run(nc, [arrays], core_ids=[0])
    return r.results[0]["out_0_dram"]
```
